# Optimizing a Trainium2 kernel written in Bass

```python
import numpy as np
import jax
import jax.numpy as jnp

def _softmax(x, axis=-1):
    return jax.nn.softmax(x, axis=axis)

def _gelu(x):
    return jax.nn.gelu(x, approximate=True)

def _silu(x):
    return jax.nn.silu(x)

def _sigmoid(x):
    return jax.nn.sigmoid(x)

def _layernorm(x, axis=-1, eps=1e-05):
    m = jnp.mean(x, axis=axis, keepdims=True)
    v = jnp.var(x, axis=axis, keepdims=True)
    return (x - m) / jnp.sqrt(v + eps)

def _scatter_add(tgt, idx, src, axis=0):
    return tgt.at[idx].add(src)

def _segment_sum(src, seg, n):
    return jax.ops.segment_sum(src, seg, n)
kernel_name = 'mk_prb_d1_jaxref_r4_629cec'

def setup_inputs(seed: int=0):
    np.random.seed(seed)
    _w = jnp.asarray

    def _L0_attn_setup():
        import math
        import jax, jax.numpy as jnp
        import numpy as np
        D_MODEL = 256
        N_HEADS = 16
        D_K = D_MODEL // N_HEADS
        D_C = 64
        B, S = (2, 512)
        key = jax.random.key(seed)
        ks = jax.random.split(key, 7)
        sd = lambda fan_in: 1.0 / math.sqrt(fan_in)
        return {'x': jax.random.normal(ks[0], (B, S, D_MODEL), dtype=jnp.float32), 'W_dq': jax.random.uniform(ks[1], (D_MODEL, D_C), minval=-sd(D_MODEL), maxval=sd(D_MODEL), dtype=jnp.float32), 'W_uq': jax.random.uniform(ks[2], (D_C, N_HEADS * D_K), minval=-sd(D_C), maxval=sd(D_C), dtype=jnp.float32), 'W_dkv': jax.random.uniform(ks[3], (D_MODEL, D_C), minval=-sd(D_MODEL), maxval=sd(D_MODEL), dtype=jnp.float32), 'W_uk': jax.random.uniform(ks[4], (D_C, N_HEADS * D_K), minval=-sd(D_C), maxval=sd(D_C), dtype=jnp.float32), 'W_uv': jax.random.uniform(ks[5], (D_C, N_HEADS * D_K), minval=-sd(D_C), maxval=sd(D_C), dtype=jnp.float32), 'W_o': jax.random.uniform(ks[6], (N_HEADS * D_K, D_MODEL), minval=-sd(N_HEADS * D_K), maxval=sd(N_HEADS * D_K), dtype=jnp.float32)}
    _L0_attn_in = _L0_attn_setup()

    def _L0_ffn_setup():
        import math
        import jax, jax.numpy as jnp
        import numpy as np
        B, S, D, H, E, F = (2, 256, 256, 16, 16, 1024)
        HEAD = D // H
        MOE_TOKEN_DROPOUT = 0.2
        EPS = 1e-05

        def layer_norm(x, w, b):
            mu = x.mean(-1, keepdims=True)
            var = ((x - mu) ** 2).mean(-1, keepdims=True)
            return (x - mu) * jax.lax.rsqrt(var + EPS) * w + b
        key = jax.random.key(seed)
        ks = jax.random.split(key, 16)
        w = lambda k, shape: jax.random.normal(k, shape, jnp.float32) * 0.02
        return {'hidden_states': jax.random.normal(ks[0], (B, S, D), jnp.float32), 'ln1_w': jnp.ones((D,), jnp.float32), 'ln1_b': jnp.zeros((D,), jnp.float32), 'q_w': w(ks[1], (D, D)), 'q_b': jnp.zeros((D,), jnp.float32), 'k_w': w(ks[2], (D, D)), 'k_b': jnp.zeros((D,), jnp.float32), 'v_w': w(ks[3], (D, D)), 'v_b': jnp.zeros((D,), jnp.float32), 'o_w': w(ks[4], (D, D)), 'o_b': jnp.zeros((D,), jnp.float32), 'ln2_w': jnp.ones((D,), jnp.float32), 'ln2_b': jnp.zeros((D,), jnp.float32), 'router_w': w(ks[5], (D, E)), 'fc1_w': w(ks[6], (E, D, F)), 'fc1_b': jnp.zeros((E, F), jnp.float32), 'fc2_w': w(ks[7], (E, F, D)), 'fc2_b': jnp.zeros((E, D), jnp.float32)}
    _L0_ffn_in = _L0_ffn_setup()
    _d = {'L0_attn_x': _L0_attn_in['x'], 'L0_attn_W_dq': _L0_attn_in['W_dq'], 'L0_attn_W_uq': _L0_attn_in['W_uq'], 'L0_attn_W_dkv': _L0_attn_in['W_dkv'], 'L0_attn_W_uk': _L0_attn_in['W_uk'], 'L0_attn_W_uv': _L0_attn_in['W_uv'], 'L0_attn_W_o': _L0_attn_in['W_o'], 'L0_ffn_ln1_w': _L0_ffn_in['ln1_w'], 'L0_ffn_ln1_b': _L0_ffn_in['ln1_b'], 'L0_ffn_q_w': _L0_ffn_in['q_w'], 'L0_ffn_q_b': _L0_ffn_in['q_b'], 'L0_ffn_k_w': _L0_ffn_in['k_w'], 'L0_ffn_k_b': _L0_ffn_in['k_b'], 'L0_ffn_v_w': _L0_ffn_in['v_w'], 'L0_ffn_v_b': _L0_ffn_in['v_b'], 'L0_ffn_o_w': _L0_ffn_in['o_w'], 'L0_ffn_o_b': _L0_ffn_in['o_b'], 'L0_ffn_ln2_w': _L0_ffn_in['ln2_w'], 'L0_ffn_ln2_b': _L0_ffn_in['ln2_b'], 'L0_ffn_router_w': _L0_ffn_in['router_w'], 'L0_ffn_fc1_w': _L0_ffn_in['fc1_w'], 'L0_ffn_fc1_b': _L0_ffn_in['fc1_b'], 'L0_ffn_fc2_w': _L0_ffn_in['fc2_w'], 'L0_ffn_fc2_b': _L0_ffn_in['fc2_b']}
    _x0 = _d['L0_attn_x']
    _d['L0_attn_x'] = jax.random.normal(jax.random.fold_in(jax.random.key(seed), 1), (2, 2048, 256), dtype=_x0.dtype)
    del _x0
    return _d

def reference(L0_attn_x, L0_attn_W_dq, L0_attn_W_uq, L0_attn_W_dkv, L0_attn_W_uk, L0_attn_W_uv, L0_attn_W_o, L0_ffn_ln1_w, L0_ffn_ln1_b, L0_ffn_q_w, L0_ffn_q_b, L0_ffn_k_w, L0_ffn_k_b, L0_ffn_v_w, L0_ffn_v_b, L0_ffn_o_w, L0_ffn_o_b, L0_ffn_ln2_w, L0_ffn_ln2_b, L0_ffn_router_w, L0_ffn_fc1_w, L0_ffn_fc1_b, L0_ffn_fc2_w, L0_ffn_fc2_b):

    def _L0_attn_ref(x, W_dq, W_uq, W_dkv, W_uk, W_uv, W_o):
        import math
        import jax, jax.numpy as jnp
        import numpy as np
        D_MODEL = 256
        N_HEADS = 16
        D_K = D_MODEL // N_HEADS
        D_C = 64
        B, S = (2, 512)
        Bx, Sx, _ = x.shape
        c_q = x @ W_dq
        Q = (c_q @ W_uq).reshape(Bx, Sx, N_HEADS, D_K)
        c_kv = x @ W_dkv
        K = (c_kv @ W_uk).reshape(Bx, Sx, N_HEADS, D_K)
        V = (c_kv @ W_uv).reshape(Bx, Sx, N_HEADS, D_K)
        scores = jnp.einsum('bqhd,bkhd->bhqk', Q, K) / math.sqrt(D_K)
        causal = jnp.tril(jnp.ones((Sx, Sx), dtype=bool))
        scores = jnp.where(causal, scores, -jnp.inf)
        attn = jax.nn.softmax(scores, axis=-1)
        out = jnp.einsum('bhqk,bkhd->bqhd', attn, V).reshape(Bx, Sx, N_HEADS * D_K)
        return out @ W_o

    def _L0_ffn_ref(hidden_states, ln1_w, ln1_b, q_w, q_b, k_w, k_b, v_w, v_b, o_w, o_b, ln2_w, ln2_b, router_w, fc1_w, fc1_b, fc2_w, fc2_b):
        import math
        import jax, jax.numpy as jnp
        import numpy as np
        B, S, D, H, E, F = (2, 256, 256, 16, 16, 1024)
        HEAD = D // H
        MOE_TOKEN_DROPOUT = 0.2
        EPS = 1e-05

        def layer_norm(x, w, b):
            mu = x.mean(-1, keepdims=True)
            var = ((x - mu) ** 2).mean(-1, keepdims=True)
            return (x - mu) * jax.lax.rsqrt(var + EPS) * w + b
        b, s, _ = hidden_states.shape
        T = b * s
        neg = jnp.finfo(jnp.float32).min
        resid = hidden_states
        x = layer_norm(hidden_states, ln1_w, ln1_b)
        q = (x @ q_w + q_b) / math.sqrt(HEAD)
        k = x @ k_w + k_b
        v = x @ v_w + v_b
        split = lambda t: t.reshape(b, s, H, HEAD).transpose(0, 2, 1, 3)
        q, k, v = (split(q), split(k), split(v))
        scores = jnp.einsum('bhqd,bhkd->bhqk', q, k)
        causal = jnp.tril(jnp.ones((s, s), bool))
        scores = jnp.where(causal, scores, neg)
        attn = jax.nn.softmax(scores, axis=-1)
        ctx = jnp.einsum('bhqk,bhkd->bhqd', attn, v)
        ctx = ctx.transpose(0, 2, 1, 3).reshape(b, s, D)
        hidden = resid + (ctx @ o_w + o_b)
        resid = hidden
        xt = layer_norm(hidden, ln2_w, ln2_b).reshape(T, D)
        logits = xt @ router_w
        probs = jax.nn.softmax(logits, axis=-1)
        top1 = jnp.argmax(probs, axis=-1)
        m1 = jax.nn.one_hot(top1, E, dtype=jnp.float32)
        logits_no1 = jnp.where(m1 > 0, -jnp.inf, logits)
        top2 = jnp.argmax(logits_no1, axis=-1)
        m2 = jax.nn.one_hot(top2, E, dtype=jnp.float32)
        loc1 = jnp.cumsum(m1, axis=0) - 1.0
        loc2 = jnp.cumsum(m2, axis=0) - 1.0 + m1.sum(axis=0, keepdims=True)
        C = 2 * math.ceil(T / E)
        m1 = m1 * (loc1 < C)
        m2 = m2 * (loc2 < C)
        g1 = (probs * m1).sum(-1)
        g2 = (probs * m2).sum(-1)
        denom = jnp.maximum(g1 + g2, jnp.finfo(jnp.float32).eps)
        g1, g2 = (g1 / denom, g2 / denom)
        slot1 = (loc1 * m1).sum(-1).astype(jnp.int32)
        slot2 = (loc2 * m2).sum(-1).astype(jnp.int32)
        d1 = m1[:, :, None] * jax.nn.one_hot(slot1, C, dtype=jnp.float32)[:, None, :]
        d2 = m2[:, :, None] * jax.nn.one_hot(slot2, C, dtype=jnp.float32)[:, None, :]
        dispatch = d1 + d2
        combine = g1[:, None, None] * d1 + g2[:, None, None] * d2
        xin = jnp.einsum('tec,td->ecd', dispatch, xt)
        h = jnp.einsum('ecd,edf->ecf', xin, fc1_w) + fc1_b[:, None, :]
        h = jax.nn.gelu(h, approximate=False)
        eout = jnp.einsum('ecf,efd->ecd', h, fc2_w) + fc2_b[:, None, :]
        eout = eout * (1.0 - MOE_TOKEN_DROPOUT)
        moe_out = jnp.einsum('tec,ecd->td', combine, eout).reshape(b, s, D)
        return resid + moe_out
    x = L0_attn_x
    xn = _layernorm(x, axis=-1)
    x = x + _L0_attn_ref(xn, L0_attn_W_dq, L0_attn_W_uq, L0_attn_W_dkv, L0_attn_W_uk, L0_attn_W_uv, L0_attn_W_o) + _L0_ffn_ref(xn, L0_ffn_ln1_w, L0_ffn_ln1_b, L0_ffn_q_w, L0_ffn_q_b, L0_ffn_k_w, L0_ffn_k_b, L0_ffn_v_w, L0_ffn_v_b, L0_ffn_o_w, L0_ffn_o_b, L0_ffn_ln2_w, L0_ffn_ln2_b, L0_ffn_router_w, L0_ffn_fc1_w, L0_ffn_fc1_b, L0_ffn_fc2_w, L0_ffn_fc2_b)
    return x

_drawn_inputs = setup_inputs


def setup_inputs(seed=0):
    import zlib

    import numpy as np

    out = dict(_drawn_inputs(seed))
    spreads = {'L0_ffn_ln1_w': (1.0, 0.6),
     'L0_ffn_ln1_b': (0.0, 2.0),
     'L0_ffn_q_b': (0.0, 2.0),
     'L0_ffn_k_b': (0.0, 2.0),
     'L0_ffn_v_b': (0.0, 2.0),
     'L0_ffn_o_b': (0.0, 0.8),
     'L0_ffn_ln2_w': (1.0, 0.6),
     'L0_ffn_ln2_b': (0.0, 2.0),
     'L0_ffn_fc1_b': (0.0, 2.0),
     'L0_ffn_fc2_b': (0.0, 0.8)}
    factors = {'L0_attn_W_dq': 8.0,
     'L0_attn_W_uq': 8.0,
     'L0_attn_W_dkv': 8.0,
     'L0_attn_W_uk': 8.0,
     'L0_attn_W_uv': 8.0,
     'L0_attn_W_o': 8.0,
     'L0_ffn_q_w': 21.345,
     'L0_ffn_k_w': 8.0,
     'L0_ffn_v_w': 5.333,
     'L0_ffn_o_w': 2.941,
     'L0_ffn_router_w': 8.0,
     'L0_ffn_fc1_w': 8.0,
     'L0_ffn_fc2_w': 8.0}
    for name, (base, spread) in spreads.items():
        noise = np.random.default_rng([zlib.crc32(name.encode()), seed]).standard_normal(out[name].shape)
        drawn = base * np.exp(spread * noise) if base else spread * noise
        out[name] = jnp.asarray(drawn.astype(out[name].dtype))
    for name, factor in factors.items():
        out[name] = (out[name] * factor).astype(out[name].dtype)
    return out
```

```python
from contextlib import ExitStack

import concourse.bass as bass
from concourse import mybir

ALU = mybir.AluOpType
ACT = mybir.ActivationFunctionType
AX = mybir.AxisListType
F32 = mybir.dt.float32
BF16 = mybir.dt.bfloat16
U32 = mybir.dt.uint32

P = 128
B, S, D = 2, 2048, 256
T = B * S
H, HD = 16, 16
DC = 64
E, F = 16, 1024
CAP = 2 * (T // E)
EPS = 1e-5
KD = D // P
CH = 512
TPC = CH // P
NCH = T // CH
NTILE = T // P
SPLIT = 3
NEG = -3.0e38
GH = 4
HG = H // GH
G = 2 * B * HG
VW = 32
PAIR_ROWS = 6 * HD
STACK = PAIR_ROWS + SPLIT
SCALE = HD ** -0.5
KEEP = 1.0 - 0.2



def stage_a(nc, x, scratch, const):
    xn_dram, q_dram, k_dram, v_dram = scratch
    UNITS = 17
    CREDIT = UNITS
    C_UNIT, V_LOW, V_FFN = 4, 9, 15
    QK = [5, 6, 7, 8, 11, 12, 13, 14]
    NQK = len(QK)
    RING = 4
    with ExitStack() as ctx:
        def sb(name, shape, dt=F32):
            return ctx.enter_context(nc.sbuf_tensor(name, shape, dt))

        def sem(name):
            return ctx.enter_context(nc.semaphore(name))

        xs = sb("xs", [P, 2, TPC, D])
        xn = sb("xn", [P, 2, TPC, D])
        hn = sb("hn", [P, 2, TPC, D])
        stats = sb("a_stats", [P, TPC, 6])
        meanvar = sb("a_meanvar", [P, TPC, 2])
        std = sb("a_std", [P, TPC])
        rstd = sb("a_rstd", [P, TPC])
        none = sb("a_none", [P, 8])
        xnT = sb("xnT", [P, KD, CH])
        hT = sb("hT", [P, KD, CH])
        cT = sb("cT", [P, CH])
        qf = sb("qf", [P, RING, CH])
        rest = sb("rest", [P, RING, CH])
        parts = sb("parts", [P, RING, SPLIT, CH], BF16)
        vt = sb("vt", [P, 2, TPC, H * VW])
        banks = ctx.enter_context(nc.psum_tensor("a_banks", [P, 8, CH], F32))

        x_in = [sem(f"x_in{i}") for i in range(2)]
        norm_step = sem("norm_step")
        var_ready = sem("var_ready")
        std_ready = sem("std_ready")
        xn_ready = sem("xn_ready")
        hn_ready = sem("hn_ready")
        unit_ready = sem("unit_ready")
        copied = sem("copied")
        vt_set = sem("vt_set")
        hi_ready = sem("hi_ready")
        rest_ready = sem("rest_ready")
        mid_ready = sem("mid_ready")
        lo_ready = sem("lo_ready")
        xn_stored = [sem(f"xn_stored{i}") for i in range(2)]
        parts_stored = [sem(f"parts_stored{i}") for i in range(RING)]
        v_stored = [sem(f"v_stored{i}") for i in range(2)]

        block = ctx.enter_context(nc.Block())
        x_chunks = x.rearrange("b (c j p) d -> (b c) p j d", j=TPC, p=P)
        xn_chunks = xn_dram.rearrange("(c j p) d -> c p j d", j=TPC, p=P)

        def unit(c, k):
            return c * UNITS + (k + 1 + CREDIT)

        @block.sync
        def _(sp):
            for n in range(2):
                sp.dma_start(xs[:, n], x_chunks[n]).then_inc(x_in[n], 16)
            for c in range(NCH):
                u, b, cc = c % 2, c // (NCH // B), c % (NCH // B)
                sp.wait_ge(xn_ready, c + 1)
                sp.dma_start(xn_chunks[c], xn[:, u]).then_inc(xn_stored[u], 16)
                if c + 2 < NCH:
                    sp.dma_start(xs[:, u], x_chunks[c + 2]).then_inc(x_in[u], 16)
                for a in range(2):
                    group = (1 - a) * B * HG + b * HG
                    for r in range(NQK // 2 * a, NQK // 2 * (a + 1)):
                        dst, half = (q_dram, k_dram)[r // 2 % 2], r % 2
                        heads = dst.rearrange("g h r t -> (g h) r t")
                        g0 = group * GH + half * (P // HD)
                        sp.wait_ge(lo_ready, NQK * c + r + 1 + RING)
                        for part in range(SPLIT):
                            sp.dma_start(heads[g0:g0 + P // HD, part * HD:(part + 1) * HD, cc * CH:(cc + 1) * CH],
                                         parts[:, r % RING, part, :]).then_inc(parts_stored[r % RING], 16)
                    sp.wait_ge(copied, unit(c, (V_LOW, V_FFN)[a] + 1))
                    for hg in range(HG):
                        dst = v_dram[group + hg, cc * CH:(cc + 1) * CH, :].rearrange("(j p) n -> p j n", p=P)
                        sp.dma_start(dst, vt[:, a, :, hg * P:(hg + 1) * P]).then_inc(v_stored[a], 16)
            for n in range(2):
                sp.wait_ge(xn_stored[n], 16 * (NCH // 2))
                sp.wait_ge(v_stored[n], 16 * HG * NCH)
            for n in range(RING):
                sp.wait_ge(parts_stored[n], 16 * SPLIT * (NQK // RING) * NCH)

        @block.vector
        def _(dve):
            dve.memset(none[:, 0:1], 0.0).then_inc(copied, CREDIT)
            dve.memset(none[:, 1:2], 0.0).then_inc(lo_ready, RING)
            dve.memset(none[:, 2:3], 0.0).then_inc(rest_ready, RING)
            dve.memset(none[:, 3:4], 0.0).then_inc(unit_ready, 2 * UNITS)
            dve.memset(vt[:, :, :, :], 0.0).then_inc(vt_set, 1)
            dve.wait_ge(vt_set, 1)
            v_ones = vt[:, :, :, :].rearrange("p a j (h w) -> p (a j h) w", w=VW)[:, :, HD:HD + 1]
            dve.memset(v_ones, 1.0).then_inc(vt_set, 1)

            def norm(c, n, src, dst):
                done = c * 4 + 2 * n
                for j in range(TPC):
                    last = dve.bn_stats(stats[:, j, :], src[:, j, :])
                last.then_inc(norm_step, 1)
                dve.wait_ge(norm_step, done + 1)
                dve.memset(none[:, 4:5], 0.0)
                for j in range(TPC):
                    last = dve.bn_aggr(meanvar[:, j, :], stats[:, j, :])
                last.then_inc(var_ready, 1)
                dve.wait_ge(std_ready, c * 2 + (n + 1))
                dve.reciprocal(rstd[:, :], std[:, :]).then_inc(norm_step, 1)
                dve.wait_ge(norm_step, done + 2)
                for j in range(TPC):
                    last = dve.tensor_scalar(dst[:, j, :], src[:, j, :], meanvar[:, j, 0:1], rstd[:, j:j + 1],
                                             ALU.subtract, ALU.mult)
                return last

            with dve.Fori(0, NCH // 2) as i:
                for u in range(2):
                    c = i * 2 + u
                    dve.wait_ge(x_in[u], i * 16 + 16)
                    dve.wait_ge(unit_ready, c * UNITS + C_UNIT)
                    dve.wait_ge(xn_stored[u], i * 16)
                    norm(c, 0, xs[:, u], xn[:, u]).then_inc(xn_ready, 1)
                    dve.wait_ge(xn_ready, c + 1)
                    norm(c, 1, xn[:, u], hn[:, u]).then_inc(hn_ready, 1)
                    for r in range(NQK):
                        slot = r % RING
                        n = c * NQK + r
                        dve.wait_ge(copied, unit(c, QK[r]))
                        dve.wait_ge(parts_stored[slot], c * (16 * SPLIT * NQK // RING) + 16 * SPLIT * (r // RING))
                        dve.tensor_copy(parts[:, slot, 0, :], qf[:, slot, :]).then_inc(hi_ready, 1)
                        dve.wait_ge(hi_ready, n + 1)
                        dve.wait_ge(lo_ready, n + 1)
                        dve.tensor_tensor(rest[:, slot, :], qf[:, slot, :], parts[:, slot, 0, :],
                                          ALU.subtract).then_inc(rest_ready, 1)
                        dve.wait_ge(rest_ready, n + (1 + RING))
                        dve.tensor_copy(parts[:, slot, 1, :], rest[:, slot, :]).then_inc(mid_ready, 1)

        @block.gpsimd
        def _(pool):
            with pool.Fori(0, NCH // 2) as i:
                for k in range(2 * NQK):
                    slot = k % RING
                    pool.wait_ge(mid_ready, i * (2 * NQK) + (k + 1))
                    pool.tensor_tensor(parts[:, slot, 2, :], rest[:, slot, :], parts[:, slot, 1, :],
                                       ALU.subtract).then_inc(lo_ready, 1)

        @block.scalar
        def _(act):
            act.wait_ge(vt_set, 2)
            with act.Fori(0, NCH // 2) as i:
                for u in range(2):
                    c = i * 2 + u
                    for n in range(2):
                        act.wait_ge(var_ready, c * 2 + (n + 1))
                        act.activation(std[:, :], meanvar[:, :, 1], ACT.Sqrt, bias=const["eps"][:, 0:1]).then_inc(std_ready, 1)
                    for k in range(UNITS):
                        src, how = banks[:, k % 8, :], {}
                        if k < 2:
                            out = xnT[:, k, :]
                        elif k < 4:
                            out = hT[:, k - 2, :]
                            how = {"scale": const["ln1w"][:, k - 2:k - 1], "bias": const["ln1b"][:, k - 2:k - 1]}
                        elif k == C_UNIT:
                            out = cT[:, :]
                        elif k in QK:
                            r = QK.index(k)
                            act.wait_ge(rest_ready, c * NQK + (r + 1))
                            out = qf[:, r % RING, :]
                            if r >= NQK // 2:
                                how = {"bias": const[("qb", "kb")[r // 2 % 2]][:, r % 2:r % 2 + 1]}
                        else:
                            a = int(k >= V_FFN)
                            half = k - (V_LOW, V_FFN)[a]
                            if half == 0:
                                act.wait_ge(v_stored[a], c * (16 * HG))
                            out = vt[:, a, 2 * half:2 * half + 2, :].rearrange("p j (h w) -> p (j h) w", w=VW)[:, :, 0:HD]
                            src = src.rearrange("p (n w) -> p n w", w=HD)
                        act.wait_ge(unit_ready, c * UNITS + (k + 1 + 2 * UNITS))
                        act.activation(out, src, ACT.Identity, **how).then_inc(copied, 1)

        @block.tensor
        def _(pe):
            with pe.Fori(0, NCH // 2) as i:
                for u in range(2):
                    c = i * 2 + u
                    for k in range(UNITS):
                        bank = banks[:, k % 8, :]
                        pe.wait_ge(copied, unit(c, k - 8) if k >= 8 else unit(c, (16 if k == 0 else k + 8) - UNITS))
                        if k in (0, 2):
                            pe.wait_ge((xn_ready, hn_ready)[k // 2], c + 1)
                        if k == C_UNIT:
                            pe.wait_ge(copied, unit(c, 3))
                        if k == C_UNIT + 1:
                            pe.wait_ge(copied, unit(c, C_UNIT))
                        if k < C_UNIT:
                            src = (xn, hn)[k // 2]
                            for j in range(TPC):
                                last = pe.transpose(bank[:, j * P:(j + 1) * P], src[:, u, j, (k % 2) * P:(k % 2 + 1) * P],
                                                    const["ident"][:, :])
                        elif k == C_UNIT:
                            for h in range(KD):
                                last = pe.matmul(bank, const["wd"][:, h, :], xnT[:, h, :], start=h == 0, stop=h == KD - 1)
                        elif k in QK[:4]:
                            r = QK.index(k)
                            rows = slice(DC * (r // 2), DC * (r // 2) + DC)
                            last = pe.matmul(bank, const["wu"][rows, 0, (r % 2) * P:(r % 2 + 1) * P], cT[rows, :],
                                             start=True, stop=True)
                        elif k in QK:
                            r = QK.index(k) - 4
                            w = const[("qw", "kw")[r // 2]]
                            for h in range(KD):
                                last = pe.matmul(bank, w[:, h, (r % 2) * P:(r % 2 + 1) * P], hT[:, h, :],
                                                 start=h == 0, stop=h == KD - 1)
                        else:
                            a = int(k >= V_FFN)
                            half = k - (V_LOW, V_FFN)[a]
                            for j in range(2):
                                out = bank[:, j * D:(j + 1) * D]
                                tokens = slice((2 * half + j) * P, (2 * half + j + 1) * P)
                                if a == 0:
                                    last = pe.matmul(out, cT[DC:2 * DC, tokens], const["wu"][DC:2 * DC, 1, :],
                                                     start=True, stop=True)
                                else:
                                    pe.matmul(out, const["ones"][0:1, :], const["vb"][0:1, :], start=True, stop=False)
                                    for h in range(KD):
                                        last = pe.matmul(out, hT[:, h, tokens], const["vw"][:, h, :],
                                                         start=False, stop=h == KD - 1)
                        last.then_inc(unit_ready, 1)


def group_order(exps, maxima):
    n_m = len(ROW_BLOCKS) if maxima else 0
    if not exps:
        return [("M", m) for m in range(n_m)] + [("N", 0)]
    order, m, turn = [], 0, None
    lead = len(SCORE_BLOCKS) - 14
    for n in range(len(SCORE_BLOCKS)):
        order.append(("S", n))
        while m < n_m and m * lead < (n + 1) * n_m:
            order.append(("M", m))
            m += 1
        if maxima and n == lead + 5:
            order.append(("N", 0))
        if n % GH == GH - 1 and n >= GH:
            batch = n // GH - 1
            order.append(("PV", batch))
            if turn is not None:
                order.append(("T", turn))
                turn = None
            if batch in CHUNK_ENDS:
                turn = CHUNK_ENDS.index(batch)
    order.append(("PV", len(SCORE_BLOCKS) // GH - 1))
    order.append(("T", S // CH - 1))
    return order


ROW_BLOCKS = [(h, t, c) for t in range(S // P) for h in range(GH) for c in range(t // TPC + 1)]
SCORE_BLOCKS = [(q, k, h) for q in range(S // CH) for k in range(TPC * (q + 1)) for h in range(GH)]
CHUNK_ENDS = [TPC * (q + 1) * (q + 2) // 2 - 1 for q in range(S // CH)]


def stage_b(nc, scratch, const):
    xin_dram, q_dram, k_dram, v_dram, ctx_dram = scratch
    SLOTS = 3
    NM, NS = len(ROW_BLOCKS) + 1, len(SCORE_BLOCKS)
    NB, NQ = NS // GH, S // CH
    PR = 8
    LOADS = 16 * 11
    MROWS = 16 * SPLIT * GH
    FILLS = 16
    with ExitStack() as ctx:
        def sb(name, shape, dt=F32):
            return ctx.enter_context(nc.sbuf_tensor(name, shape, dt))

        def sem(name):
            return ctx.enter_context(nc.semaphore(name))

        qs = sb("qs", [STACK, SLOTS, GH, S], BF16)
        ks = sb("ks", [STACK, SLOTS, GH, S], BF16)
        vs = sb("vs", [P, SLOTS, S // P, GH * VW])
        probs = sb("probs", [P, PR, CH])
        pv_sb = sb("pv_sb", [P, 2, CH])
        inv = sb("inv", [P, 2, TPC, GH])
        ctx_sb = sb("ctx_sb", [P, 2, TPC, GH, HD])
        rowmax = sb("rowmax", [P, GH, S // P, NQ])
        negmax = sb("negmax", [P, P])
        mrest = sb("mrest", [GH * S // P, P])
        mrows = sb("mrows", [GH * S // P, SPLIT, P], BF16)
        none = sb("b_none", [P, 8])
        zeros = sb("zeros", [P, E * CAP * D // P // FILLS])
        m_banks = ctx.enter_context(nc.psum_tensor("m_banks", [P, SLOTS, CH], F32))
        s_banks = ctx.enter_context(nc.psum_tensor("s_banks", [P, SLOTS, CH], F32))
        v_banks = ctx.enter_context(nc.psum_tensor("v_banks", [P, 2, CH], F32))

        loaded = [sem(f"loaded{i}") for i in range(SLOTS)]
        m_ready = sem("m_ready")
        m_used = sem("m_used")
        cleared = sem("cleared")
        negmax_ready = sem("negmax_ready")
        m_step = sem("m_step")
        mrows_ready = sem("mrows_ready")
        mrows_in = sem("mrows_in")
        s_ready = sem("s_ready")
        p_ready = sem("p_ready")
        p_used = sem("p_used")
        pv_copied = sem("pv_copied")
        turned = sem("turned")
        inv_ready = sem("inv_ready")
        ctx_ready = sem("ctx_ready")
        ctx_stored = [sem(f"ctx_stored{i}") for i in range(2)]
        ones_set = sem("ones_set")
        zeros_set = sem("zeros_set")
        filled = sem("filled")

        block = ctx.enter_context(nc.Block())

        def at(i, u, per, off):
            return i * (SLOTS * per) + (u * per + off)

        @block.sync
        def _(sp):
            def load(i, u, g):
                slot = (u + 2) % SLOTS
                rows = k_dram[g].rearrange("h r t -> r h t")
                for at_row, n in ((0, 3), (3, 2), (5, 1)):
                    sp.dma_start(ks[at_row * HD:(at_row + n) * HD, slot], rows[0:n * HD]).then_inc(loaded[slot], 16)
                rows = q_dram[g].rearrange("h r t -> r h t")
                for n, part in enumerate((0, 0, 0, 1, 1, 2)):
                    sp.dma_start(qs[n * HD:(n + 1) * HD, slot], rows[part * HD:(part + 1) * HD]).then_inc(loaded[slot], 16)
                tiles = v_dram[g].rearrange("(k p) n -> p k n", p=P)
                for n in range(0, S // P, S // P // 2):
                    sp.dma_start(vs[:, slot, n:n + S // P // 2], tiles[:, n:n + S // P // 2]).then_inc(loaded[slot], 16)

            def maxima(i, u):
                slot = (u + 1) % SLOTS
                sp.wait_ge(mrows_ready, at(i, u, 1, 2))
                for h in range(GH):
                    for part in range(SPLIT):
                        row = PAIR_ROWS + part
                        sp.dma_start(qs[row:row + 1, slot, h, :], mrows[h * (S // P):(h + 1) * (S // P), part, :])\
                            .then_inc(mrows_in, 16)

            load(-1, 1, 0)
            load(-1, 2, 1)
            maxima(-1, 2)

            def step(i, u, g, more):
                if more:
                    sp.wait_ge(p_used, at(i, u, NB, PR // GH))
                    load(i, u, g)
                maxima(i, u)

            with sp.Fori(0, 4) as i:
                for u in range(SLOTS):
                    step(i, u, i * SLOTS + (u + 2), True)
            for s in range(12, G - 1):
                step(s // SLOTS, s % SLOTS, s + 2, s + 2 < G)
            for n in range(2):
                sp.wait_ge(ctx_stored[n], 16 * G * NQ // 2)
            sp.wait_ge(filled, 16 * FILLS)

        @block.gpsimd
        def _(pool):
            pool.memset(zeros[:, :], 0.0).then_inc(zeros_set, 1)
            pool.wait_ge(zeros_set, 1)
            pool.memset(ks[PAIR_ROWS:STACK, :, :, :], 1.0).then_inc(ones_set, 1)
            fill = xin_dram.rearrange("(f p r) d -> f p (r d)", f=FILLS, p=P)
            for n in range(FILLS):
                pool.dma_start(fill[n], zeros[:, :]).then_inc(filled, 16)

            def step(i, u, g):
                for q in range(NQ):
                    pool.wait_ge(ctx_ready, at(i, u, NQ, q + 1 + 2))
                    dst = ctx_dram[g, q * CH:(q + 1) * CH, :].rearrange("(j p) n -> p j n", p=P)
                    pool.dma_start(dst, ctx_sb[:, q % 2].rearrange("p j h w -> p j (h w)")).then_inc(ctx_stored[q % 2], 16)

            with pool.Fori(0, G // SLOTS) as i:
                for u in range(SLOTS):
                    step(i, u, i * SLOTS + u)
            step(G // SLOTS, 0, G - 1)

        @block.tensor
        def _(pe):
            def step(i, u, exps, maxima):
                now, nxt = u % SLOTS, (u + 1) % SLOTS
                for what, n in group_order(exps, maxima):
                    if what == "S":
                        q, k, h = SCORE_BLOCKS[n]
                        first = max(k - TPC * q, 0) * P
                        bank = s_banks[:, (u * NS + n) % SLOTS, 0:CH - first]
                        if n == 0:
                            pe.wait_ge(mrows_in, at(i, u, MROWS, MROWS))
                        pe.wait_ge(p_ready, at(i, u, NS, n + 1))
                        ins = pe.matmul(bank, ks[:, now, h, k * P:(k + 1) * P],
                                        qs[:, now, h, q * CH + first:(q + 1) * CH], start=True, stop=k < TPC * q)
                        if k >= TPC * q:
                            ins = pe.matmul(bank[:, 0:P], const["identb"][:, :], const["mask"][:, :], start=False, stop=True)
                        ins.then_inc(s_ready, 1)
                    elif what == "M":
                        h, t, c = ROW_BLOCKS[n]
                        width = min(CH, (t + 1) * P - c * CH)
                        bank = m_banks[:, ((u + 1) * NM + n) % SLOTS, 0:width]
                        if n == 0:
                            pe.wait_ge(loaded[nxt], (i + (u + 1) // SLOTS) * LOADS + LOADS)
                        pe.wait_ge(m_used, at(i, u, NM, NM + n + 1))
                        ins = pe.matmul(bank, qs[0:PAIR_ROWS, nxt, h, t * P:(t + 1) * P],
                                        ks[0:PAIR_ROWS, nxt, h, c * CH:c * CH + width], start=True, stop=c < t // TPC)
                        if c == t // TPC:
                            ins = pe.matmul(bank[:, width - P:width], const["mask"][:, :], const["identb"][:, :],
                                            start=False, stop=True)
                        ins.then_inc(m_ready, 1)
                    elif what == "N":
                        bank = m_banks[:, ((u + 1) * NM + NM - 1) % SLOTS, 0:P]
                        pe.wait_ge(m_used, at(i, u, NM, NM + NM))
                        pe.wait_ge(negmax_ready, at(i, u, 1, 2))
                        pe.transpose(bank, negmax[:, :], const["ident"][:, :]).then_inc(m_ready, 1)
                    elif what == "PV":
                        q, k, _ = SCORE_BLOCKS[n * GH]
                        first = max(k - TPC * q, 0) * P
                        if k == 0:
                            pe.wait_ge(ctx_ready, at(i, u, NQ, q + 1))
                        pe.wait_ge(p_ready, at(i, u, NS, GH * (n + 1) + SLOTS))
                        for h in range(GH):
                            rows = slice(h * VW, (h + 1) * VW)
                            ins = pe.matmul(v_banks[rows, q % 2, first:CH], vs[:, now, k, rows],
                                            probs[:, (n * GH + h) % PR, 0:CH - first],
                                            start=k == 0, stop=k == TPC * (q + 1) - 1, tile_position=(0, h * VW))
                        ins.then_inc(p_used, 1)
                    elif what == "T":
                        pe.wait_ge(pv_copied, at(i, u, NQ, n + 1))
                        for t in range(TPC):
                            ins = pe.transpose(v_banks[:, n % 2, t * P:(t + 1) * P], pv_sb[:, n % 2, t * P:(t + 1) * P],
                                               const["ident"][:, :])
                        ins.then_inc(turned, 1)

            step(-1, 2, False, True)
            pe.wait_ge(ones_set, 1)
            with pe.Fori(0, G // SLOTS) as i:
                for u in range(SLOTS):
                    step(i, u, True, True)
            step(G // SLOTS, 0, True, False)

        @block.scalar
        def _(act):
            def step(i, u, maxima):
                for what, n in group_order(True, maxima):
                    if what == "S":
                        q, k, h = SCORE_BLOCKS[n]
                        width = CH - max(k - TPC * q, 0) * P
                        if h == 0:
                            act.wait_ge(p_used, at(i, u, NB, n // GH + 1))
                        act.wait_ge(s_ready, at(i, u, NS, n + 1))
                        act.activation(probs[:, n % PR, 0:width], s_banks[:, (u * NS + n) % SLOTS, 0:width],
                                       ACT.Exp, scale=SCALE).then_inc(p_ready, 1)
                    elif what == "PV" and n in CHUNK_ENDS:
                        q = CHUNK_ENDS.index(n)
                        act.wait_ge(turned, at(i, u, NQ, q + 1))
                        act.wait_ge(p_used, at(i, u, NB, n + 1 + PR // GH))
                        act.activation(pv_sb[:, q % 2, :], v_banks[:, q % 2, :], ACT.Copy).then_inc(pv_copied, 1)

            with act.Fori(0, G // SLOTS) as i:
                for u in range(SLOTS):
                    step(i, u, True)
            step(G // SLOTS, 0, False)

        @block.vector
        def _(dve):
            dve.memset(none[:, 0:1], 0.0).then_inc(m_used, SLOTS)
            dve.memset(none[:, 1:2], 0.0).then_inc(p_ready, SLOTS)
            dve.memset(none[:, 2:3], 0.0).then_inc(p_used, PR // GH)
            dve.memset(none[:, 3:4], 0.0).then_inc(ctx_ready, 2)
            dve.memset(none[:, 4:5], 0.0).then_inc(turned, 2)
            dve.memset(rowmax[:, :, :, :], NEG)
            dve.memset(negmax[:, :], 0.0).then_inc(cleared, 1)
            dve.wait_ge(cleared, 1)

            def step(i, u, exps, maxima):
                for what, n in group_order(exps, maxima):
                    if what == "M":
                        h, t, c = ROW_BLOCKS[n]
                        width = min(CH, (t + 1) * P - c * CH)
                        dve.wait_ge(m_ready, at(i, u, NM, NM + n + 1))
                        dve.tensor_reduce(rowmax[:, h, t, c:c + 1], m_banks[:, ((u + 1) * NM + n) % SLOTS, 0:width],
                                          AX.X, ALU.max).then_inc(m_used, 1)
                        if n == NM - 2:
                            dve.wait_ge(m_used, at(i, u, NM, NM + NM - 1 + SLOTS))
                            dve.tensor_reduce(negmax[:, 0:GH * S // P], rowmax[:, :, :, :].rearrange("p h t c -> p (h t) c"),
                                              AX.X, ALU.max, negate=True).then_inc(negmax_ready, 1)
                    elif what == "N":
                        bank = m_banks[0:GH * S // P, ((u + 1) * NM + NM - 1) % SLOTS, 0:P]
                        dve.wait_ge(m_ready, at(i, u, NM, NM + NM))
                        dve.wait_ge(mrows_in, at(i, u, MROWS, MROWS))
                        dve.tensor_copy(mrows[:, 0, :], bank).then_inc(m_step, 1)
                        dve.wait_ge(m_step, at(i, u, 3, 3 + 1))
                        dve.tensor_tensor(mrest[:, :], bank, mrows[:, 0, :], ALU.subtract).then_inc(m_used, 1)
                        dve.wait_ge(m_used, at(i, u, NM, NM + NM + SLOTS))
                        dve.tensor_copy(mrows[:, 1, :], mrest[:, :]).then_inc(m_step, 2)
                        dve.wait_ge(m_step, at(i, u, 3, 3 + 3))
                        dve.tensor_tensor(mrows[:, 2, :], mrest[:, :], mrows[:, 1, :], ALU.subtract).then_inc(mrows_ready, 1)
                    elif what == "T":
                        heads = v_banks[:, n % 2, :].rearrange("p (j h w) -> p (j h) w", h=GH, w=VW)
                        dve.wait_ge(turned, at(i, u, NQ, n + 1 + 2))
                        dve.reciprocal(inv[:, n % 2].rearrange("p j h -> p (j h)"), heads[:, :, HD]).then_inc(inv_ready, 1)
                        dve.wait_ge(inv_ready, at(i, u, NQ, n + 1))
                        dve.wait_ge(ctx_stored[n % 2], at(i, u, 16 * NQ // 2, 16 * (n // 2)))
                        dve.tensor_tensor(ctx_sb[:, n % 2].rearrange("p j h w -> p (j h) w"), heads[:, :, 0:HD],
                                          inv[:, n % 2].rearrange("p j h -> p (j h)").unsqueeze(2).to_broadcast([P, TPC * GH, HD]),
                                          ALU.mult).then_inc(ctx_ready, 1)

            step(-1, 2, False, True)
            with dve.Fori(0, G // SLOTS) as i:
                for u in range(SLOTS):
                    step(i, u, True, True)
            step(G // SLOTS, 0, True, False)


def stage_c(nc, x, scratch, const, keep):
    xn_dram, ctx_dram = scratch
    xt, base, logits = keep
    UNITS = 11
    BY_ACT = [0, 1, 2, 3, 8, 9, 10]
    BY_DVE = [4, 5, 6, 7]
    with ExitStack() as ctx:
        def sb(name, shape, dt=F32):
            return ctx.enter_context(nc.sbuf_tensor(name, shape, dt))

        def sem(name):
            return ctx.enter_context(nc.semaphore(name))

        xs = sb("c_xs", [P, 2, TPC, D])
        xn = sb("c_xn", [P, 2, TPC, D])
        att = sb("att", [P, 2, 2, TPC, HG, GH * HD])
        attT = sb("attT", [P, 2, KD, CH])
        xtT = sb("xtT", [P, KD, CH])
        hidden = sb("hidden", [P, TPC, D])
        xt_now = sb("xt_now", [P, 2, TPC, D])
        sums = sb("sums", [P, TPC, D])
        stats = sb("c_stats", [P, TPC, 6])
        meanvar = sb("c_meanvar", [P, TPC, 2])
        std = sb("c_std", [P, TPC])
        rstd = sb("c_rstd", [P, TPC])
        none = sb("c_none", [P, 8])
        banks = ctx.enter_context(nc.psum_tensor("c_banks", [P, 8, CH], F32))

        arrived = [sem(f"arrived{i}") for i in range(2)]
        unit_ready = sem("c_unit_ready")
        copied = sem("c_copied")
        added = sem("c_added")
        norm_step = sem("c_norm_step")
        var_ready = sem("c_var_ready")
        std_ready = sem("c_std_ready")
        xt_ready = sem("c_xt_ready")
        xt_kept = sem("xt_kept")
        sums_ready = sem("c_sums_ready")

        block = ctx.enter_context(nc.Block())
        x_chunks = x.rearrange("b (c j p) d -> (b c) p j d", j=TPC, p=P)
        xn_chunks = xn_dram.rearrange("(c j p) d -> c p j d", j=TPC, p=P)
        A_CREDIT, D_CREDIT = len(BY_ACT), len(BY_DVE)

        def emptied(eng, c, k):
            if k in BY_ACT:
                eng.wait_ge(copied, c * A_CREDIT + (BY_ACT.index(k) + 1 + A_CREDIT))
            else:
                eng.wait_ge(added, c * D_CREDIT + (BY_DVE.index(k) + 1 + D_CREDIT))

        @block.sync
        def _(sp):
            for c in range(NCH):
                u, b, cc = c % 2, c // (NCH // B), c % (NCH // B)
                if c >= 2:
                    sp.wait_ge(added, D_CREDIT * c)
                sp.dma_start(xn[:, u], xn_chunks[c]).then_inc(arrived[u], 16)
                sp.dma_start(xs[:, u], x_chunks[c]).then_inc(arrived[u], 16)
                for a in range(2):
                    for hg in range(HG):
                        src = ctx_dram[(a * B + b) * HG + hg, cc * CH:(cc + 1) * CH, :].rearrange("(j p) n -> p j n", p=P)
                        sp.dma_start(att[:, u, a, :, hg, :], src).then_inc(arrived[u], 16)

        ARRIVED = 16 * (2 + 2 * HG)

        @block.gpsimd
        def _(pool):
            with pool.Fori(0, NCH // 2) as i:
                for u in range(2):
                    c = i * 2 + u
                    pool.wait_ge(added, c * D_CREDIT + (2 + D_CREDIT))
                    pool.tensor_tensor(sums[:, :, :], hidden[:, :, :], xs[:, u], ALU.add).then_inc(sums_ready, 1)
                    pool.wait_ge(xt_ready, c + 1)
                    pool.tensor_copy(xt[:, bass.ds(i * (2 * TPC) + u * TPC, TPC), :], xt_now[:, u]).then_inc(xt_kept, 1)

        @block.vector
        def _(dve):
            dve.memset(none[:, 0:1], 0.0).then_inc(copied, A_CREDIT)
            dve.memset(none[:, 1:2], 0.0).then_inc(added, D_CREDIT)
            dve.memset(none[:, 2:3], 0.0).then_inc(xt_kept, 2)
            with dve.Fori(0, NCH // 2) as i:
                for u in range(2):
                    c = i * 2 + u
                    tiles = i * (2 * TPC) + u * TPC
                    dve.wait_ge(arrived[u], i * ARRIVED + ARRIVED)
                    dve.wait_ge(sums_ready, c)
                    for half, k in enumerate((4, 5)):
                        dve.wait_ge(unit_ready, c * UNITS + (k + 1))
                        pair = slice(2 * half, 2 * half + 2)
                        dve.tensor_tensor(hidden[:, pair, :], banks[:, k, :].rearrange("p (j d) -> p j d", d=D),
                                          xn[:, u, pair, :], ALU.add).then_inc(added, 1)
                    dve.wait_ge(added, c * D_CREDIT + (2 + D_CREDIT))
                    for j in range(TPC):
                        last = dve.bn_stats(stats[:, j, :], hidden[:, j, :])
                    last.then_inc(norm_step, 1)
                    dve.wait_ge(norm_step, c * 4 + 1)
                    dve.memset(none[:, 4:5], 0.0)
                    for j in range(TPC):
                        last = dve.bn_aggr(meanvar[:, j, :], stats[:, j, :])
                    last.then_inc(var_ready, 1)
                    dve.wait_ge(std_ready, c + 1)
                    dve.reciprocal(rstd[:, :], std[:, :]).then_inc(norm_step, 1)
                    dve.wait_ge(norm_step, c * 4 + 2)
                    dve.wait_ge(xt_kept, c + 1)
                    for j in range(TPC):
                        last = dve.tensor_scalar(xt_now[:, u, j, :], hidden[:, j, :], meanvar[:, j, 0:1],
                                                 rstd[:, j:j + 1], ALU.subtract, ALU.mult)
                    last.then_inc(norm_step, 1)
                    now = xt_now[:, u]
                    dve.wait_ge(norm_step, c * 4 + 3)
                    dve.tensor_tensor(now, now, const["ln2w"][:, :].unsqueeze(1).to_broadcast([P, TPC, D]),
                                      ALU.mult).then_inc(norm_step, 1)
                    dve.wait_ge(norm_step, c * 4 + 4)
                    dve.tensor_tensor(now, now, const["ln2b"][:, :].unsqueeze(1).to_broadcast([P, TPC, D]),
                                      ALU.add).then_inc(xt_ready, 1)
                    dve.wait_ge(sums_ready, c + 1)
                    for half, k in enumerate((6, 7)):
                        dve.wait_ge(unit_ready, c * UNITS + (k + 1))
                        dve.tensor_tensor(base[:, bass.ds(tiles + 2 * half, 2), :],
                                          banks[:, k, :].rearrange("p (j d) -> p j d", d=D),
                                          sums[:, 2 * half:2 * half + 2, :], ALU.add).then_inc(added, 1)

        @block.scalar
        def _(act):
            with act.Fori(0, NCH // 2) as i:
                for u in range(2):
                    c = i * 2 + u
                    for k in BY_ACT:
                        if k == 8:
                            act.wait_ge(var_ready, c + 1)
                            act.activation(std[:, :], meanvar[:, :, 1], ACT.Sqrt, bias=const["eps"][:, 0:1]).then_inc(std_ready, 1)
                        src = banks[:, k % 8, :]
                        if k < 4:
                            out = attT[:, k // 2, k % 2, :]
                        elif k < 10:
                            out = xtT[:, k - 8, :]
                        else:
                            out = logits[:, bass.ds(i * (2 * TPC) + u * TPC, TPC), :]
                            src = src[:, 0:TPC * E].rearrange("p (j e) -> p j e", e=E)
                        act.wait_ge(unit_ready, c * UNITS + (k + 1))
                        act.activation(out, src, ACT.Copy).then_inc(copied, 1)

        @block.tensor
        def _(pe):
            with pe.Fori(0, NCH // 2) as i:
                for u in range(2):
                    c = i * 2 + u
                    pe.wait_ge(arrived[u], i * ARRIVED + ARRIVED)
                    for k in range(UNITS):
                        bank = banks[:, k % 8, :]
                        if k >= 8:
                            emptied(pe, c, k - 8)
                        else:
                            emptied(pe, c - 1, k + 8 if k + 8 < UNITS else k)
                        if k == 4:
                            emptied(pe, c, 3)
                        if k == 8:
                            pe.wait_ge(xt_ready, c + 1)
                        if k == 10:
                            emptied(pe, c, 9)
                        for j in range(TPC):
                            cols = slice(j * P, (j + 1) * P)
                            if k < 4:
                                src = att[:, u, k // 2, j, 2 * (k % 2):2 * (k % 2) + 2, :].rearrange("p g w -> p (g w)")
                                last = pe.transpose(bank[:, cols], src, const["ident"][:, :])
                            elif k < 8 and j < 2:
                                a, out = (k - 4) // 2, bank[:, j * D:(j + 1) * D]
                                tile = 2 * (k % 2) + j
                                if a == 0:
                                    pe.matmul(out, const["ones"][0:1, :], const["ob"][0:1, :], start=True, stop=False)
                                for h in range(KD):
                                    last = pe.matmul(out, attT[:, a, h, tile * P:(tile + 1) * P],
                                                     const[("ow", "Wo")[a]][:, h, :], start=a == 1 and h == 0, stop=h == KD - 1)
                            elif k in (8, 9):
                                last = pe.transpose(bank[:, cols], xt_now[:, u, j, (k - 8) * P:(k - 7) * P], const["ident"][:, :])
                            elif k == 10:
                                for h in range(KD):
                                    last = pe.matmul(bank[:, j * E:(j + 1) * E], xtT[:, h, cols], const["rw"][:, h, :],
                                                     start=h == 0, stop=h == KD - 1)
                        last.then_inc(unit_ready, 1)


def stage_d(nc, scratch, const, keep):
    xin_dram, = scratch
    xt, logits, gates, gather_row = keep
    with ExitStack() as ctx:
        def sb(name, shape, dt=F32):
            return ctx.enter_context(nc.sbuf_tensor(name, shape, dt))

        def sem(name):
            return ctx.enter_context(nc.semaphore(name))

        cube = [P, NTILE, E]
        flat = [P, NTILE]
        probs, other, expert_ids = sb("d_probs", cube), sb("d_other", cube), sb("expert_ids", cube)
        ids_int = sb("ids_int", [P, NTILE * E], mybir.dt.int32)
        mask = [sb(f"mask{n}", cube) for n in range(2)]
        place = [sb(f"place{n}", cube) for n in range(2)]
        total = [sb(f"total{n}", cube) for n in range(2)]
        upto = [sb(f"upto{n}", cube) for n in range(2)]
        kept = [sb(f"kept{n}", cube) for n in range(2)]
        work = sb("d_work", cube)
        top8 = sb("top8", [P, NTILE, 8])
        top8_id = sb("top8_id", [P, NTILE, 8], U32)
        expert = [sb(f"expert{n}", flat) for n in range(2)]
        slot = [sb(f"slot{n}", flat) for n in range(2)]
        any_kept = [sb(f"any_kept{n}", flat) for n in range(2)]
        one, two, denom = sb("d_one", flat), sb("d_two", flat), sb("denom", flat)
        scatter_row = [sb(f"scatter_row{n}", flat, U32) for n in range(2)]
        ones_cube = sb("ones_cube", [P, NTILE])
        banks = ctx.enter_context(nc.psum_tensor("d_banks", [P, 4, CH], F32))

        step_done = sem("d_step_done")
        shifted = sem("d_shifted")
        exped = sem("d_exped")
        ids_ready = sem("ids_ready")
        masks_ready = sem("masks_ready")
        counted = sem("counted")
        rows_ready = sem("rows_ready")
        scattered = sem("scattered")

        block = ctx.enter_context(nc.Block())

        @block.tensor
        def _(pe):
            for n in range(2):
                pe.wait_ge(masks_ready, n + 1)
                m = mask[n][:, :, :].rearrange("p t e -> p (t e)")
                pe.matmul(banks[:, 2 * n, :], const["upper"][:, :], m, start=True, stop=True)
                pe.matmul(banks[:, 2 * n + 1, :], const["ones"][:, :], m, start=True, stop=True).then_inc(counted, 1)

        @block.scalar
        def _(act):
            act.wait_ge(shifted, 1)
            act.activation(probs[:, :, :], work[:, :, :], ACT.Exp).then_inc(exped, 1)

        @block.gpsimd
        def _(pool):
            pool.iota(ids_int[:, :], [[0, NTILE], [1, E]], base=0, channel_multiplier=0).then_inc(ids_ready, 1)
            pool.wait_ge(rows_ready, 1)
            for t in range(NTILE):
                for n in range(2):
                    pool.indirect_dma_start(out=xin_dram, out_offset=bass.IndirectOffsetOnAxis(ap=scatter_row[n][:, t:t + 1], axis=0),
                                            in_=xt[:, t, :], in_offset=None, bounds_check=E * CAP - 1,
                                            oob_is_err=False).then_inc(scattered, 16)
            pool.wait_ge(scattered, 16 * 2 * NTILE)

        @block.vector
        def _(dve):
            count = [0]

            def settle(ins):
                count[0] += 1
                ins.then_inc(step_done, 1)
                dve.wait_ge(step_done, count[0])

            def wide(a):
                return a.unsqueeze(2).to_broadcast(cube)

            settle(dve.memset(ones_cube[:, :], 1.0))
            dve.wait_ge(ids_ready, 1)
            settle(dve.tensor_copy(expert_ids[:, :, :].rearrange("p t e -> p (t e)"), ids_int[:, :]))
            settle(dve.tensor_reduce(one[:, :], logits[:, :, :], AX.X, ALU.max))
            dve.tensor_tensor(work[:, :, :], logits[:, :, :], wide(one[:, :]), ALU.subtract).then_inc(shifted, 1)
            dve.wait_ge(exped, 1)
            settle(dve.tensor_reduce(two[:, :], probs[:, :, :], AX.X, ALU.add))
            settle(dve.reciprocal(denom[:, :], two[:, :]))
            settle(dve.tensor_tensor(probs[:, :, :], probs[:, :, :], wide(denom[:, :]), ALU.mult))
            for n in range(2):
                src = (probs, other)[n]
                for t in range(NTILE):
                    ins = dve.max(top8[:, t, :], src[:, t, :])
                settle(ins)
                for t in range(NTILE):
                    ins = dve.max_index(top8_id[:, t, :], top8[:, t, :], src[:, t, :])
                settle(ins)
                settle(dve.tensor_copy(expert[n][:, :], top8_id[:, :, 0]))
                ins = dve.tensor_tensor(mask[n][:, :, :], expert_ids[:, :, :], wide(expert[n][:, :]), ALU.is_equal)
                ins.then_inc(masks_ready, 1)
                dve.wait_ge(masks_ready, n + 1)
                if n == 0:
                    settle(dve.scalar_tensor_tensor(out=other[:, :, :].rearrange("p t e -> p (t e)"),
                                                    in0=mask[0][:, :, :].rearrange("p t e -> p (t e)"), scalar=NEG,
                                                    in1=logits[:, :, :].rearrange("p t e -> p (t e)"), op0=ALU.mult, op1=ALU.add))
            for n in range(2):
                dve.wait_ge(counted, n + 1)
                by_tile = banks[:, 2 * n + 1, :].rearrange("p (t e) -> p t e", e=E)
                settle(dve.tensor_copy(total[n][:, :, :], by_tile))
                for e in range(E):
                    ins = dve.tensor_tensor_scan(upto[n][:, :, e], ones_cube[:, :], total[n][:, :, e], 0.0, ALU.mult, ALU.add)
                settle(ins)
                settle(dve.tensor_tensor(work[:, :, :], upto[n][:, :, :], total[n][:, :, :], ALU.subtract))
                settle(dve.tensor_tensor(place[n][:, :, :], banks[:, 2 * n, :].rearrange("p (t e) -> p t e", e=E),
                                         work[:, :, :], ALU.add))
                settle(dve.tensor_scalar(place[n][:, :, :], place[n][:, :, :], -1.0, None, ALU.add))
                if n == 1:
                    firsts = upto[0][:, NTILE - 1:NTILE, :].to_broadcast(cube)
                    settle(dve.tensor_tensor(place[1][:, :, :], place[1][:, :, :], firsts, ALU.add))
                settle(dve.tensor_scalar(work[:, :, :], place[n][:, :, :], float(CAP), None, ALU.is_lt))
                settle(dve.tensor_tensor(kept[n][:, :, :], work[:, :, :], mask[n][:, :, :], ALU.mult))
                settle(dve.tensor_reduce(any_kept[n][:, :], kept[n][:, :, :], AX.X, ALU.add))
                settle(dve.tensor_tensor(work[:, :, :], place[n][:, :, :], kept[n][:, :, :], ALU.mult))
                settle(dve.tensor_reduce(slot[n][:, :], work[:, :, :], AX.X, ALU.add))
                settle(dve.tensor_tensor(work[:, :, :], probs[:, :, :], kept[n][:, :, :], ALU.mult))
                settle(dve.tensor_reduce(gates[:, n, :], work[:, :, :], AX.X, ALU.add))
                settle(dve.tensor_scalar(one[:, :], expert[n][:, :], float(CAP), None, ALU.mult))
                settle(dve.tensor_tensor(one[:, :], one[:, :], slot[n][:, :], ALU.add))
                settle(dve.tensor_tensor(two[:, :], one[:, :], any_kept[n][:, :], ALU.mult))
                settle(dve.tensor_copy(gather_row[:, n, :], two[:, :]))
                settle(dve.tensor_scalar(two[:, :], any_kept[n][:, :], -float(E * CAP), float(E * CAP), ALU.mult, ALU.add))
                settle(dve.tensor_tensor(one[:, :], one[:, :], two[:, :], ALU.add))
                settle(dve.tensor_copy(scatter_row[n][:, :], one[:, :]))
            dve.memset(two[:, 0:1], 0.0).then_inc(rows_ready, 1)
            settle(dve.tensor_tensor(denom[:, :], gates[:, 0, :], gates[:, 1, :], ALU.add))
            settle(dve.tensor_scalar(denom[:, :], denom[:, :], 2.0 ** -23, None, ALU.max))
            settle(dve.reciprocal(one[:, :], denom[:, :]))
            settle(dve.tensor_tensor(gates[:, :, :], gates[:, :, :], one[:, :].unsqueeze(1).to_broadcast([P, 2, NTILE]), ALU.mult))


def stage_e(nc, weights, scratch, const):
    fc1_w, fc2_w = weights
    xin_dram, eout_dram = scratch
    FB = F // P
    UNITS = KD + FB + 2
    TO_ACT, TO_DVE = KD + FB, 2
    LOADS = 16 * 3
    with ExitStack() as ctx:
        def sb(name, shape, dt=F32):
            return ctx.enter_context(nc.sbuf_tensor(name, shape, dt))

        def sem(name):
            return ctx.enter_context(nc.semaphore(name))

        w1 = sb("w1", [P, 2, KD, F])
        w2 = sb("w2", [P, 2, FB, D])
        xin = sb("xin", [P, 2, CAP // P, D])
        xinT = sb("xinT", [P, KD, CAP])
        hid = sb("e_hid", [P, FB, CAP])
        eout = sb("eout", [P, 2, CAP // P, D])
        none = sb("e_none", [P, 8])
        banks = ctx.enter_context(nc.psum_tensor("e_banks", [P, 8, CAP], F32))

        loaded = [sem(f"e_loaded{i}") for i in range(2)]
        unit_ready = sem("e_unit_ready")
        copied = sem("e_copied")
        added = sem("e_added")
        stored = [sem(f"e_stored{i}") for i in range(2)]

        block = ctx.enter_context(nc.Block())

        def emptied(eng, e, k):
            if k < TO_ACT:
                eng.wait_ge(copied, e * TO_ACT + (k + 1 + TO_ACT))
            else:
                eng.wait_ge(added, e * TO_DVE + (k - TO_ACT + 1 + TO_DVE))

        @block.sync
        def _(sp):
            def load(e, u):
                sp.dma_start(xin[:, u], xin_dram[bass.ds(e * CAP, CAP), :].rearrange("(j p) d -> p j d", p=P)).then_inc(loaded[u], 16)
                sp.dma_start(w1[:, u], fc1_w[e].rearrange("(h p) f -> p h f", p=P)).then_inc(loaded[u], 16)
                sp.dma_start(w2[:, u], fc2_w[e].rearrange("(f p) d -> p f d", p=P)).then_inc(loaded[u], 16)

            for u in range(2):
                load(u, u)
            with sp.Fori(0, E // 2 - 1) as i:
                for u in range(2):
                    sp.wait_ge(unit_ready, i * (2 * UNITS) + (u + 1) * UNITS)
                    load(i * 2 + (u + 2), u)

        @block.gpsimd
        def _(pool):
            with pool.Fori(0, E // 2) as i:
                for u in range(2):
                    e = i * 2 + u
                    pool.wait_ge(added, e * TO_DVE + 2 * TO_DVE)
                    dst = eout_dram[bass.ds(e * CAP, CAP), :].rearrange("(j p) d -> p j d", p=P)
                    pool.dma_start(dst, eout[:, u]).then_inc(stored[u], 16)
            for u in range(2):
                pool.wait_ge(stored[u], 16 * E // 2)

        @block.vector
        def _(dve):
            dve.memset(none[:, 0:1], 0.0).then_inc(copied, TO_ACT)
            dve.memset(none[:, 1:2], 0.0).then_inc(added, TO_DVE)
            with dve.Fori(0, E // 2) as i:
                for u in range(2):
                    e = i * 2 + u
                    dve.wait_ge(stored[u], i * 16)
                    for n in range(2):
                        k = TO_ACT + n
                        dve.wait_ge(unit_ready, e * UNITS + (k + 1))
                        src = banks[:, (UNITS * u + k) % 8, :].rearrange("p (j d) -> p j d", d=D)
                        bias = const["b2"][:, bass.ds(e, 1), :].to_broadcast([P, 2, D])
                        dve.scalar_tensor_tensor(out=eout[:, u, 2 * n:2 * n + 2, :], in0=src, scalar=KEEP, in1=bias,
                                                 op0=ALU.mult, op1=ALU.add).then_inc(added, 1)

        @block.scalar
        def _(act):
            with act.Fori(0, E // 2) as i:
                for u in range(2):
                    e = i * 2 + u
                    for k in range(TO_ACT):
                        src = banks[:, (UNITS * u + k) % 8, :]
                        act.wait_ge(unit_ready, e * UNITS + (k + 1))
                        if k < KD:
                            act.activation(xinT[:, k, :], src, ACT.Copy).then_inc(copied, 1)
                        else:
                            act.activation(hid[:, k - KD, :], src, ACT.Gelu,
                                           bias=const["b1T"][:, bass.ds(e * FB + (k - KD), 1)]).then_inc(copied, 1)

        @block.tensor
        def _(pe):
            with pe.Fori(0, E // 2) as i:
                for u in range(2):
                    e = i * 2 + u
                    pe.wait_ge(loaded[u], i * LOADS + LOADS)
                    for k in range(UNITS):
                        bank = banks[:, (UNITS * u + k) % 8, :]
                        emptied(pe, e if k >= 8 else e - 1, k - 8 if k >= 8 else k + UNITS - 8)
                        if k in (KD, TO_ACT):
                            emptied(pe, e, k - 1)
                        if k < KD:
                            for j in range(CAP // P):
                                last = pe.transpose(bank[:, j * P:(j + 1) * P], xin[:, u, j, k * P:(k + 1) * P],
                                                    const["ident"][:, :])
                        elif k < TO_ACT:
                            f = k - KD
                            for h in range(KD):
                                last = pe.matmul(bank, w1[:, u, h, f * P:(f + 1) * P], xinT[:, h, :],
                                                 start=h == 0, stop=h == KD - 1)
                        else:
                            for j in range(2):
                                tile = 2 * (k - TO_ACT) + j
                                for f in range(FB):
                                    last = pe.matmul(bank[:, j * D:(j + 1) * D], hid[:, f, tile * P:(tile + 1) * P],
                                                     w2[:, u, f, :], start=f == 0, stop=f == FB - 1)
                        last.then_inc(unit_ready, 1)


def stage_f(nc, out, eout_dram, keep):
    base, gates, gather_row = keep
    RING = 4
    with ExitStack() as ctx:
        def sb(name, shape, dt=F32):
            return ctx.enter_context(nc.sbuf_tensor(name, shape, dt))

        def sem(name):
            return ctx.enter_context(nc.semaphore(name))

        rows = sb("rows", [P, RING, 2, D])
        half = sb("half", [P, RING, D])
        total = sb("f_total", [P, RING, D])
        gathered = [sem(f"gathered{i}") for i in range(RING)]
        half_ready = sem("half_ready")
        total_ready = sem("total_ready")
        stored = [sem(f"f_stored{i}") for i in range(RING)]
        block = ctx.enter_context(nc.Block())
        out_tiles = out.rearrange("b (t p) d -> (b t) p d", p=P)

        @block.gpsimd
        def _(pool):
            for t in range(NTILE):
                if t >= RING:
                    pool.wait_ge(total_ready, t - RING + 1)
                for n in range(2):
                    pool.indirect_dma_start(out=rows[:, t % RING, n, :], out_offset=None, in_=eout_dram,
                                            in_offset=bass.IndirectOffsetOnAxis(ap=gather_row[:, n, t:t + 1], axis=0))\
                        .then_inc(gathered[t % RING], 16)

        @block.vector
        def _(dve):
            for t in range(NTILE):
                r = t % RING
                dve.wait_ge(gathered[r], 32 * (t // RING + 1))
                dve.scalar_tensor_tensor(out=half[:, r, :], in0=rows[:, r, 0, :], scalar=gates[:, 0, t:t + 1],
                                         in1=base[:, t, :], op0=ALU.mult, op1=ALU.add).then_inc(half_ready, 1)
                dve.wait_ge(half_ready, t + 1)
                if t >= RING:
                    dve.wait_ge(stored[r], 16 * (t // RING))
                dve.scalar_tensor_tensor(out=total[:, r, :], in0=rows[:, r, 1, :], scalar=gates[:, 1, t:t + 1],
                                         in1=half[:, r, :], op0=ALU.mult, op1=ALU.add).then_inc(total_ready, 1)

        @block.sync
        def _(sp):
            for t in range(NTILE):
                sp.wait_ge(total_ready, t + 1)
                sp.dma_start(out_tiles[t], total[:, t % RING, :]).then_inc(stored[t % RING], 16)
            for r in range(RING):
                sp.wait_ge(stored[r], 16 * (NTILE // RING))


def load_constants(nc, w, const, b1_rows):
    with ExitStack() as ctx:
        def sem(name):
            return ctx.enter_context(nc.semaphore(name))

        arrived, blank, made, turned, scaled = sem("w_arrived"), sem("w_blank"), sem("w_made"), sem("b1_turned"), sem("b2_scaled")
        bank = ctx.enter_context(nc.psum_tensor("w_bank", [P, P], F32))
        loads = []
        halves = "(h p) n -> p h n"
        loads.append((const["wd"][:, :, 0:DC], w["W_dq"].rearrange(halves, p=P)))
        loads.append((const["wd"][:, :, DC:2 * DC], w["W_dkv"].rearrange(halves, p=P)))
        loads.append((const["wu"][0:DC, 0, :], w["W_uq"]))
        loads.append((const["wu"][DC:2 * DC, 0, :], w["W_uk"]))
        loads.append((const["wu"][DC:2 * DC, 1, :], w["W_uv"]))
        for name, key in (("qw", "q_w"), ("kw", "k_w"), ("vw", "v_w"), ("ow", "o_w"), ("Wo", "W_o"), ("rw", "router_w")):
            loads.append((const[name][:, :, :], w[key].rearrange(halves, p=P)))
        for name, key in (("vb", "v_b"), ("ob", "o_b")):
            loads.append((const[name][0:1, :], w[key].rearrange("(a d) -> a d", a=1)))
        for name, key in (("ln2w", "ln2_w"), ("ln2b", "ln2_b")):
            loads.append((const[name][:, :], w[key].rearrange("(a d) -> a d", a=1).to_broadcast([P, D])))
        loads.append((const["b2"][:, :, :], w["fc2_b"].rearrange("(a e) d -> a e d", a=1).to_broadcast([P, E, D])))
        loads.append((b1_rows[:, :], w["fc1_b"].rearrange("e (f p) -> (e f) p", p=P)))
        columns = [(const[name][:, :], w[key].rearrange("(h p) -> p h", p=P))
                   for name, key in (("ln1w", "ln1_w"), ("ln1b", "ln1_b"), ("qb", "q_b"), ("kb", "k_b"))]
        ALL = 16 * (len(loads) + len(columns))
        block = ctx.enter_context(nc.Block())

        @block.sync
        def _(sp):
            for dst, src in loads:
                sp.dma_start(dst, src).then_inc(arrived, 16)
            with nc.allow_non_contiguous_dma(reason="four short vectors, one value per partition"):
                for dst, src in columns:
                    sp.dma_start(dst, src).then_inc(arrived, 16)
            sp.wait_ge(arrived, ALL)

        @block.gpsimd
        def _(pool):
            pool.memset(const["ident"][:, :], 0.0)
            pool.memset(const["identb"][:, :], 0.0)
            pool.memset(const["mask"][:, :], 0.0)
            pool.memset(const["upper"][:, :], 1.0)
            pool.memset(const["eps"][:, :], EPS)
            pool.memset(const["ones"][:, :], 1.0).then_inc(blank, 1)
            pool.wait_ge(blank, 1)
            for m in ("ident", "identb"):
                pool.affine_select(out=const[m][:, :], in_=const[m][:, :], compare_op=ALU.not_equal, fill=1.0, base=0,
                                   pattern=[[-1, P]], channel_multiplier=1).then_inc(made, 1)
            pool.affine_select(out=const["mask"][:, :], in_=const["mask"][:, :], compare_op=ALU.is_ge, fill=NEG, base=0,
                               pattern=[[1, P]], channel_multiplier=-1).then_inc(made, 1)
            pool.affine_select(out=const["upper"][:, :], in_=const["upper"][:, :], compare_op=ALU.is_ge, fill=0.0, base=0,
                               pattern=[[1, P]], channel_multiplier=-1).then_inc(made, 1)

        @block.tensor
        def _(pe):
            pe.wait_ge(arrived, ALL)
            pe.wait_ge(made, 4)
            pe.transpose(bank[:, :], b1_rows[:, :], const["ident"][:, :]).then_inc(turned, 1)

        @block.vector
        def _(dve):
            dve.wait_ge(turned, 1)
            dve.tensor_copy(const["b1T"][:, :], bank[:, :])
            dve.tensor_scalar(const["b2"][:, :, :], const["b2"][:, :, :], KEEP, None, ALU.mult).then_inc(scaled, 1)


def layer(nc, x, w, out):
    xn_dram = nc.dram_tensor("xn_scratch", [T, D], F32).ap()
    q_dram = nc.dram_tensor("q_scratch", [G, GH, SPLIT * HD, S], BF16).ap()
    k_dram = nc.dram_tensor("k_scratch", [G, GH, SPLIT * HD, S], BF16).ap()
    v_dram = nc.dram_tensor("v_scratch", [G, S, GH * VW], F32).ap()
    ctx_dram = nc.dram_tensor("ctx_scratch", [G, S, GH * HD], F32).ap()
    xin_dram = nc.dram_tensor("xin_scratch", [E * CAP, D], F32).ap()
    eout_dram = nc.dram_tensor("eout_scratch", [E * CAP, D], F32).ap()
    with ExitStack() as ctx:
        shapes = {"wd": [P, KD, 2 * DC], "wu": [P, 2, D], "qw": [P, KD, D], "kw": [P, KD, D], "vw": [P, KD, D],
                  "ow": [P, KD, D], "Wo": [P, KD, D], "rw": [P, KD, E], "vb": [1, D], "ob": [1, D],
                  "ln1w": [P, KD], "ln1b": [P, KD], "qb": [P, KD], "kb": [P, KD], "ln2w": [P, D], "ln2b": [P, D],
                  "b2": [P, E, D], "b1T": [P, E * F // P], "ident": [P, P], "upper": [P, P], "ones": [P, P], "eps": [P, 1]}
        const = {n: ctx.enter_context(nc.sbuf_tensor(f"c_{n}", s, F32)) for n, s in shapes.items()}
        for n in ("identb", "mask"):
            const[n] = ctx.enter_context(nc.sbuf_tensor(f"c_{n}", [P, P], BF16))
        with nc.sbuf_tensor("b1_rows", [E * F // P, P], F32) as b1_rows:
            load_constants(nc, w, const, b1_rows)
        stage_a(nc, x, (xn_dram, q_dram, k_dram, v_dram), const)
        stage_b(nc, (xin_dram, q_dram, k_dram, v_dram, ctx_dram), const)
        with ExitStack() as late:
            def sb(name, shape, dt=F32):
                return late.enter_context(nc.sbuf_tensor(name, shape, dt))

            base = sb("base", [P, NTILE, D])
            gates = sb("gates", [P, 2, NTILE])
            gather_row = sb("gather_row", [P, 2, NTILE], U32)
            with nc.sbuf_tensor("xt", [P, NTILE, D], F32) as xt, nc.sbuf_tensor("logits", [P, NTILE, E], F32) as logits:
                stage_c(nc, x, (xn_dram, ctx_dram), const, (xt, base, logits))
                stage_d(nc, (xin_dram,), const, (xt, logits, gates, gather_row))
            stage_e(nc, (w["fc1_w"], w["fc2_w"]), (xin_dram, eout_dram), const)
            stage_f(nc, out, eout_dram, (base, gates, gather_row))


_ATTN = ["W_dq", "W_uq", "W_dkv", "W_uk", "W_uv", "W_o"]
_FFN = ["ln1_w", "ln1_b", "q_w", "q_b", "k_w", "k_b", "v_w", "v_b", "o_w", "o_b", "ln2_w", "ln2_b", "router_w",
        "fc1_w", "fc1_b", "fc2_w", "fc2_b"]
_INS = {"x": "L0_attn_x", **{n: f"L0_attn_{n}" for n in _ATTN}, **{n: f"L0_ffn_{n}" for n in _FFN}}


def kernel(**inputs):
    import numpy as _np
    import concourse.bacc as _bacc
    from concourse import mybir as _mybir
    from concourse.bass_utils import run_bass_kernel_spmd as _run

    nc = _bacc.Bacc("TRN2", target_bir_lowering=False, num_devices=1)
    arrays, args = {}, {}
    for short, name in _INS.items():
        a = _np.ascontiguousarray(inputs[name])
        arrays[f"in_{name}"] = a
        args[short] = nc.dram_tensor(f"in_{name}", a.shape, _mybir.dt.from_np(a.dtype), kind="ExternalInput").ap()
    out = nc.dram_tensor("out_0", (B, S, D), F32, kind="ExternalOutput").ap()
    layer(nc, args.pop("x"), args, out)
    r = _run(nc, [arrays], core_ids=[0])
    return r.results[0]["out_0"]
```

```python
from contextlib import ExitStack

import concourse.bass as bass
from concourse import mybir

ALU = mybir.AluOpType
ACT = mybir.ActivationFunctionType
AX = mybir.AxisListType
F32 = mybir.dt.float32
BF16 = mybir.dt.bfloat16
U32 = mybir.dt.uint32

P = 128
B, S, D = 2, 2048, 256
T = B * S
H, HD = 16, 16
DC = 64
E, F = 16, 1024
CAP = 2 * (T // E)
EPS = 1e-5
KD = D // P
CH = 512
TPC = CH // P
NCH = T // CH
NTILE = T // P
SPLIT = 3
NEG = -3.0e38
GH = 4
HG = H // GH
G = 2 * B * HG
VW = 32
PAIR_ROWS = 6 * HD
STACK = PAIR_ROWS + SPLIT
SCALE = HD ** -0.5
KEEP = 1.0 - 0.2



def stage_a(nc, x, scratch, const):
    xn_dram, q_dram, k_dram, v_dram = scratch
    UNITS = 17
    CREDIT = UNITS
    C_UNIT, V_LOW, V_FFN = 4, 13, 15
    QK = list(range(5, 13))
    NQK = len(QK)
    RING = 4
    with ExitStack() as ctx:
        def sb(name, shape, dt=F32):
            return ctx.enter_context(nc.sbuf_tensor(name, shape, dt))

        def sem(name):
            return ctx.enter_context(nc.semaphore(name))

        xs = sb("xs", [P, 2, TPC, D])
        xn = sb("xn", [P, 2, TPC, D])
        hn = sb("hn", [P, 2, TPC, D])
        stats = sb("a_stats", [P, TPC, 6])
        meanvar = sb("a_meanvar", [P, TPC, 2])
        std = sb("a_std", [P, TPC])
        rstd = sb("a_rstd", [P, TPC])
        none = sb("a_none", [P, 8])
        xnT = sb("xnT", [P, KD, CH])
        hT = sb("hT", [P, KD, CH])
        cT = sb("cT", [P, CH])
        qf = sb("qf", [P, RING, CH])
        rest = sb("rest", [P, RING, CH])
        parts = sb("parts", [P, RING, SPLIT, CH], BF16)
        vt = sb("vt", [P, 2, TPC, H * VW])
        banks = ctx.enter_context(nc.psum_tensor("a_banks", [P, 8, CH], F32))

        x_in = [sem(f"x_in{i}") for i in range(2)]
        norm_step = sem("norm_step")
        var_ready = sem("var_ready")
        std_ready = sem("std_ready")
        xn_ready = sem("xn_ready")
        hn_ready = sem("hn_ready")
        unit_ready = sem("unit_ready")
        copied = sem("copied")
        vt_set = sem("vt_set")
        rest_ready = sem("rest_ready")
        mid_ready = sem("mid_ready")
        lo_ready = sem("lo_ready")
        xn_stored = [sem(f"xn_stored{i}") for i in range(2)]
        parts_stored = [sem(f"parts_stored{i}") for i in range(RING)]
        v_stored = [sem(f"v_stored{i}") for i in range(2)]

        block = ctx.enter_context(nc.Block())
        x_chunks = x.rearrange("b (c j p) d -> (b c) p j d", j=TPC, p=P)
        xn_chunks = xn_dram.rearrange("(c j p) d -> c p j d", j=TPC, p=P)

        def unit(c, k):
            return c * UNITS + (k + 1 + CREDIT)

        @block.sync
        def _(sp):
            for n in range(2):
                sp.dma_start(xs[:, n], x_chunks[n]).then_inc(x_in[n], 16)
            for c in range(NCH):
                u, b, cc = c % 2, c // (NCH // B), c % (NCH // B)
                sp.wait_ge(xn_ready, c + 1)
                sp.dma_start(xn_chunks[c], xn[:, u]).then_inc(xn_stored[u], 16)
                if c + 2 < NCH:
                    sp.dma_start(xs[:, u], x_chunks[c + 2]).then_inc(x_in[u], 16)
                for a in range(2):
                    group = a * B * HG + b * HG
                    for r in range(NQK // 2 * a, NQK // 2 * (a + 1)):
                        dst, half = (q_dram, k_dram)[r // 2 % 2], r % 2
                        heads = dst.rearrange("g h r t -> (g h) r t")
                        g0 = group * GH + half * (P // HD)
                        sp.wait_ge(lo_ready, NQK * c + r + 1 + RING)
                        for part in range(SPLIT):
                            sp.dma_start(heads[g0:g0 + P // HD, part * HD:(part + 1) * HD, cc * CH:(cc + 1) * CH],
                                         parts[:, r % RING, part, :]).then_inc(parts_stored[r % RING], 16)
                for a in (1, 0):
                    group = a * B * HG + b * HG
                    sp.wait_ge(copied, unit(c, (V_FFN, V_LOW)[a] + 1))
                    for hg in range(HG):
                        dst = v_dram[group + hg, cc * CH:(cc + 1) * CH, :].rearrange("(j p) n -> p j n", p=P)
                        sp.dma_start(dst, vt[:, a, :, hg * P:(hg + 1) * P]).then_inc(v_stored[a], 16)
            for n in range(2):
                sp.wait_ge(xn_stored[n], 16 * (NCH // 2))
                sp.wait_ge(v_stored[n], 16 * HG * NCH)
            for n in range(RING):
                sp.wait_ge(parts_stored[n], 16 * SPLIT * (NQK // RING) * NCH)

        @block.vector
        def _(dve):
            dve.memset(none[:, 0:1], 0.0).then_inc(copied, CREDIT)
            dve.memset(none[:, 1:2], 0.0).then_inc(lo_ready, RING)
            dve.memset(none[:, 2:3], 0.0).then_inc(rest_ready, RING)
            dve.memset(none[:, 3:4], 0.0).then_inc(unit_ready, 2 * UNITS)
            dve.memset(vt[:, :, :, :], 0.0).then_inc(vt_set, 1)
            dve.wait_ge(vt_set, 1)
            v_ones = vt[:, :, :, :].rearrange("p a j (h w) -> p (a j h) w", w=VW)[:, :, HD:HD + 1]
            dve.memset(v_ones, 1.0).then_inc(vt_set, 1)

            def norm(c, n, src, dst):
                done = c * 4 + 2 * n
                for j in range(TPC):
                    last = dve.bn_stats(stats[:, j, :], src[:, j, :])
                last.then_inc(norm_step, 1)
                dve.wait_ge(norm_step, done + 1)
                dve.memset(none[:, 4:5], 0.0)
                for j in range(TPC):
                    last = dve.bn_aggr(meanvar[:, j, :], stats[:, j, :])
                last.then_inc(var_ready, 1)
                dve.wait_ge(std_ready, c * 2 + (n + 1))
                dve.reciprocal(rstd[:, :], std[:, :]).then_inc(norm_step, 1)
                dve.wait_ge(norm_step, done + 2)
                for j in range(TPC):
                    last = dve.tensor_scalar(dst[:, j, :], src[:, j, :], meanvar[:, j, 0:1], rstd[:, j:j + 1],
                                             ALU.subtract, ALU.mult)
                return last

            def norms(i, u):
                c, par = i * 2 + u, u % 2
                dve.wait_ge(x_in[par], i * 16 + 16 * (u // 2 + 1))
                dve.wait_ge(unit_ready, c * UNITS + C_UNIT)
                dve.wait_ge(xn_stored[par], i * 16 + 16 * (u // 2))
                norm(c, 0, xs[:, par], xn[:, par]).then_inc(xn_ready, 1)
                dve.wait_ge(xn_ready, c + 1)
                norm(c, 1, xn[:, par], hn[:, par]).then_inc(hn_ready, 1)

            def split(i, u, r):
                c, slot = i * 2 + u, r % RING
                n = c * NQK + r
                dve.wait_ge(copied, unit(c, QK[r]))
                dve.wait_ge(lo_ready, n + 1)
                dve.tensor_tensor(rest[:, slot, :], qf[:, slot, :], parts[:, slot, 0, :],
                                  ALU.subtract).then_inc(rest_ready, 1)
                dve.wait_ge(rest_ready, n + (1 + RING))
                dve.tensor_copy(parts[:, slot, 1, :], rest[:, slot, :]).then_inc(mid_ready, 1)

            def chunk(i, u, more):
                for r in range(NQK // 2):
                    split(i, u, r)
                if more:
                    norms(i, u + 1)
                for r in range(NQK // 2, NQK):
                    split(i, u, r)

            norms(0, 0)
            with dve.Fori(0, NCH // 2 - 1) as i:
                for u in range(2):
                    chunk(i, u, True)
            chunk(NCH // 2 - 1, 0, True)
            chunk(NCH // 2 - 1, 1, False)

        @block.gpsimd
        def _(pool):
            with pool.Fori(0, NCH // 2) as i:
                for k in range(2 * NQK):
                    slot = k % RING
                    pool.wait_ge(mid_ready, i * (2 * NQK) + (k + 1))
                    pool.tensor_tensor(parts[:, slot, 2, :], rest[:, slot, :], parts[:, slot, 1, :],
                                       ALU.subtract).then_inc(lo_ready, 1)

        @block.scalar
        def _(act):
            act.wait_ge(vt_set, 2)

            def roots(i, u):
                c = i * 2 + u
                for n in range(2):
                    act.wait_ge(var_ready, c * 2 + (n + 1))
                    act.activation(std[:, :], meanvar[:, :, 1], ACT.Sqrt, bias=const["eps"][:, 0:1]).then_inc(std_ready, 1)

            def chunk(i, u, more):
                c = i * 2 + u
                for k in range(UNITS):
                    src, how = banks[:, k % 8, :], {}
                    if more and k == QK[NQK // 2]:
                        roots(i, u + 1)
                    if k < 2:
                        out = xnT[:, k, :]
                    elif k < 4:
                        out = hT[:, k - 2, :]
                        how = {"scale": const["ln1w"][:, k - 2:k - 1], "bias": const["ln1b"][:, k - 2:k - 1]}
                    elif k == C_UNIT:
                        out = cT[:, :]
                    elif k in QK:
                        r = QK.index(k)
                        out = qf[:, r % RING, :]
                        if r < NQK // 2:
                            how = {"bias": const[("qb", "kb")[r // 2]][:, r % 2:r % 2 + 1]}
                    else:
                        a = int(k >= V_FFN)
                        half = k - (V_LOW, V_FFN)[a]
                        if half == 0:
                            act.wait_ge(v_stored[1 - a], c * (16 * HG))
                        out = vt[:, 1 - a, 2 * half:2 * half + 2, :].rearrange("p j (h w) -> p (j h) w", w=VW)[:, :, 0:HD]
                        src = src.rearrange("p (n w) -> p n w", w=HD)
                    if k in QK:
                        act.wait_ge(rest_ready, c * NQK + (r + 1))
                        act.wait_ge(unit_ready, c * UNITS + (k + 1 + 2 * UNITS))
                        act.activation(out, src, ACT.Identity, **how)
                        act.wait_ge(parts_stored[r % RING], c * (16 * SPLIT * NQK // RING) + 16 * SPLIT * (r // RING))
                        out = parts[:, r % RING, 0, :]
                    else:
                        act.wait_ge(unit_ready, c * UNITS + (k + 1 + 2 * UNITS))
                    act.activation(out, src, ACT.Identity, **how).then_inc(copied, 1)

            roots(0, 0)
            with act.Fori(0, NCH // 2 - 1) as i:
                for u in range(2):
                    chunk(i, u, True)
            chunk(NCH // 2 - 1, 0, True)
            chunk(NCH // 2 - 1, 1, False)

        @block.tensor
        def _(pe):
            with pe.Fori(0, NCH // 2) as i:
                for u in range(2):
                    c = i * 2 + u
                    for k in range(UNITS):
                        bank = banks[:, k % 8, :]
                        pe.wait_ge(copied, unit(c, k - 8) if k >= 8 else unit(c, (16 if k == 0 else k + 8) - UNITS))
                        if k in (0, 2):
                            pe.wait_ge((xn_ready, hn_ready)[k // 2], c + 1)
                        if k == C_UNIT:
                            pe.wait_ge(copied, unit(c, 3))
                        if k == QK[NQK // 2]:
                            pe.wait_ge(copied, unit(c, C_UNIT))
                        if k < C_UNIT:
                            src = (xn, hn)[k // 2]
                            for j in range(TPC):
                                last = pe.transpose(bank[:, j * P:(j + 1) * P], src[:, u, j, (k % 2) * P:(k % 2 + 1) * P],
                                                    const["ident"][:, :])
                        elif k == C_UNIT:
                            for h in range(KD):
                                last = pe.matmul(bank, const["wd"][:, h, :], xnT[:, h, :], start=h == 0, stop=h == KD - 1)
                        elif k in QK[:4]:
                            r = QK.index(k)
                            w = const[("qw", "kw")[r // 2]]
                            for h in range(KD):
                                last = pe.matmul(bank, w[:, h, (r % 2) * P:(r % 2 + 1) * P], hT[:, h, :],
                                                 start=h == 0, stop=h == KD - 1)
                        elif k in QK:
                            r = QK.index(k) - 4
                            last = pe.matmul(bank, const["wu"][:, r // 2, (r % 2) * P:(r % 2 + 1) * P], cT[:, :],
                                             start=True, stop=True)
                        else:
                            a = int(k >= V_FFN)
                            half = k - (V_LOW, V_FFN)[a]
                            for j in range(2):
                                out = bank[:, j * D:(j + 1) * D]
                                tokens = slice((2 * half + j) * P, (2 * half + j + 1) * P)
                                if a == 0:
                                    last = pe.matmul(out, cT[:, tokens], const["wu"][:, 2, :], start=True, stop=True)
                                else:
                                    for h in range(KD):
                                        last = pe.matmul(out, hT[:, h, tokens], const["vw"][:, h, :],
                                                         start=h == 0, stop=h == KD - 1)
                        last.then_inc(unit_ready, 1)


def group_order(exps, maxima):
    n_m = len(ROW_BLOCKS) if maxima else 0
    if not exps:
        return [("M", m) for m in range(n_m)] + [("N", 0)]
    order, m, turn = [], 0, None
    ahead, last = 10, len(SCORE_BLOCKS) - 20
    for n in range(len(SCORE_BLOCKS)):
        while m < n_m and (m < ahead or (m - ahead) * last < n * (n_m - ahead)):
            order.append(("M", m))
            m += 1
        order.append(("S", n))
        if maxima and n == last + 8:
            order.append(("N", 0))
        if n % GH == GH - 1 and n >= GH:
            batch = n // GH - 1
            order.append(("PV", batch))
            if turn is not None:
                order.append(("T", turn))
                turn = None
            if batch in CHUNK_ENDS:
                turn = CHUNK_ENDS.index(batch)
    order.append(("PV", len(SCORE_BLOCKS) // GH - 1))
    order.append(("T", S // CH - 1))
    return order


ROW_BLOCKS = [(h, t, c) for t in range(S // P) for h in range(GH) for c in range(t // TPC + 1)]
SCORE_BLOCKS = [(q, k, h) for q in range(S // CH) for k in range(TPC * (q + 1)) for h in range(GH)]
CHUNK_ENDS = [TPC * (q + 1) * (q + 2) // 2 - 1 for q in range(S // CH)]


def stage_b(nc, scratch, const):
    xin_dram, q_dram, k_dram, v_dram, ctx_dram = scratch
    SLOTS = 3
    NM, NS = len(ROW_BLOCKS) + 1, len(SCORE_BLOCKS)
    NB, NQ = NS // GH, S // CH
    PR = 8
    LOADS = 16 * 11
    MROWS = 16 * SPLIT * GH
    FILLS = 16
    with ExitStack() as ctx:
        def sb(name, shape, dt=F32):
            return ctx.enter_context(nc.sbuf_tensor(name, shape, dt))

        def sem(name):
            return ctx.enter_context(nc.semaphore(name))

        qs = sb("qs", [STACK, SLOTS, GH, S], BF16)
        ks = sb("ks", [STACK, SLOTS, GH, S], BF16)
        vs = sb("vs", [P, SLOTS, S // P, GH * VW])
        probs = sb("probs", [P, PR, CH])
        pv_sb = sb("pv_sb", [P, 2, CH])
        inv = sb("inv", [P, 2, TPC, GH])
        ctx_sb = sb("ctx_sb", [P, 2, TPC, GH, HD])
        rowmax = sb("rowmax", [P, GH, S // P, NQ])
        unused = sb("unused", [P, GH, CH], BF16)
        negmax = sb("negmax", [P, P])
        mrest = sb("mrest", [GH * S // P, P])
        mrows = sb("mrows", [GH * S // P, SPLIT, P], BF16)
        none = sb("b_none", [P, 8])
        dve_pause = sb("dve_pause", [P, GH])
        zeros = sb("zeros", [P, E * CAP * D // P // FILLS])
        m_banks = ctx.enter_context(nc.psum_tensor("m_banks", [P, SLOTS, CH], F32))
        s_banks = ctx.enter_context(nc.psum_tensor("s_banks", [P, SLOTS, CH], F32))
        v_banks = ctx.enter_context(nc.psum_tensor("v_banks", [P, 2, CH], F32))

        loaded = [sem(f"loaded{i}") for i in range(SLOTS)]
        m_ready = sem("m_ready")
        m_used = sem("m_used")
        cleared = sem("cleared")
        negmax_ready = sem("negmax_ready")
        m_step = sem("m_step")
        mrows_ready = sem("mrows_ready")
        mrows_in = sem("mrows_in")
        s_ready = sem("s_ready")
        p_ready = sem("p_ready")
        p_used = sem("p_used")
        pv_copied = sem("pv_copied")
        turned = sem("turned")
        inv_ready = sem("inv_ready")
        ctx_ready = sem("ctx_ready")
        ctx_stored = [sem(f"ctx_stored{i}") for i in range(2)]
        ones_set = sem("ones_set")
        zeros_set = sem("zeros_set")
        filled = sem("filled")

        block = ctx.enter_context(nc.Block())

        def at(i, u, per, off):
            return i * (SLOTS * per) + (u * per + off)

        @block.sync
        def _(sp):
            def load(i, u, g):
                slot = (u + 2) % SLOTS
                rows = k_dram[g].rearrange("h r t -> r h t")
                for at_row, n in ((0, 3), (3, 2), (5, 1)):
                    sp.dma_start(ks[at_row * HD:(at_row + n) * HD, slot], rows[0:n * HD]).then_inc(loaded[slot], 16)
                rows = q_dram[g].rearrange("h r t -> r h t")
                for n, part in enumerate((0, 0, 0, 1, 1, 2)):
                    sp.dma_start(qs[n * HD:(n + 1) * HD, slot], rows[part * HD:(part + 1) * HD]).then_inc(loaded[slot], 16)
                tiles = v_dram[g].rearrange("(k p) n -> p k n", p=P)
                for n in range(0, S // P, S // P // 2):
                    sp.dma_start(vs[:, slot, n:n + S // P // 2], tiles[:, n:n + S // P // 2]).then_inc(loaded[slot], 16)

            def maxima(i, u):
                slot = (u + 1) % SLOTS
                sp.wait_ge(mrows_ready, at(i, u, 1, 2))
                for h in range(GH):
                    for part in range(SPLIT):
                        row = PAIR_ROWS + part
                        sp.dma_start(qs[row:row + 1, slot, h, :], mrows[h * (S // P):(h + 1) * (S // P), part, :])\
                            .then_inc(mrows_in, 16)

            load(-1, 1, 0)
            load(-1, 2, 1)
            maxima(-1, 2)

            def store(i, u, q):
                sp.wait_ge(ctx_ready, at(i, u, NQ, q + 1 + 2))
                dst = ctx_dram[i * SLOTS + u, q * CH:(q + 1) * CH, :].rearrange("(j p) n -> p j n", p=P)
                sp.dma_start(dst, ctx_sb[:, q % 2].rearrange("p j h w -> p j (h w)")).then_inc(ctx_stored[q % 2], 16)

            def step(i, u, g, more):
                if more:
                    sp.wait_ge(p_used, at(i, u, NB, PR // GH))
                    load(i, u, g)
                for q in range(NQ - 1):
                    store(i, u, q)
                maxima(i, u)
                store(i, u, NQ - 1)

            with sp.Fori(0, 4) as i:
                for u in range(SLOTS):
                    step(i, u, i * SLOTS + (u + 2), True)
            for s in range(12, G - 1):
                step(s // SLOTS, s % SLOTS, s + 2, s + 2 < G)
            for q in range(NQ):
                store(G // SLOTS, 0, q)
            for n in range(2):
                sp.wait_ge(ctx_stored[n], 16 * G * NQ // 2)
            sp.wait_ge(filled, 16 * FILLS)

        @block.gpsimd
        def _(pool):
            pool.memset(zeros[:, :], 0.0).then_inc(zeros_set, 1)
            pool.wait_ge(zeros_set, 1)
            pool.memset(ks[PAIR_ROWS:STACK, :, :, :], 1.0).then_inc(ones_set, 1)
            fill = xin_dram.rearrange("(f p r) d -> f p (r d)", f=FILLS, p=P)
            for n in range(FILLS):
                pool.dma_start(fill[n], zeros[:, :]).then_inc(filled, 16)

        @block.tensor
        def _(pe):
            def step(i, u, exps, maxima):
                now, nxt = u % SLOTS, (u + 1) % SLOTS
                for what, n in group_order(exps, maxima):
                    if what == "S":
                        q, k, h = SCORE_BLOCKS[n]
                        first = max(k - TPC * q, 0) * P
                        bank = s_banks[:, (u * NS + n) % SLOTS, 0:CH - first]
                        if n == 0:
                            pe.wait_ge(mrows_in, at(i, u, MROWS, MROWS))
                        pe.wait_ge(p_ready, at(i, u, NS, n + 1))
                        diagonal = k >= TPC * q
                        ins = pe.matmul(bank, ks[:, now, h, k * P:(k + 1) * P],
                                        qs[:, now, h, q * CH + first:(q + 1) * CH], start=True, stop=not diagonal)
                        if diagonal:
                            ins = pe.matmul(bank[:, 0:P], const["identb"][:, :], const["maskk"][:, :], start=False, stop=True)
                        ins.then_inc(s_ready, 1)
                    elif what == "M":
                        h, t, c = ROW_BLOCKS[n]
                        width = min(CH, (t + 1) * P - c * CH)
                        bank = m_banks[:, ((u + 1) * NM + n) % SLOTS, 0:width]
                        if n == 0:
                            pe.wait_ge(loaded[nxt], (i + (u + 1) // SLOTS) * LOADS + LOADS)
                        pe.wait_ge(m_used, at(i, u, NM, NM + n + 1))
                        ins = pe.matmul(bank, qs[0:PAIR_ROWS, nxt, h, t * P:(t + 1) * P],
                                        ks[0:PAIR_ROWS, nxt, h, c * CH:c * CH + width], start=True, stop=True)
                        ins.then_inc(m_ready, 1)
                    elif what == "N":
                        bank = m_banks[:, ((u + 1) * NM + NM - 1) % SLOTS, 0:P]
                        pe.wait_ge(m_used, at(i, u, NM, NM + NM))
                        pe.wait_ge(negmax_ready, at(i, u, 1, 2))
                        pe.transpose(bank, negmax[:, :], const["ident"][:, :]).then_inc(m_ready, 1)
                    elif what == "PV":
                        q, k, _ = SCORE_BLOCKS[n * GH]
                        first = max(k - TPC * q, 0) * P
                        if k == 0:
                            pe.wait_ge(ctx_ready, at(i, u, NQ, q + 1))
                        pe.wait_ge(p_ready, at(i, u, NS, GH * (n + 1) + SLOTS))
                        for h in range(GH):
                            rows = slice(h * VW, (h + 1) * VW)
                            ins = pe.matmul(v_banks[rows, q % 2, first:CH], vs[:, now, k, rows],
                                            probs[:, (n * GH + h) % PR, 0:CH - first],
                                            start=k == 0, stop=k == TPC * (q + 1) - 1, tile_position=(0, h * VW))
                        ins.then_inc(p_used, 1)
                    elif what == "T":
                        pe.wait_ge(pv_copied, at(i, u, NQ, n + 1))
                        for t in range(TPC):
                            ins = pe.transpose(v_banks[:, n % 2, t * P:(t + 1) * P], pv_sb[:, n % 2, t * P:(t + 1) * P],
                                               const["ident"][:, :])
                        ins.then_inc(turned, 1)

            step(-1, 2, False, True)
            pe.wait_ge(ones_set, 1)
            with pe.Fori(0, G // SLOTS) as i:
                for u in range(SLOTS):
                    step(i, u, True, True)
            step(G // SLOTS, 0, True, False)

        @block.scalar
        def _(act):
            def step(i, u, maxima):
                for what, n in group_order(True, maxima):
                    if what == "S":
                        q, k, h = SCORE_BLOCKS[n]
                        width = CH - max(k - TPC * q, 0) * P
                        if h == 0:
                            act.wait_ge(p_used, at(i, u, NB, n // GH + 1))
                        act.wait_ge(s_ready, at(i, u, NS, n + 1))
                        act.activation(probs[:, n % PR, 0:width], s_banks[:, (u * NS + n) % SLOTS, 0:width],
                                       ACT.Exp, scale=SCALE).then_inc(p_ready, 1)
                    elif what == "PV" and n in CHUNK_ENDS:
                        q = CHUNK_ENDS.index(n)
                        act.wait_ge(turned, at(i, u, NQ, q + 1))
                        act.wait_ge(p_used, at(i, u, NB, n + 1 + PR // GH))
                        act.activation(pv_sb[:, q % 2, :], v_banks[:, q % 2, :], ACT.Copy).then_inc(pv_copied, 1)

            with act.Fori(0, G // SLOTS) as i:
                for u in range(SLOTS):
                    step(i, u, True)
            step(G // SLOTS, 0, False)

        @block.vector
        def _(dve):
            dve.memset(none[:, 0:1], 0.0).then_inc(m_used, SLOTS)
            dve.memset(none[:, 1:2], 0.0).then_inc(p_ready, SLOTS)
            dve.memset(none[:, 2:3], 0.0).then_inc(p_used, PR // GH)
            dve.memset(none[:, 3:4], 0.0).then_inc(ctx_ready, 2)
            dve.memset(none[:, 4:5], 0.0).then_inc(turned, 2)
            dve.memset(rowmax[:, :, :, :], NEG)
            dve.memset(negmax[:, :], 0.0).then_inc(cleared, 1)
            dve.wait_ge(cleared, 1)

            def step(i, u, exps, maxima):
                for what, n in group_order(exps, maxima):
                    if what == "M":
                        h, t, c = ROW_BLOCKS[n]
                        width = min(CH, (t + 1) * P - c * CH)
                        dve.wait_ge(m_ready, at(i, u, NM, NM + n + 1))
                        scores = m_banks[:, ((u + 1) * NM + n) % SLOTS, 0:width]
                        if c == t // TPC:
                            dve.memset(dve_pause[:, n % GH:n % GH + 1], 0.0)
                            dve.tensor_tensor_reduce(unused[:, n % GH, 0:width], scores, const["maskq"][:, CH - width:CH], 1.0, NEG,
                                                     ALU.add, ALU.max, rowmax[:, h, t, c:c + 1]).then_inc(m_used, 1)
                        else:
                            dve.tensor_reduce(rowmax[:, h, t, c:c + 1], scores, AX.X, ALU.max).then_inc(m_used, 1)
                        if n == NM - 2:
                            dve.wait_ge(m_used, at(i, u, NM, NM + NM - 1 + SLOTS))
                            dve.tensor_reduce(negmax[:, 0:GH * S // P], rowmax[:, :, :, :].rearrange("p h t c -> p (h t) c"),
                                              AX.X, ALU.max, negate=True).then_inc(negmax_ready, 1)
                    elif what == "N":
                        bank = m_banks[0:GH * S // P, ((u + 1) * NM + NM - 1) % SLOTS, 0:P]
                        dve.wait_ge(m_ready, at(i, u, NM, NM + NM))
                        dve.wait_ge(mrows_in, at(i, u, MROWS, MROWS))
                        dve.tensor_copy(mrows[:, 0, :], bank).then_inc(m_step, 1)
                        dve.wait_ge(m_step, at(i, u, 3, 3 + 1))
                        dve.tensor_tensor(mrest[:, :], bank, mrows[:, 0, :], ALU.subtract).then_inc(m_used, 1)
                        dve.wait_ge(m_used, at(i, u, NM, NM + NM + SLOTS))
                        dve.tensor_copy(mrows[:, 1, :], mrest[:, :]).then_inc(m_step, 2)
                        dve.wait_ge(m_step, at(i, u, 3, 3 + 3))
                        dve.tensor_tensor(mrows[:, 2, :], mrest[:, :], mrows[:, 1, :], ALU.subtract).then_inc(mrows_ready, 1)
                    elif what == "T":
                        heads = v_banks[:, n % 2, :].rearrange("p (j h w) -> p (j h) w", h=GH, w=VW)
                        dve.wait_ge(turned, at(i, u, NQ, n + 1 + 2))
                        dve.reciprocal(inv[:, n % 2].rearrange("p j h -> p (j h)"), heads[:, :, HD]).then_inc(inv_ready, 1)
                        dve.wait_ge(inv_ready, at(i, u, NQ, n + 1))
                        dve.wait_ge(ctx_stored[n % 2], at(i, u, 16 * NQ // 2, 16 * (n // 2)))
                        dve.tensor_tensor(ctx_sb[:, n % 2].rearrange("p j h w -> p (j h) w"), heads[:, :, 0:HD],
                                          inv[:, n % 2].rearrange("p j h -> p (j h)").unsqueeze(2).to_broadcast([P, TPC * GH, HD]),
                                          ALU.mult).then_inc(ctx_ready, 1)

            step(-1, 2, False, True)
            with dve.Fori(0, G // SLOTS) as i:
                for u in range(SLOTS):
                    step(i, u, True, True)
            step(G // SLOTS, 0, True, False)


def stage_c(nc, x, scratch, const, keep):
    xn_dram, ctx_dram = scratch
    xt, base, logits = keep
    FRONT, BACK = 8, 3
    TURNS, SUMS = 4, 4
    FRONT_BANK = [0, 1, 2, 3, 4, 5, 0, 1]
    BACK_BANK = [6, 7, 2]
    with ExitStack() as ctx:
        def sb(name, shape, dt=F32):
            return ctx.enter_context(nc.sbuf_tensor(name, shape, dt))

        def sem(name):
            return ctx.enter_context(nc.semaphore(name))

        xs = sb("c_xs", [P, 2, TPC, D])
        xn = sb("c_xn", [P, 2, TPC, D])
        att = sb("att", [P, 2, 2, TPC, HG, GH * HD])
        attT = sb("attT", [P, 2, KD, CH])
        xtT = sb("xtT", [P, KD, CH])
        hidden = sb("hidden", [P, TPC, D])
        xt_now = sb("xt_now", [P, 2, TPC, D])
        sums = sb("sums", [P, TPC, D])
        stats = sb("c_stats", [P, TPC, 6])
        meanvar = sb("c_meanvar", [P, TPC, 2])
        std = sb("c_std", [P, TPC])
        rstd = sb("c_rstd", [P, TPC])
        none = sb("c_none", [P, 8])
        banks = ctx.enter_context(nc.psum_tensor("c_banks", [P, 8, CH], F32))

        arrived = [sem(f"arrived{i}") for i in range(2)]
        front_ready = sem("front_ready")
        back_ready = sem("back_ready")
        turned = sem("c_turned")
        back_out = sem("back_out")
        biased = sem("biased")
        added = sem("c_added")
        norm_step = sem("c_norm_step")
        var_ready = sem("c_var_ready")
        std_ready = sem("c_std_ready")
        xt_ready = sem("c_xt_ready")
        xt_kept = sem("xt_kept")
        sums_ready = sem("c_sums_ready")

        block = ctx.enter_context(nc.Block())
        x_chunks = x.rearrange("b (c j p) d -> (b c) p j d", j=TPC, p=P)
        xn_chunks = xn_dram.rearrange("(c j p) d -> c p j d", j=TPC, p=P)
        ARRIVED = 16 * (2 + 2 * HG)

        @block.sync
        def _(sp):
            for c in range(NCH):
                u, b, cc = c % 2, c // (NCH // B), c % (NCH // B)
                if c >= 2:
                    sp.wait_ge(added, SUMS * c)
                for a in range(2):
                    for hg in range(HG):
                        src = ctx_dram[(a * B + b) * HG + hg, cc * CH:(cc + 1) * CH, :].rearrange("(j p) n -> p j n", p=P)
                        sp.dma_start(att[:, u, a, :, hg, :], src).then_inc(arrived[u], 16)
                sp.dma_start(xn[:, u], xn_chunks[c]).then_inc(arrived[u], 16)
                sp.dma_start(xs[:, u], x_chunks[c]).then_inc(arrived[u], 16)

        @block.gpsimd
        def _(pool):
            with pool.Fori(0, NCH // 2) as i:
                for u in range(2):
                    c = i * 2 + u
                    pool.wait_ge(arrived[u], i * ARRIVED + ARRIVED)
                    pool.tensor_tensor(xn[:, u], xn[:, u], const["ob"][:, :].unsqueeze(1).to_broadcast([P, TPC, D]),
                                       ALU.add).then_inc(biased, 1)
                    pool.wait_ge(added, c * SUMS + (2 + SUMS))
                    pool.tensor_tensor(sums[:, :, :], hidden[:, :, :], xs[:, u], ALU.add).then_inc(sums_ready, 1)
                    pool.wait_ge(xt_ready, c + 1)
                    pool.tensor_copy(xt[:, bass.ds(i * (2 * TPC) + u * TPC, TPC), :], xt_now[:, u]).then_inc(xt_kept, 1)

        @block.vector
        def _(dve):
            dve.memset(none[:, 0:1], 0.0).then_inc(turned, TURNS)
            dve.memset(none[:, 1:2], 0.0).then_inc(added, SUMS)
            dve.memset(none[:, 2:3], 0.0).then_inc(xt_kept, 2)
            dve.memset(none[:, 3:4], 0.0).then_inc(back_out, BACK)
            with dve.Fori(0, NCH // 2) as i:
                for u in range(2):
                    c = i * 2 + u
                    tiles = i * (2 * TPC) + u * TPC
                    dve.wait_ge(biased, c + 1)
                    dve.wait_ge(sums_ready, c)
                    for half in range(2):
                        k = TURNS + half
                        dve.wait_ge(front_ready, c * FRONT + (k + 1))
                        pair = slice(2 * half, 2 * half + 2)
                        dve.tensor_tensor(hidden[:, pair, :], banks[:, FRONT_BANK[k], :].rearrange("p (j d) -> p j d", d=D),
                                          xn[:, u, pair, :], ALU.add).then_inc(added, 1)
                    dve.wait_ge(added, c * SUMS + (2 + SUMS))
                    for j in range(TPC):
                        last = dve.bn_stats(stats[:, j, :], hidden[:, j, :])
                    last.then_inc(norm_step, 1)
                    dve.wait_ge(norm_step, c * 4 + 1)
                    dve.memset(none[:, 4:5], 0.0)
                    for j in range(TPC):
                        last = dve.bn_aggr(meanvar[:, j, :], stats[:, j, :])
                    last.then_inc(var_ready, 1)
                    dve.wait_ge(std_ready, c + 1)
                    dve.reciprocal(rstd[:, :], std[:, :]).then_inc(norm_step, 1)
                    dve.wait_ge(norm_step, c * 4 + 2)
                    dve.wait_ge(xt_kept, c + 1)
                    for j in range(TPC):
                        last = dve.tensor_scalar(xt_now[:, u, j, :], hidden[:, j, :], meanvar[:, j, 0:1],
                                                 rstd[:, j:j + 1], ALU.subtract, ALU.mult)
                    last.then_inc(norm_step, 1)
                    now = xt_now[:, u]
                    dve.wait_ge(norm_step, c * 4 + 3)
                    dve.tensor_tensor(now, now, const["ln2w"][:, :].unsqueeze(1).to_broadcast([P, TPC, D]),
                                      ALU.mult).then_inc(norm_step, 1)
                    dve.wait_ge(norm_step, c * 4 + 4)
                    dve.tensor_tensor(now, now, const["ln2b"][:, :].unsqueeze(1).to_broadcast([P, TPC, D]),
                                      ALU.add).then_inc(xt_ready, 1)
                    dve.wait_ge(sums_ready, c + 1)
                    for half in range(2):
                        k = TURNS + 2 + half
                        dve.wait_ge(front_ready, c * FRONT + (k + 1))
                        dve.tensor_tensor(base[:, bass.ds(tiles + 2 * half, 2), :],
                                          banks[:, FRONT_BANK[k], :].rearrange("p (j d) -> p j d", d=D),
                                          sums[:, 2 * half:2 * half + 2, :], ALU.add).then_inc(added, 1)

        @block.scalar
        def _(act):
            def turn(c):
                for k in range(TURNS):
                    how = {"bias": const["vb"][:, k:k + 1]} if k < KD else {}
                    act.wait_ge(front_ready, c * FRONT + (k + 1))
                    act.activation(attT[:, k // 2, k % 2, :], banks[:, FRONT_BANK[k], :], ACT.Identity, **how).then_inc(turned, 1)

            def root(c):
                act.wait_ge(var_ready, c + 1)
                act.activation(std[:, :], meanvar[:, :, 1], ACT.Sqrt, bias=const["eps"][:, 0:1]).then_inc(std_ready, 1)

            def back(c, tiles):
                for k in range(BACK):
                    src, out = banks[:, BACK_BANK[k], :], None
                    if k < KD:
                        out = xtT[:, k, :]
                    else:
                        out = logits[:, bass.ds(tiles, TPC), :]
                        src = src[:, 0:TPC * E].rearrange("p (j e) -> p j e", e=E)
                    act.wait_ge(back_ready, c * BACK + (k + 1))
                    act.activation(out, src, ACT.Copy).then_inc(back_out, 1)

            turn(0)
            root(0)
            with act.Fori(0, NCH // 2 - 1) as i:
                for u in range(2):
                    c = i * 2 + (u + 1)
                    turn(c)
                    back(i * 2 + u, i * (2 * TPC) + u * TPC)
                    root(c)
            turn(NCH - 1)
            back(NCH - 2, (NCH - 2) * TPC)
            root(NCH - 1)
            back(NCH - 1, (NCH - 1) * TPC)

        @block.tensor
        def _(pe):
            def front(i, u):
                c, par = i * 2 + u, u % 2
                for k in range(FRONT):
                    bank = banks[:, FRONT_BANK[k], :]
                    if k == 0:
                        pe.wait_ge(arrived[par], i * ARRIVED + ARRIVED * (1 + u // 2))
                    if k < 2:
                        pe.wait_ge(added, c * SUMS + (3 + k))
                    elif k == 2:
                        pe.wait_ge(back_out, c * BACK)
                    elif k == 3:
                        pe.wait_ge(turned, c * TURNS + TURNS)
                    elif k < 6:
                        pe.wait_ge(added, c * SUMS + (k - 3))
                    if k == 4:
                        pe.wait_ge(turned, c * TURNS + (KD + TURNS))
                    elif k == 6:
                        pe.wait_ge(turned, c * TURNS + 2 * TURNS)
                    if k < TURNS:
                        for j in range(TPC):
                            src = att[:, par, k // 2, j, 2 * (k % 2):2 * (k % 2) + 2, :].rearrange("p g w -> p (g w)")
                            last = pe.transpose(bank[:, j * P:(j + 1) * P], src, const["ident"][:, :])
                    else:
                        a = (k - TURNS) // 2
                        for j in range(2):
                            tile = 2 * (k % 2) + j
                            for h in range(KD):
                                last = pe.matmul(bank[:, j * D:(j + 1) * D], attT[:, a, h, tile * P:(tile + 1) * P],
                                                 const[("ow", "Wo")[a]][:, h, :], start=h == 0, stop=h == KD - 1)
                    last.then_inc(front_ready, 1)

            def back(i, u, newest):
                c = i * 2 + u
                for k in range(BACK):
                    bank = banks[:, BACK_BANK[k], :]
                    if k < KD:
                        pe.wait_ge(back_out, c * BACK + (k + 1))
                        if k == 0:
                            pe.wait_ge(xt_ready, c + 1)
                    else:
                        pe.wait_ge(back_out, c * BACK + (KD + BACK))
                        pe.wait_ge(turned, newest * TURNS + (3 + TURNS))
                    for j in range(TPC):
                        cols = slice(j * P, (j + 1) * P)
                        if k < KD:
                            last = pe.transpose(bank[:, cols], xt_now[:, u, j, k * P:(k + 1) * P], const["ident"][:, :])
                        else:
                            for h in range(KD):
                                last = pe.matmul(bank[:, j * E:(j + 1) * E], xtT[:, h, cols], const["rw"][:, h, :],
                                                 start=h == 0, stop=h == KD - 1)
                    last.then_inc(back_ready, 1)

            front(0, 0)
            with pe.Fori(0, NCH // 2 - 1) as i:
                for u in range(2):
                    front(i, u + 1)
                    back(i, u, i * 2 + (u + 1))
            last_pair = NCH // 2 - 1
            front(last_pair, 1)
            back(last_pair, 0, NCH - 1)
            back(last_pair, 1, NCH - 1)


def stage_d(nc, scratch, const, keep):
    xin_dram, = scratch
    xt, logits, gates, gather_row = keep
    with ExitStack() as ctx:
        def sb(name, shape, dt=F32):
            return ctx.enter_context(nc.sbuf_tensor(name, shape, dt))

        def sem(name):
            return ctx.enter_context(nc.semaphore(name))

        cube = [P, NTILE, E]
        flat = [P, NTILE]
        probs, other, expert_ids = sb("d_probs", cube), sb("d_other", cube), sb("expert_ids", cube)
        ids_int = sb("ids_int", [P, NTILE * E], mybir.dt.int32)
        mask = [sb(f"mask{n}", cube) for n in range(2)]
        place = [sb(f"place{n}", cube) for n in range(2)]
        total = [sb(f"total{n}", cube) for n in range(2)]
        upto = [sb(f"upto{n}", cube) for n in range(2)]
        kept = [sb(f"kept{n}", cube) for n in range(2)]
        work = sb("d_work", cube)
        top8 = sb("top8", [P, NTILE, 8])
        top8_id = sb("top8_id", [P, NTILE, 8], U32)
        expert = [sb(f"expert{n}", flat) for n in range(2)]
        slot = [sb(f"slot{n}", flat) for n in range(2)]
        any_kept = [sb(f"any_kept{n}", flat) for n in range(2)]
        one, two, denom = sb("d_one", flat), sb("d_two", flat), sb("denom", flat)
        scatter_row = [sb(f"scatter_row{n}", flat, U32) for n in range(2)]
        ones_cube = sb("ones_cube", [P, NTILE])
        banks = ctx.enter_context(nc.psum_tensor("d_banks", [P, 4, CH], F32))

        step_done = sem("d_step_done")
        shifted = sem("d_shifted")
        exped = sem("d_exped")
        ids_ready = sem("ids_ready")
        masks_ready = sem("masks_ready")
        counted = sem("counted")
        rows_ready = sem("rows_ready")
        scattered = sem("scattered")

        block = ctx.enter_context(nc.Block())

        @block.tensor
        def _(pe):
            for n in range(2):
                pe.wait_ge(masks_ready, n + 1)
                m = mask[n][:, :, :].rearrange("p t e -> p (t e)")
                pe.matmul(banks[:, 2 * n, :], const["upper"][:, :], m, start=True, stop=True)
                pe.matmul(banks[:, 2 * n + 1, :], const["ones"][:, :], m, start=True, stop=True).then_inc(counted, 1)

        @block.scalar
        def _(act):
            act.wait_ge(shifted, 1)
            act.activation(probs[:, :, :], work[:, :, :], ACT.Exp).then_inc(exped, 1)

        @block.gpsimd
        def _(pool):
            pool.iota(ids_int[:, :], [[0, NTILE], [1, E]], base=0, channel_multiplier=0).then_inc(ids_ready, 1)
            for n in range(2):
                pool.wait_ge(rows_ready, n + 1)
                for t in range(NTILE):
                    pool.indirect_dma_start(out=xin_dram, out_offset=bass.IndirectOffsetOnAxis(ap=scatter_row[n][:, t:t + 1], axis=0),
                                            in_=xt[:, t, :], in_offset=None, bounds_check=E * CAP - 1,
                                            oob_is_err=False).then_inc(scattered, 16)
            pool.wait_ge(scattered, 16 * 2 * NTILE)

        @block.vector
        def _(dve):
            count = [0]

            def settle(ins):
                count[0] += 1
                ins.then_inc(step_done, 1)
                dve.wait_ge(step_done, count[0])

            def wide(a):
                return a.unsqueeze(2).to_broadcast(cube)

            settle(dve.memset(ones_cube[:, :], 1.0))
            dve.wait_ge(ids_ready, 1)
            settle(dve.tensor_copy(expert_ids[:, :, :].rearrange("p t e -> p (t e)"), ids_int[:, :]))
            settle(dve.tensor_reduce(one[:, :], logits[:, :, :], AX.X, ALU.max))
            dve.tensor_tensor(work[:, :, :], logits[:, :, :], wide(one[:, :]), ALU.subtract).then_inc(shifted, 1)
            dve.wait_ge(exped, 1)
            settle(dve.tensor_reduce(two[:, :], probs[:, :, :], AX.X, ALU.add))
            settle(dve.reciprocal(denom[:, :], two[:, :]))
            settle(dve.tensor_tensor(probs[:, :, :], probs[:, :, :], wide(denom[:, :]), ALU.mult))

            def choose(n):
                src = (probs, other)[n]
                for t in range(NTILE):
                    ins = dve.max(top8[:, t, :], src[:, t, :])
                settle(ins)
                for t in range(NTILE):
                    ins = dve.max_index(top8_id[:, t, :], top8[:, t, :], src[:, t, :])
                settle(ins)
                settle(dve.tensor_copy(expert[n][:, :], top8_id[:, :, 0]))
                ins = dve.tensor_tensor(mask[n][:, :, :], expert_ids[:, :, :], wide(expert[n][:, :]), ALU.is_equal)
                ins.then_inc(masks_ready, 1)
                dve.wait_ge(masks_ready, n + 1)
                if n == 0:
                    settle(dve.scalar_tensor_tensor(out=other[:, :, :].rearrange("p t e -> p (t e)"),
                                                    in0=mask[0][:, :, :].rearrange("p t e -> p (t e)"), scalar=NEG,
                                                    in1=logits[:, :, :].rearrange("p t e -> p (t e)"), op0=ALU.mult, op1=ALU.add))

            def find_rows(n):
                dve.wait_ge(counted, n + 1)
                by_tile = banks[:, 2 * n + 1, :].rearrange("p (t e) -> p t e", e=E)
                settle(dve.tensor_copy(total[n][:, :, :], by_tile))
                for e in range(E):
                    ins = dve.tensor_tensor_scan(upto[n][:, :, e], ones_cube[:, :], total[n][:, :, e], 0.0, ALU.mult, ALU.add)
                settle(ins)
                settle(dve.tensor_tensor(work[:, :, :], upto[n][:, :, :], total[n][:, :, :], ALU.subtract))
                settle(dve.tensor_tensor(place[n][:, :, :], banks[:, 2 * n, :].rearrange("p (t e) -> p t e", e=E),
                                         work[:, :, :], ALU.add))
                settle(dve.tensor_scalar(place[n][:, :, :], place[n][:, :, :], -1.0, None, ALU.add))
                if n == 1:
                    firsts = upto[0][:, NTILE - 1:NTILE, :].to_broadcast(cube)
                    settle(dve.tensor_tensor(place[1][:, :, :], place[1][:, :, :], firsts, ALU.add))
                settle(dve.tensor_scalar(work[:, :, :], place[n][:, :, :], float(CAP), None, ALU.is_lt))
                settle(dve.tensor_tensor(kept[n][:, :, :], work[:, :, :], mask[n][:, :, :], ALU.mult))
                settle(dve.tensor_reduce(any_kept[n][:, :], kept[n][:, :, :], AX.X, ALU.add))
                settle(dve.tensor_tensor(work[:, :, :], place[n][:, :, :], kept[n][:, :, :], ALU.mult))
                settle(dve.tensor_reduce(slot[n][:, :], work[:, :, :], AX.X, ALU.add))
                settle(dve.tensor_scalar(one[:, :], expert[n][:, :], float(CAP), None, ALU.mult))
                settle(dve.tensor_tensor(one[:, :], one[:, :], slot[n][:, :], ALU.add))
                settle(dve.tensor_scalar(two[:, :], any_kept[n][:, :], -float(E * CAP), float(E * CAP), ALU.mult, ALU.add))
                settle(dve.tensor_tensor(two[:, :], one[:, :], two[:, :], ALU.add))
                dve.tensor_copy(scatter_row[n][:, :], two[:, :]).then_inc(rows_ready, 1)
                dve.wait_ge(rows_ready, n + 1)
                settle(dve.tensor_tensor(two[:, :], one[:, :], any_kept[n][:, :], ALU.mult))
                settle(dve.tensor_copy(gather_row[:, n, :], two[:, :]))

            for n in range(2):
                choose(n)
                find_rows(n)
            for n in range(2):
                settle(dve.tensor_tensor(work[:, :, :], probs[:, :, :], kept[n][:, :, :], ALU.mult))
                settle(dve.tensor_reduce(gates[:, n, :], work[:, :, :], AX.X, ALU.add))
            settle(dve.tensor_tensor(denom[:, :], gates[:, 0, :], gates[:, 1, :], ALU.add))
            settle(dve.tensor_scalar(denom[:, :], denom[:, :], 2.0 ** -23, None, ALU.max))
            settle(dve.reciprocal(one[:, :], denom[:, :]))
            settle(dve.tensor_tensor(gates[:, :, :], gates[:, :, :], one[:, :].unsqueeze(1).to_broadcast([P, 2, NTILE]), ALU.mult))


def stage_e(nc, weights, scratch, const):
    fc1_w, fc2_w = weights
    xin_dram, eout_dram = scratch
    FB = F // P
    UNITS = KD + FB + 2
    TO_ACT, TO_DVE = KD + FB, 2
    LOADS = 16 * 3
    with ExitStack() as ctx:
        def sb(name, shape, dt=F32):
            return ctx.enter_context(nc.sbuf_tensor(name, shape, dt))

        def sem(name):
            return ctx.enter_context(nc.semaphore(name))

        w1 = sb("w1", [P, 2, KD, F])
        w2 = sb("w2", [P, 2, FB, D])
        xin = sb("xin", [P, 2, CAP // P, D])
        xinT = sb("xinT", [P, KD, CAP])
        hid = sb("e_hid", [P, FB, CAP])
        eout = sb("eout", [P, 2, CAP // P, D])
        none = sb("e_none", [P, 8])
        banks = ctx.enter_context(nc.psum_tensor("e_banks", [P, 8, CAP], F32))

        loaded = [sem(f"e_loaded{i}") for i in range(2)]
        unit_ready = sem("e_unit_ready")
        copied = sem("e_copied")
        added = sem("e_added")
        stored = [sem(f"e_stored{i}") for i in range(2)]

        block = ctx.enter_context(nc.Block())

        def emptied(eng, e, k):
            if k < TO_ACT:
                eng.wait_ge(copied, e * TO_ACT + (k + 1 + TO_ACT))
            else:
                eng.wait_ge(added, e * TO_DVE + (k - TO_ACT + 1 + TO_DVE))

        @block.sync
        def _(sp):
            def load(e, u):
                sp.dma_start(xin[:, u], xin_dram[bass.ds(e * CAP, CAP), :].rearrange("(j p) d -> p j d", p=P)).then_inc(loaded[u], 16)
                sp.dma_start(w1[:, u], fc1_w[e].rearrange("(h p) f -> p h f", p=P)).then_inc(loaded[u], 16)
                sp.dma_start(w2[:, u], fc2_w[e].rearrange("(f p) d -> p f d", p=P)).then_inc(loaded[u], 16)

            for u in range(2):
                load(u, u)
            with sp.Fori(0, E // 2 - 1) as i:
                for u in range(2):
                    sp.wait_ge(unit_ready, i * (2 * UNITS) + (u + 1) * UNITS)
                    load(i * 2 + (u + 2), u)

        @block.gpsimd
        def _(pool):
            with pool.Fori(0, E // 2) as i:
                for u in range(2):
                    e = i * 2 + u
                    pool.wait_ge(added, e * TO_DVE + 2 * TO_DVE)
                    dst = eout_dram[bass.ds(e * CAP, CAP), :].rearrange("(j p) d -> p j d", p=P)
                    pool.dma_start(dst, eout[:, u]).then_inc(stored[u], 16)
            for u in range(2):
                pool.wait_ge(stored[u], 16 * E // 2)

        @block.vector
        def _(dve):
            dve.memset(none[:, 0:1], 0.0).then_inc(copied, TO_ACT)
            dve.memset(none[:, 1:2], 0.0).then_inc(added, TO_DVE)
            with dve.Fori(0, E // 2) as i:
                for u in range(2):
                    e = i * 2 + u
                    dve.wait_ge(stored[u], i * 16)
                    for n in range(2):
                        k = TO_ACT + n
                        dve.wait_ge(unit_ready, e * UNITS + (k + 1))
                        src = banks[:, (UNITS * u + k) % 8, :].rearrange("p (j d) -> p j d", d=D)
                        bias = const["b2"][:, bass.ds(e, 1), :].to_broadcast([P, 2, D])
                        dve.scalar_tensor_tensor(out=eout[:, u, 2 * n:2 * n + 2, :], in0=src, scalar=KEEP, in1=bias,
                                                 op0=ALU.mult, op1=ALU.add).then_inc(added, 1)

        @block.scalar
        def _(act):
            with act.Fori(0, E // 2) as i:
                for u in range(2):
                    e = i * 2 + u
                    for k in range(TO_ACT):
                        src = banks[:, (UNITS * u + k) % 8, :]
                        act.wait_ge(unit_ready, e * UNITS + (k + 1))
                        if k < KD:
                            act.activation(xinT[:, k, :], src, ACT.Copy).then_inc(copied, 1)
                        else:
                            act.activation(hid[:, k - KD, :], src, ACT.Gelu,
                                           bias=const["b1T"][:, bass.ds(e * FB + (k - KD), 1)]).then_inc(copied, 1)

        @block.tensor
        def _(pe):
            with pe.Fori(0, E // 2) as i:
                for u in range(2):
                    e = i * 2 + u
                    pe.wait_ge(loaded[u], i * LOADS + LOADS)
                    for k in range(UNITS):
                        bank = banks[:, (UNITS * u + k) % 8, :]
                        emptied(pe, e if k >= 8 else e - 1, k - 8 if k >= 8 else k + UNITS - 8)
                        if k in (KD, TO_ACT):
                            emptied(pe, e, k - 1)
                        if k < KD:
                            for j in range(CAP // P):
                                last = pe.transpose(bank[:, j * P:(j + 1) * P], xin[:, u, j, k * P:(k + 1) * P],
                                                    const["ident"][:, :])
                        elif k < TO_ACT:
                            f = k - KD
                            for h in range(KD):
                                last = pe.matmul(bank, w1[:, u, h, f * P:(f + 1) * P], xinT[:, h, :],
                                                 start=h == 0, stop=h == KD - 1)
                        else:
                            for j in range(2):
                                tile = 2 * (k - TO_ACT) + j
                                for f in range(FB):
                                    last = pe.matmul(bank[:, j * D:(j + 1) * D], hid[:, f, tile * P:(tile + 1) * P],
                                                     w2[:, u, f, :], start=f == 0, stop=f == FB - 1)
                        last.then_inc(unit_ready, 1)


def stage_f(nc, out, eout_dram, keep):
    base, gates, gather_row = keep
    RING = 4
    with ExitStack() as ctx:
        def sb(name, shape, dt=F32):
            return ctx.enter_context(nc.sbuf_tensor(name, shape, dt))

        def sem(name):
            return ctx.enter_context(nc.semaphore(name))

        rows = sb("rows", [P, RING, 2, D])
        half = sb("half", [P, RING, D])
        total = sb("f_total", [P, RING, D])
        gathered = [sem(f"gathered{i}") for i in range(RING)]
        half_ready = sem("half_ready")
        total_ready = sem("total_ready")
        stored = [sem(f"f_stored{i}") for i in range(RING)]
        block = ctx.enter_context(nc.Block())
        out_tiles = out.rearrange("b (t p) d -> (b t) p d", p=P)

        @block.gpsimd
        def _(pool):
            for t in range(NTILE):
                if t >= RING:
                    pool.wait_ge(total_ready, t - RING + 1)
                for n in range(2):
                    pool.indirect_dma_start(out=rows[:, t % RING, n, :], out_offset=None, in_=eout_dram,
                                            in_offset=bass.IndirectOffsetOnAxis(ap=gather_row[:, n, t:t + 1], axis=0))\
                        .then_inc(gathered[t % RING], 16)

        @block.vector
        def _(dve):
            for t in range(NTILE):
                r = t % RING
                dve.wait_ge(gathered[r], 32 * (t // RING + 1))
                dve.scalar_tensor_tensor(out=half[:, r, :], in0=rows[:, r, 0, :], scalar=gates[:, 0, t:t + 1],
                                         in1=base[:, t, :], op0=ALU.mult, op1=ALU.add).then_inc(half_ready, 1)
                dve.wait_ge(half_ready, t + 1)
                if t >= RING:
                    dve.wait_ge(stored[r], 16 * (t // RING))
                dve.scalar_tensor_tensor(out=total[:, r, :], in0=rows[:, r, 1, :], scalar=gates[:, 1, t:t + 1],
                                         in1=half[:, r, :], op0=ALU.mult, op1=ALU.add).then_inc(total_ready, 1)

        @block.sync
        def _(sp):
            for t in range(NTILE):
                sp.wait_ge(total_ready, t + 1)
                sp.dma_start(out_tiles[t], total[:, t % RING, :]).then_inc(stored[t % RING], 16)
            for r in range(RING):
                sp.wait_ge(stored[r], 16 * (NTILE // RING))


def load_constants(nc, w, const, b1_rows):
    with ExitStack() as ctx:
        def sem(name):
            return ctx.enter_context(nc.semaphore(name))

        arrived, blank, made, turned, scaled = sem("w_arrived"), sem("w_blank"), sem("w_made"), sem("b1_turned"), sem("b2_scaled")
        bank = ctx.enter_context(nc.psum_tensor("w_bank", [P, P], F32))
        loads = []
        halves = "(h p) n -> p h n"
        loads.append((const["wd"][:, :, 0:DC], w["W_dq"].rearrange(halves, p=P)))
        loads.append((const["wd"][:, :, DC:2 * DC], w["W_dkv"].rearrange(halves, p=P)))
        loads.append((const["wu"][0:DC, 0, :], w["W_uq"]))
        loads.append((const["wu"][DC:2 * DC, 1, :], w["W_uk"]))
        loads.append((const["wu"][DC:2 * DC, 2, :], w["W_uv"]))
        for name, key in (("qw", "q_w"), ("kw", "k_w"), ("vw", "v_w"), ("ow", "o_w"), ("Wo", "W_o"), ("rw", "router_w")):
            loads.append((const[name][:, :, :], w[key].rearrange(halves, p=P)))
        for name, key in (("ln2w", "ln2_w"), ("ln2b", "ln2_b"), ("ob", "o_b")):
            loads.append((const[name][:, :], w[key].rearrange("(a d) -> a d", a=1).to_broadcast([P, D])))
        loads.append((const["b2"][:, :, :], w["fc2_b"].rearrange("(a e) d -> a e d", a=1).to_broadcast([P, E, D])))
        loads.append((b1_rows[:, :], w["fc1_b"].rearrange("e (f p) -> (e f) p", p=P)))
        columns = [(const[name][:, :], w[key].rearrange("(h p) -> p h", p=P))
                   for name, key in (("ln1w", "ln1_w"), ("ln1b", "ln1_b"), ("qb", "q_b"), ("kb", "k_b"), ("vb", "v_b"))]
        ALL = 16 * (len(loads) + len(columns))
        block = ctx.enter_context(nc.Block())

        @block.sync
        def _(sp):
            sp.wait_ge(blank, 1)
            for dst, src in loads:
                sp.dma_start(dst, src).then_inc(arrived, 16)
            with nc.allow_non_contiguous_dma(reason="short vectors, one value per partition"):
                for dst, src in columns:
                    sp.dma_start(dst, src).then_inc(arrived, 16)
            sp.wait_ge(arrived, ALL)

        @block.gpsimd
        def _(pool):
            pool.memset(const["ident"][:, :], 0.0)
            pool.memset(const["maskq"][:, :], 0.0)
            pool.memset(const["maskk"][:, :], 0.0)
            pool.memset(const["identb"][:, :], 0.0)
            pool.memset(const["wu"][:, :, :], 0.0)
            pool.memset(const["upper"][:, :], 1.0)
            pool.memset(const["eps"][:, :], EPS)
            pool.memset(const["ones"][:, :], 1.0).then_inc(blank, 1)
            pool.wait_ge(blank, 1)
            for m in ("ident", "identb"):
                pool.affine_select(out=const[m][:, :], in_=const[m][:, :], compare_op=ALU.not_equal, fill=1.0, base=0,
                                   pattern=[[-1, P]], channel_multiplier=1).then_inc(made, 1)
            diagonal = const["maskq"][:, CH - P:CH]
            pool.affine_select(out=diagonal, in_=diagonal, compare_op=ALU.is_ge, fill=NEG, base=0,
                               pattern=[[-1, P]], channel_multiplier=1).then_inc(made, 1)
            pool.affine_select(out=const["maskk"][:, :], in_=const["maskk"][:, :], compare_op=ALU.is_ge, fill=NEG, base=0,
                               pattern=[[1, P]], channel_multiplier=-1).then_inc(made, 1)
            pool.affine_select(out=const["upper"][:, :], in_=const["upper"][:, :], compare_op=ALU.is_ge, fill=0.0, base=0,
                               pattern=[[1, P]], channel_multiplier=-1).then_inc(made, 1)

        @block.tensor
        def _(pe):
            pe.wait_ge(arrived, ALL)
            pe.wait_ge(made, 5)
            pe.transpose(bank[:, :], b1_rows[:, :], const["ident"][:, :]).then_inc(turned, 1)

        @block.vector
        def _(dve):
            dve.wait_ge(turned, 1)
            dve.tensor_copy(const["b1T"][:, :], bank[:, :])
            dve.tensor_scalar(const["b2"][:, :, :], const["b2"][:, :, :], KEEP, None, ALU.mult).then_inc(scaled, 1)


def layer(nc, x, w, out):
    xn_dram = nc.dram_tensor("xn_scratch", [T, D], F32).ap()
    q_dram = nc.dram_tensor("q_scratch", [G, GH, SPLIT * HD, S], BF16).ap()
    k_dram = nc.dram_tensor("k_scratch", [G, GH, SPLIT * HD, S], BF16).ap()
    v_dram = nc.dram_tensor("v_scratch", [G, S, GH * VW], F32).ap()
    ctx_dram = nc.dram_tensor("ctx_scratch", [G, S, GH * HD], F32).ap()
    xin_dram = nc.dram_tensor("xin_scratch", [E * CAP, D], F32).ap()
    eout_dram = nc.dram_tensor("eout_scratch", [E * CAP, D], F32).ap()
    with ExitStack() as ctx:
        shapes = {"wd": [P, KD, 2 * DC], "wu": [P, 3, D], "qw": [P, KD, D], "kw": [P, KD, D], "vw": [P, KD, D],
                  "ow": [P, KD, D], "Wo": [P, KD, D], "rw": [P, KD, E], "vb": [P, KD], "ob": [P, D],
                  "ln1w": [P, KD], "ln1b": [P, KD], "qb": [P, KD], "kb": [P, KD], "ln2w": [P, D], "ln2b": [P, D],
                  "b2": [P, E, D], "b1T": [P, E * F // P], "ident": [P, P], "upper": [P, P], "ones": [P, P], "eps": [P, 1],
                  "maskq": [P, CH]}
        const = {n: ctx.enter_context(nc.sbuf_tensor(f"c_{n}", s, F32)) for n, s in shapes.items()}
        for n in ("identb", "maskk"):
            const[n] = ctx.enter_context(nc.sbuf_tensor(f"c_{n}", [P, P], BF16))
        with nc.sbuf_tensor("b1_rows", [E * F // P, P], F32) as b1_rows:
            load_constants(nc, w, const, b1_rows)
        stage_a(nc, x, (xn_dram, q_dram, k_dram, v_dram), const)
        stage_b(nc, (xin_dram, q_dram, k_dram, v_dram, ctx_dram), const)
        with ExitStack() as late:
            def sb(name, shape, dt=F32):
                return late.enter_context(nc.sbuf_tensor(name, shape, dt))

            base = sb("base", [P, NTILE, D])
            gates = sb("gates", [P, 2, NTILE])
            gather_row = sb("gather_row", [P, 2, NTILE], U32)
            with nc.sbuf_tensor("xt", [P, NTILE, D], F32) as xt, nc.sbuf_tensor("logits", [P, NTILE, E], F32) as logits:
                stage_c(nc, x, (xn_dram, ctx_dram), const, (xt, base, logits))
                stage_d(nc, (xin_dram,), const, (xt, logits, gates, gather_row))
            stage_e(nc, (w["fc1_w"], w["fc2_w"]), (xin_dram, eout_dram), const)
            stage_f(nc, out, eout_dram, (base, gates, gather_row))


_ATTN = ["W_dq", "W_uq", "W_dkv", "W_uk", "W_uv", "W_o"]
_FFN = ["ln1_w", "ln1_b", "q_w", "q_b", "k_w", "k_b", "v_w", "v_b", "o_w", "o_b", "ln2_w", "ln2_b", "router_w",
        "fc1_w", "fc1_b", "fc2_w", "fc2_b"]
_INS = {"x": "L0_attn_x", **{n: f"L0_attn_{n}" for n in _ATTN}, **{n: f"L0_ffn_{n}" for n in _FFN}}


def kernel(**inputs):
    import numpy as _np
    import concourse.bacc as _bacc
    from concourse import mybir as _mybir
    from concourse.bass_utils import run_bass_kernel_spmd as _run

    nc = _bacc.Bacc("TRN2", target_bir_lowering=False, num_devices=1)
    arrays, args = {}, {}
    for short, name in _INS.items():
        a = _np.ascontiguousarray(inputs[name])
        arrays[f"in_{name}"] = a
        args[short] = nc.dram_tensor(f"in_{name}", a.shape, _mybir.dt.from_np(a.dtype), kind="ExternalInput").ap()
    out = nc.dram_tensor("out_0", (B, S, D), F32, kind="ExternalOutput").ap()
    layer(nc, args.pop("x"), args, out)
    r = _run(nc, [arrays], core_ids=[0])
    return r.results[0]["out_0"]
```

```python
from contextlib import ExitStack

import concourse.bass as bass
from concourse import mybir

ALU = mybir.AluOpType
ACT = mybir.ActivationFunctionType
AX = mybir.AxisListType
F32 = mybir.dt.float32
BF16 = mybir.dt.bfloat16
F32R = mybir.dt.float32r
U32 = mybir.dt.uint32

P = 128
B, S, D = 2, 2048, 256
T = B * S
H, HD = 16, 16
DC = 64
E, F = 16, 1024
CAP = 2 * (T // E)
EPS = 1e-5
KD = D // P
CH = 512
TPC = CH // P
NCH = T // CH
NTILE = T // P
SPLIT = 3
NEG = -3.0e38
GH = 4
HG = H // GH
G = 2 * B * HG
VW = 32
PAIR_ROWS = 6 * HD
STACK = PAIR_ROWS + SPLIT
SCALE = HD ** -0.5
KEEP = 1.0 - 0.2



def stage_a(nc, x, scratch, const):
    xn_dram, q_dram, k_dram, v_dram = scratch
    UNITS = 17
    CREDIT = UNITS
    C_UNIT, V_LOW, V_FFN = 4, 13, 15
    QK = list(range(5, 13))
    NQK = len(QK)
    FIRST_NORM, SECOND_NORM = 0, 2
    RING = 8
    with ExitStack() as ctx:
        def sb(name, shape, dt=F32):
            return ctx.enter_context(nc.sbuf_tensor(name, shape, dt))

        def sem(name):
            return ctx.enter_context(nc.semaphore(name))

        xs = sb("xs", [P, 2, TPC, D])
        xn = sb("xn", [P, 2, TPC, D])
        hn = sb("hn", [P, 2, TPC, D])
        stats = sb("a_stats", [P, TPC, 6])
        meanvar = sb("a_meanvar", [P, TPC, 2])
        std = sb("a_std", [P, TPC])
        rstd = sb("a_rstd", [P, TPC])
        none = sb("a_none", [P, 8])
        xnT = sb("xnT", [P, KD, CH])
        hT = sb("hT", [P, KD, CH])
        cT = sb("cT", [P, CH])
        qf = sb("qf", [P, RING, CH])
        rest = sb("rest", [P, RING, CH])
        parts = sb("parts", [P, RING, SPLIT, CH], BF16)
        vt = sb("vt", [P, 2, TPC, H * VW])
        banks = ctx.enter_context(nc.psum_tensor("a_banks", [P, 8, CH], F32))

        x_in = [sem(f"x_in{i}") for i in range(2)]
        norm_step = sem("norm_step")
        var_ready = sem("var_ready")
        std_ready = sem("std_ready")
        xn_ready = sem("xn_ready")
        hn_ready = sem("hn_ready")
        unit_ready = sem("unit_ready")
        copied = sem("copied")
        vt_set = sem("vt_set")
        rest_ready = sem("rest_ready")
        mid_ready = sem("mid_ready")
        lo_ready = sem("lo_ready")
        xn_stored = [sem(f"xn_stored{i}") for i in range(2)]
        parts_stored = [sem(f"parts_stored{i}") for i in range(RING)]
        v_stored = [sem(f"v_stored{i}") for i in range(2)]

        block = ctx.enter_context(nc.Block())
        x_chunks = x.rearrange("b (c j p) d -> (b c) p j d", j=TPC, p=P)
        xn_chunks = xn_dram.rearrange("(c j p) d -> c p j d", j=TPC, p=P)

        def unit(c, k):
            return c * UNITS + (k + 1 + CREDIT)

        @block.sync
        def _(sp):
            for n in range(2):
                sp.dma_start(xs[:, n], x_chunks[n]).then_inc(x_in[n], 16)
            for c in range(NCH):
                u, b, cc = c % 2, c // (NCH // B), c % (NCH // B)
                sp.wait_ge(xn_ready, c + 1)
                sp.dma_start(xn_chunks[c], xn[:, u]).then_inc(xn_stored[u], 16)
                if c + 2 < NCH:
                    sp.dma_start(xs[:, u], x_chunks[c + 2]).then_inc(x_in[u], 16)
                for a in range(2):
                    group = a * B * HG + b * HG
                    for r in range(NQK // 2 * a, NQK // 2 * (a + 1)):
                        dst, half = (q_dram, k_dram)[r // 2 % 2], r % 2
                        heads = dst.rearrange("g h r t -> (g h) r t")
                        g0 = group * GH + half * (P // HD)
                        sp.wait_ge(lo_ready, NQK * c + r + 1 + RING)
                        for part in range(SPLIT):
                            sp.dma_start(heads[g0:g0 + P // HD, part * HD:(part + 1) * HD, cc * CH:(cc + 1) * CH],
                                         parts[:, r % RING, part, :]).then_inc(parts_stored[r % RING], 16)
                for a in (1, 0):
                    group = a * B * HG + b * HG
                    sp.wait_ge(copied, unit(c, (V_FFN, V_LOW)[a] + 1))
                    for hg in range(HG):
                        dst = v_dram[group + hg, cc * CH:(cc + 1) * CH, :].rearrange("(j p) n -> p j n", p=P)
                        sp.dma_start(dst, vt[:, a, :, hg * P:(hg + 1) * P]).then_inc(v_stored[a], 16)
            for n in range(2):
                sp.wait_ge(xn_stored[n], 16 * (NCH // 2))
                sp.wait_ge(v_stored[n], 16 * HG * NCH)
            for n in range(RING):
                sp.wait_ge(parts_stored[n], 16 * SPLIT * (NQK // RING) * NCH)

        @block.vector
        def _(dve):
            dve.memset(none[:, 0:1], 0.0).then_inc(copied, CREDIT)
            dve.memset(none[:, 1:2], 0.0).then_inc(lo_ready, RING)
            dve.memset(none[:, 2:3], 0.0).then_inc(rest_ready, RING)
            dve.memset(none[:, 3:4], 0.0).then_inc(unit_ready, 2 * UNITS)
            dve.memset(vt[:, :, :, :], 0.0).then_inc(vt_set, 1)
            dve.wait_ge(vt_set, 1)
            v_ones = vt[:, :, :, :].rearrange("p a j (h w) -> p (a j h) w", w=VW)[:, :, HD:HD + 1]
            dve.memset(v_ones, 1.0).then_inc(vt_set, 1)

            def norm(c, n, src, dst):
                done = c * 4 + 2 * n
                for j in range(TPC):
                    last = dve.bn_stats(stats[:, j, :], src[:, j, :])
                last.then_inc(norm_step, 1)
                dve.wait_ge(norm_step, done + 1)
                dve.memset(none[:, 4:5], 0.0)
                for j in range(TPC):
                    last = dve.bn_aggr(meanvar[:, j, :], stats[:, j, :])
                last.then_inc(var_ready, 1)
                dve.wait_ge(std_ready, c * 2 + (n + 1))
                dve.reciprocal(rstd[:, :], std[:, :]).then_inc(norm_step, 1)
                dve.wait_ge(norm_step, done + 2)
                for j in range(TPC):
                    last = dve.tensor_scalar(dst[:, j, :], src[:, j, :], meanvar[:, j, 0:1], rstd[:, j:j + 1],
                                             ALU.subtract, ALU.mult)
                return last

            def first_norm(i, u):
                c, par = i * 2 + u, u % 2
                dve.wait_ge(x_in[par], i * 16 + 16 * (u // 2 + 1))
                dve.wait_ge(unit_ready, c * UNITS + C_UNIT)
                dve.wait_ge(xn_stored[par], i * 16 + 16 * (u // 2))
                norm(c, 0, xs[:, par], xn[:, par]).then_inc(xn_ready, 1)

            def second_norm(i, u):
                c, par = i * 2 + u, u % 2
                dve.wait_ge(xn_ready, c + 1)
                norm(c, 1, xn[:, par], hn[:, par]).then_inc(hn_ready, 1)

            def split(i, u, r):
                c, slot = i * 2 + u, r % RING
                n = c * NQK + r
                dve.wait_ge(copied, unit(c, QK[r]))
                dve.wait_ge(lo_ready, n + 1)
                dve.tensor_tensor(rest[:, slot, :], qf[:, slot, :], parts[:, slot, 0, :],
                                  ALU.subtract).then_inc(rest_ready, 1)
                dve.wait_ge(rest_ready, n + (1 + RING))
                dve.tensor_copy(parts[:, slot, 1, :], rest[:, slot, :]).then_inc(mid_ready, 1)

            def chunk(i, u, more):
                for r in range(NQK):
                    if more and r == FIRST_NORM:
                        first_norm(i, u + 1)
                    if more and r == SECOND_NORM:
                        second_norm(i, u + 1)
                    split(i, u, r)

            first_norm(0, 0)
            second_norm(0, 0)
            with dve.Fori(0, NCH // 2 - 1) as i:
                for u in range(2):
                    chunk(i, u, True)
            chunk(NCH // 2 - 1, 0, True)
            chunk(NCH // 2 - 1, 1, False)

        @block.gpsimd
        def _(pool):
            with pool.Fori(0, NCH // 2) as i:
                for k in range(2 * NQK):
                    slot = k % RING
                    pool.wait_ge(mid_ready, i * (2 * NQK) + (k + 1))
                    pool.tensor_tensor(parts[:, slot, 2, :], rest[:, slot, :], parts[:, slot, 1, :],
                                       ALU.subtract).then_inc(lo_ready, 1)

        @block.scalar
        def _(act):
            act.wait_ge(vt_set, 2)

            def root(i, u, n):
                c = i * 2 + u
                act.wait_ge(var_ready, c * 2 + (n + 1))
                act.activation(std[:, :], meanvar[:, :, 1], ACT.Sqrt, bias=const["eps"][:, 0:1]).then_inc(std_ready, 1)

            def chunk(i, u, more):
                c = i * 2 + u
                for k in range(UNITS):
                    src, how = banks[:, k % 8, :], {}
                    if more and k == QK[FIRST_NORM + 1]:
                        root(i, u + 1, 0)
                    if more and k == QK[SECOND_NORM + 1]:
                        root(i, u + 1, 1)
                    if k < 2:
                        out = xnT[:, k, :]
                    elif k < 4:
                        out = hT[:, k - 2, :]
                        how = {"scale": const["ln1w"][:, k - 2:k - 1], "bias": const["ln1b"][:, k - 2:k - 1]}
                    elif k == C_UNIT:
                        out = cT[:, :]
                    elif k in QK:
                        r = QK.index(k)
                        out = qf[:, r % RING, :]
                        if r < NQK // 2:
                            how = {"bias": const[("qb", "kb")[r // 2]][:, r % 2:r % 2 + 1]}
                    else:
                        a = int(k >= V_FFN)
                        half = k - (V_LOW, V_FFN)[a]
                        if half == 0:
                            act.wait_ge(v_stored[1 - a], c * (16 * HG))
                        out = vt[:, 1 - a, 2 * half:2 * half + 2, :].rearrange("p j (h w) -> p (j h) w", w=VW)[:, :, 0:HD]
                        src = src.rearrange("p (n w) -> p n w", w=HD)
                    if k in QK:
                        act.wait_ge(rest_ready, c * NQK + (r + 1))
                        act.wait_ge(unit_ready, c * UNITS + (k + 1 + 2 * UNITS))
                        act.activation(out, src, ACT.Identity, **how)
                        act.wait_ge(parts_stored[r % RING], c * (16 * SPLIT * NQK // RING) + 16 * SPLIT * (r // RING))
                        out = parts[:, r % RING, 0, :]
                    else:
                        act.wait_ge(unit_ready, c * UNITS + (k + 1 + 2 * UNITS))
                    act.activation(out, src, ACT.Identity, **how).then_inc(copied, 1)

            root(0, 0, 0)
            root(0, 0, 1)
            with act.Fori(0, NCH // 2 - 1) as i:
                for u in range(2):
                    chunk(i, u, True)
            chunk(NCH // 2 - 1, 0, True)
            chunk(NCH // 2 - 1, 1, False)

        @block.tensor
        def _(pe):
            with pe.Fori(0, NCH // 2) as i:
                for u in range(2):
                    c = i * 2 + u
                    for k in range(UNITS):
                        bank = banks[:, k % 8, :]
                        pe.wait_ge(copied, unit(c, k - 8) if k >= 8 else unit(c, (16 if k == 0 else k + 8) - UNITS))
                        if k in (0, 2):
                            pe.wait_ge((xn_ready, hn_ready)[k // 2], c + 1)
                        if k == C_UNIT:
                            pe.wait_ge(copied, unit(c, 3))
                        if k == QK[NQK // 2]:
                            pe.wait_ge(copied, unit(c, C_UNIT))
                        if k < C_UNIT:
                            src = (xn, hn)[k // 2]
                            for j in range(TPC):
                                last = pe.transpose(bank[:, j * P:(j + 1) * P], src[:, u, j, (k % 2) * P:(k % 2 + 1) * P],
                                                    const["ident"][:, :])
                        elif k == C_UNIT:
                            for h in range(KD):
                                last = pe.matmul(bank, const["wd"][:, h, :], xnT[:, h, :], start=h == 0, stop=h == KD - 1)
                        elif k in QK[:4]:
                            r = QK.index(k)
                            w = const[("qw", "kw")[r // 2]]
                            for h in range(KD):
                                last = pe.matmul(bank, w[:, h, (r % 2) * P:(r % 2 + 1) * P], hT[:, h, :],
                                                 start=h == 0, stop=h == KD - 1)
                        elif k in QK:
                            r = QK.index(k) - 4
                            last = pe.matmul(bank, const["wu"][:, r // 2, (r % 2) * P:(r % 2 + 1) * P], cT[:, :],
                                             start=True, stop=True)
                        else:
                            a = int(k >= V_FFN)
                            half = k - (V_LOW, V_FFN)[a]
                            for j in range(2):
                                out = bank[:, j * D:(j + 1) * D]
                                tokens = slice((2 * half + j) * P, (2 * half + j + 1) * P)
                                if a == 0:
                                    last = pe.matmul(out, cT[:, tokens], const["wu"][:, 2, :], start=True, stop=True)
                                else:
                                    for h in range(KD):
                                        last = pe.matmul(out, hT[:, h, tokens], const["vw"][:, h, :],
                                                         start=h == 0, stop=h == KD - 1)
                        last.then_inc(unit_ready, 1)


EARLY = 16


def group_order(exps, maxima, carried, early):
    n_m, n_s = len(ROW_BLOCKS), len(SCORE_BLOCKS)
    if not exps and not maxima:
        return [("PV", -1), ("T", -1)]
    if not exps:
        return [("M", m) for m in range(n_m)] + [("N", 0)] + [("E", m) for m in range(EARLY)]
    turn_at = n_s - EARLY - 1
    last = turn_at - 3
    order, m, e, turn = [], EARLY, 0, None
    for n in range(n_s):
        while maxima and m < n_m and (m - EARLY) * last <= n * (n_m - EARLY):
            order.append(("M", m))
            m += 1
        if maxima and n == turn_at:
            order.append(("N", 0))
        if early and n > turn_at:
            order.append(("E", e))
            e += 1
        if carried and n in (2, 6):
            order.append(("PV", -1) if n == 2 else ("T", -1))
        order.append(("S", n))
        if n % GH == GH - 1 and n >= GH:
            batch = n // GH - 1
            order.append(("PV", batch))
            if turn is not None:
                order.append(("T", turn))
                turn = None
            if batch in CHUNK_ENDS:
                turn = CHUNK_ENDS.index(batch)
    return order


ROW_BLOCKS = [(h, t, c) for t in reversed(range(S // P)) for h in range(GH) for c in range(t // TPC + 1)]
SCORE_BLOCKS = [(q, k, h) for q in range(S // CH) for k in range(TPC * (q + 1)) for h in range(GH)]
CHUNK_ENDS = [TPC * (q + 1) * (q + 2) // 2 - 1 for q in range(S // CH)]


def stage_b(nc, scratch, const):
    xin_dram, q_dram, k_dram, v_dram, ctx_dram = scratch
    SLOTS = 3
    NM, NS = len(ROW_BLOCKS) + 1, len(SCORE_BLOCKS)
    NB, NQ = NS // GH, S // CH
    PR = 8
    LOADS = 16 * 11
    MROWS = 16 * SPLIT * GH
    FILLS = 16
    LOOPED = 12
    with ExitStack() as ctx:
        def sb(name, shape, dt=F32):
            return ctx.enter_context(nc.sbuf_tensor(name, shape, dt))

        def sem(name):
            return ctx.enter_context(nc.semaphore(name))

        qs = sb("qs", [STACK, SLOTS, GH, S], BF16)
        ks = sb("ks", [STACK, SLOTS, GH, S], BF16)
        vs = sb("vs", [P, SLOTS, S // P, GH * VW])
        probs = sb("probs", [P, PR, CH])
        pv_sb = sb("pv_sb", [P, 2, CH])
        inv = sb("inv", [P, 2, TPC, GH])
        ctx_sb = sb("ctx_sb", [P, 2, TPC, GH, HD])
        rowmax = sb("rowmax", [P, GH, S // P, NQ])
        unused = sb("unused", [P, GH, CH], BF16)
        negmax = sb("negmax", [P, P])
        mrest = sb("mrest", [GH * S // P, P])
        mrows = sb("mrows", [GH * S // P, SPLIT, P], BF16)
        none = sb("b_none", [P, 8])
        dve_pause = sb("dve_pause", [P, GH])
        zeros = sb("zeros", [P, E * CAP * D // P // FILLS])
        m_banks = ctx.enter_context(nc.psum_tensor("m_banks", [P, SLOTS, CH], F32))
        s_banks = ctx.enter_context(nc.psum_tensor("s_banks", [P, SLOTS, CH], F32))
        v_banks = ctx.enter_context(nc.psum_tensor("v_banks", [P, 2, CH], F32))

        loaded = [sem(f"loaded{i}") for i in range(SLOTS)]
        m_ready = sem("m_ready")
        m_used = sem("m_used")
        cleared = sem("cleared")
        negmax_ready = sem("negmax_ready")
        m_step = sem("m_step")
        mrows_ready = sem("mrows_ready")
        mrows_in = sem("mrows_in")
        s_ready = sem("s_ready")
        p_ready = sem("p_ready")
        p_used = sem("p_used")
        pv_copied = sem("pv_copied")
        turned = sem("turned")
        inv_ready = sem("inv_ready")
        ctx_ready = sem("ctx_ready")
        ctx_stored = [sem(f"ctx_stored{i}") for i in range(2)]
        ones_set = sem("ones_set")
        zeros_set = sem("zeros_set")
        filled = sem("filled")

        block = ctx.enter_context(nc.Block())

        def at(i, u, per, off):
            return i * (SLOTS * per) + (u * per + off)

        @block.sync
        def _(sp):
            def load(i, u, g):
                slot = (u + 2) % SLOTS
                rows = k_dram[g].rearrange("h r t -> r h t")
                for at_row, n in ((0, 3), (3, 2), (5, 1)):
                    sp.dma_start(ks[at_row * HD:(at_row + n) * HD, slot], rows[0:n * HD]).then_inc(loaded[slot], 16)
                rows = q_dram[g].rearrange("h r t -> r h t")
                for n, part in enumerate((0, 0, 0, 1, 1, 2)):
                    sp.dma_start(qs[n * HD:(n + 1) * HD, slot], rows[part * HD:(part + 1) * HD]).then_inc(loaded[slot], 16)
                tiles = v_dram[g].rearrange("(k p) n -> p k n", p=P)
                for n in range(0, S // P, S // P // 2):
                    sp.dma_start(vs[:, slot, n:n + S // P // 2], tiles[:, n:n + S // P // 2]).then_inc(loaded[slot], 16)

            def maxima(i, u):
                slot = (u + 1) % SLOTS
                sp.wait_ge(mrows_ready, at(i, u, 1, 2))
                for h in range(GH):
                    for part in range(SPLIT):
                        row = PAIR_ROWS + part
                        sp.dma_start(qs[row:row + 1, slot, h, :], mrows[h * (S // P):(h + 1) * (S // P), part, :])\
                            .then_inc(mrows_in, 16)

            load(-1, 1, 0)
            load(-1, 2, 1)
            maxima(-1, 2)

            def store(i, u, q):
                sp.wait_ge(ctx_ready, at(i, u, NQ, q + 1 + 2))
                dst = ctx_dram[i * SLOTS + u, q * CH:(q + 1) * CH, :].rearrange("(j p) n -> p j n", p=P)
                sp.dma_start(dst, ctx_sb[:, q % 2].rearrange("p j h w -> p j (h w)")).then_inc(ctx_stored[q % 2], 16)

            def step(i, u, g, more):
                if more:
                    sp.wait_ge(p_used, at(i, u, NB, PR // GH))
                    load(i, u, g)
                for q in range(NQ - 1):
                    store(i, u, q)
                maxima(i, u)
                store(i, u, NQ - 1)

            with sp.Fori(0, 4) as i:
                for u in range(SLOTS):
                    step(i, u, i * SLOTS + (u + 2), True)
            for s in range(12, G - 1):
                step(s // SLOTS, s % SLOTS, s + 2, s + 2 < G)
            for q in range(NQ):
                store(G // SLOTS, 0, q)
            for n in range(2):
                sp.wait_ge(ctx_stored[n], 16 * G * NQ // 2)
            sp.wait_ge(filled, 16 * FILLS)

        @block.gpsimd
        def _(pool):
            pool.memset(zeros[:, :], 0.0).then_inc(zeros_set, 1)
            pool.wait_ge(zeros_set, 1)
            pool.memset(ks[PAIR_ROWS:STACK, :, :, :], 1.0).then_inc(ones_set, 1)
            fill = xin_dram.rearrange("(f p r) d -> f p (r d)", f=FILLS, p=P)
            for n in range(FILLS):
                pool.dma_start(fill[n], zeros[:, :]).then_inc(filled, 16)

        @block.tensor
        def _(pe):
            def step(i, u, exps, maxima, carried, early):
                now = u % SLOTS
                for what, n in group_order(exps, maxima, carried, early):
                    if what == "S":
                        q, k, h = SCORE_BLOCKS[n]
                        first = max(k - TPC * q, 0) * P
                        bank = s_banks[:, (u * NS + n) % SLOTS, 0:CH - first]
                        if n == 0:
                            pe.wait_ge(mrows_in, at(i, u, MROWS, MROWS))
                        pe.wait_ge(p_ready, at(i, u, NS, n + 1))
                        diagonal = k >= TPC * q
                        ins = pe.matmul(bank, ks[:, now, h, k * P:(k + 1) * P],
                                        qs[:, now, h, q * CH + first:(q + 1) * CH], start=True, stop=not diagonal)
                        if diagonal:
                            ins = pe.matmul(bank[:, 0:P], const["identb"][:, :], const["maskk"][:, :], start=False, stop=True)
                        ins.then_inc(s_ready, 1)
                    elif what in ("M", "E"):
                        v = u + (1 if what == "M" else 2)
                        nxt = v % SLOTS
                        h, t, c = ROW_BLOCKS[n]
                        width = min(CH, (t + 1) * P - c * CH)
                        bank = m_banks[:, (v * NM + n) % SLOTS, 0:width]
                        if n == 0:
                            pe.wait_ge(loaded[nxt], (i + v // SLOTS) * LOADS + LOADS)
                        pe.wait_ge(m_used, at(i, v, NM, n + 1))
                        ins = pe.matmul(bank, qs[0:PAIR_ROWS, nxt, h, t * P:(t + 1) * P],
                                        ks[0:PAIR_ROWS, nxt, h, c * CH:c * CH + width], start=True, stop=True)
                        ins.then_inc(m_ready, 1)
                    elif what == "N":
                        bank = m_banks[:, ((u + 1) * NM + NM - 1) % SLOTS, 0:P]
                        pe.wait_ge(m_used, at(i, u, NM, NM + NM))
                        pe.wait_ge(negmax_ready, at(i, u, 1, 2))
                        pe.transpose(bank, negmax[:, :], const["ident"][:, :]).then_inc(m_ready, 1)
                    elif what == "PV":
                        n, v = (n, u) if n >= 0 else (NB - 1, u - 1)
                        q, k, _ = SCORE_BLOCKS[n * GH]
                        first = max(k - TPC * q, 0) * P
                        if k == 0:
                            pe.wait_ge(ctx_ready, at(i, v, NQ, q + 1))
                        pe.wait_ge(p_ready, at(i, v, NS, GH * (n + 1) + SLOTS))
                        for h in range(GH):
                            rows = slice(h * VW, (h + 1) * VW)
                            ins = pe.matmul(v_banks[rows, q % 2, first:CH], vs[:, v % SLOTS, k, rows],
                                            probs[:, (n * GH + h) % PR, 0:CH - first],
                                            start=k == 0, stop=k == TPC * (q + 1) - 1, tile_position=(0, h * VW))
                        ins.then_inc(p_used, 1)
                    elif what == "T":
                        n, v = (n, u) if n >= 0 else (NQ - 1, u - 1)
                        pe.wait_ge(pv_copied, at(i, v, NQ, n + 1))
                        for t in range(TPC):
                            ins = pe.transpose(v_banks[:, n % 2, t * P:(t + 1) * P], pv_sb[:, n % 2, t * P:(t + 1) * P],
                                               const["ident"][:, :])
                        ins.then_inc(turned, 1)

            step(-1, 2, False, True, False, True)
            pe.wait_ge(ones_set, 1)
            step(0, 0, True, True, False, True)
            with pe.Fori(0, LOOPED // SLOTS) as i:
                for u in range(SLOTS):
                    step(i, u + 1, True, True, True, True)
            for s in range(1 + LOOPED, G):
                step(s // SLOTS, s % SLOTS, True, s + 1 < G, True, s + 2 < G)
            step(G // SLOTS, G % SLOTS, False, False, True, False)

        @block.scalar
        def _(act):
            def step(i, u, exps, maxima, carried, early):
                for what, n in group_order(exps, maxima, carried, early):
                    if what == "S":
                        q, k, h = SCORE_BLOCKS[n]
                        width = CH - max(k - TPC * q, 0) * P
                        if h == 0:
                            act.wait_ge(p_used, at(i, u, NB, n // GH + 1))
                        act.wait_ge(s_ready, at(i, u, NS, n + 1))
                        act.activation(probs[:, n % PR, 0:width], s_banks[:, (u * NS + n) % SLOTS, 0:width],
                                       ACT.Exp, scale=SCALE).then_inc(p_ready, 1)
                    elif what == "PV" and (n < 0 or n in CHUNK_ENDS):
                        n, v = (n, u) if n >= 0 else (NB - 1, u - 1)
                        q = CHUNK_ENDS.index(n)
                        act.wait_ge(turned, at(i, v, NQ, q + 1))
                        act.wait_ge(p_used, at(i, v, NB, n + 1 + PR // GH))
                        act.activation(pv_sb[:, q % 2, :], v_banks[:, q % 2, :], ACT.Copy).then_inc(pv_copied, 1)

            step(0, 0, True, True, False, True)
            with act.Fori(0, LOOPED // SLOTS) as i:
                for u in range(SLOTS):
                    step(i, u + 1, True, True, True, True)
            for s in range(1 + LOOPED, G):
                step(s // SLOTS, s % SLOTS, True, s + 1 < G, True, s + 2 < G)
            step(G // SLOTS, G % SLOTS, False, False, True, False)

        @block.vector
        def _(dve):
            dve.memset(none[:, 0:1], 0.0).then_inc(m_used, SLOTS)
            dve.memset(none[:, 1:2], 0.0).then_inc(p_ready, SLOTS)
            dve.memset(none[:, 2:3], 0.0).then_inc(p_used, PR // GH)
            dve.memset(none[:, 3:4], 0.0).then_inc(ctx_ready, 2)
            dve.memset(none[:, 4:5], 0.0).then_inc(turned, 2)
            dve.memset(rowmax[:, :, :, :], NEG)
            dve.memset(negmax[:, :], 0.0).then_inc(cleared, 1)
            dve.wait_ge(cleared, 1)

            def step(i, u, exps, maxima, carried, early):
                for what, n in group_order(exps, maxima, carried, early):
                    if what in ("M", "E"):
                        v = u + (1 if what == "M" else 2)
                        h, t, c = ROW_BLOCKS[n]
                        width = min(CH, (t + 1) * P - c * CH)
                        dve.wait_ge(m_ready, at(i, v, NM, n + 1))
                        scores = m_banks[:, (v * NM + n) % SLOTS, 0:width]
                        if c == t // TPC:
                            dve.memset(dve_pause[:, n % GH:n % GH + 1], 0.0)
                            dve.tensor_tensor_reduce(unused[:, n % GH, 0:width], scores, const["maskq"][:, CH - width:CH], 1.0, NEG,
                                                     ALU.add, ALU.max, rowmax[:, h, t, c:c + 1]).then_inc(m_used, 1)
                        else:
                            dve.tensor_reduce(rowmax[:, h, t, c:c + 1], scores, AX.X, ALU.max).then_inc(m_used, 1)
                        if n == NM - 2:
                            dve.wait_ge(m_used, at(i, u, NM, NM + NM - 1 + SLOTS))
                            dve.tensor_reduce(negmax[:, 0:GH * S // P], rowmax[:, :, :, :].rearrange("p h t c -> p (h t) c"),
                                              AX.X, ALU.max, negate=True).then_inc(negmax_ready, 1)
                    elif what == "N":
                        bank = m_banks[0:GH * S // P, ((u + 1) * NM + NM - 1) % SLOTS, 0:P]
                        dve.wait_ge(m_ready, at(i, u, NM, NM + NM))
                        dve.wait_ge(mrows_in, at(i, u, MROWS, MROWS))
                        dve.tensor_copy(mrows[:, 0, :], bank).then_inc(m_step, 1)
                        dve.wait_ge(m_step, at(i, u, 3, 3 + 1))
                        dve.tensor_tensor(mrest[:, :], bank, mrows[:, 0, :], ALU.subtract).then_inc(m_used, 1)
                        dve.wait_ge(m_used, at(i, u, NM, NM + NM + SLOTS))
                        dve.tensor_copy(mrows[:, 1, :], mrest[:, :]).then_inc(m_step, 2)
                        dve.wait_ge(m_step, at(i, u, 3, 3 + 3))
                        dve.tensor_tensor(mrows[:, 2, :], mrest[:, :], mrows[:, 1, :], ALU.subtract).then_inc(mrows_ready, 1)
                    elif what == "T":
                        n, v = (n, u) if n >= 0 else (NQ - 1, u - 1)
                        heads = v_banks[:, n % 2, :].rearrange("p (j h w) -> p (j h) w", h=GH, w=VW)
                        dve.wait_ge(turned, at(i, v, NQ, n + 1 + 2))
                        dve.reciprocal(inv[:, n % 2].rearrange("p j h -> p (j h)"), heads[:, :, HD]).then_inc(inv_ready, 1)
                        dve.wait_ge(inv_ready, at(i, v, NQ, n + 1))
                        dve.wait_ge(ctx_stored[n % 2], at(i, v, 16 * NQ // 2, 16 * (n // 2)))
                        dve.tensor_tensor(ctx_sb[:, n % 2].rearrange("p j h w -> p (j h) w"), heads[:, :, 0:HD],
                                          inv[:, n % 2].rearrange("p j h -> p (j h)").unsqueeze(2).to_broadcast([P, TPC * GH, HD]),
                                          ALU.mult).then_inc(ctx_ready, 1)

            step(-1, 2, False, True, False, True)
            step(0, 0, True, True, False, True)
            with dve.Fori(0, LOOPED // SLOTS) as i:
                for u in range(SLOTS):
                    step(i, u + 1, True, True, True, True)
            for s in range(1 + LOOPED, G):
                step(s // SLOTS, s % SLOTS, True, s + 1 < G, True, s + 2 < G)
            step(G // SLOTS, G % SLOTS, False, False, True, False)


def stage_c(nc, x, scratch, const, keep):
    xn_dram, ctx_dram = scratch
    xt, base, logits = keep
    FRONT, BACK = 8, 3
    TURNS, SUMS = 4, 4
    with ExitStack() as ctx:
        def sb(name, shape, dt=F32):
            return ctx.enter_context(nc.sbuf_tensor(name, shape, dt))

        def sem(name):
            return ctx.enter_context(nc.semaphore(name))

        xs = sb("c_xs", [P, 2, TPC, D])
        xn = sb("c_xn", [P, 2, TPC, D])
        att = sb("att", [P, 2, 2, TPC, HG, GH * HD])
        attT = sb("attT", [P, 2, KD, CH])
        xtT = sb("xtT", [P, KD, CH])
        hidden = sb("hidden", [P, TPC, D])
        xt_now = sb("xt_now", [P, 2, TPC, D])
        sums = sb("sums", [P, TPC, D])
        stats = sb("c_stats", [P, TPC, 6])
        meanvar = sb("c_meanvar", [P, TPC, 2])
        std = sb("c_std", [P, TPC])
        rstd = sb("c_rstd", [P, TPC])
        none = sb("c_none", [P, 8])
        banks = ctx.enter_context(nc.psum_tensor("c_banks", [P, 8, CH], F32))

        arrived = [sem(f"arrived{i}") for i in range(2)]
        front_ready = sem("front_ready")
        back_ready = sem("back_ready")
        turned = sem("c_turned")
        back_out = sem("back_out")
        biased = sem("biased")
        added = sem("c_added")
        norm_step = sem("c_norm_step")
        var_ready = sem("c_var_ready")
        std_ready = sem("c_std_ready")
        xt_ready = sem("c_xt_ready")
        xt_kept = sem("xt_kept")
        sums_ready = sem("c_sums_ready")

        block = ctx.enter_context(nc.Block())
        x_chunks = x.rearrange("b (c j p) d -> (b c) p j d", j=TPC, p=P)
        xn_chunks = xn_dram.rearrange("(c j p) d -> c p j d", j=TPC, p=P)
        ARRIVED = 16 * (2 + 2 * HG)

        @block.sync
        def _(sp):
            for c in range(NCH):
                u, b, cc = c % 2, c // (NCH // B), c % (NCH // B)
                if c >= 2:
                    sp.wait_ge(added, SUMS * c)
                for a in range(2):
                    for hg in range(HG):
                        src = ctx_dram[(a * B + b) * HG + hg, cc * CH:(cc + 1) * CH, :].rearrange("(j p) n -> p j n", p=P)
                        sp.dma_start(att[:, u, a, :, hg, :], src).then_inc(arrived[u], 16)
                sp.dma_start(xn[:, u], xn_chunks[c]).then_inc(arrived[u], 16)
                sp.dma_start(xs[:, u], x_chunks[c]).then_inc(arrived[u], 16)

        @block.gpsimd
        def _(pool):
            with pool.Fori(0, NCH // 2) as i:
                for u in range(2):
                    c = i * 2 + u
                    pool.wait_ge(arrived[u], i * ARRIVED + ARRIVED)
                    pool.tensor_tensor(xn[:, u], xn[:, u], const["ob"][:, :].unsqueeze(1).to_broadcast([P, TPC, D]),
                                       ALU.add).then_inc(biased, 1)
                    pool.wait_ge(added, c * SUMS + (2 + SUMS))
                    pool.tensor_tensor(sums[:, :, :], hidden[:, :, :], xs[:, u], ALU.add).then_inc(sums_ready, 1)
                    pool.wait_ge(xt_ready, c + 1)
                    pool.tensor_copy(xt[:, bass.ds(i * (2 * TPC) + u * TPC, TPC), :], xt_now[:, u]).then_inc(xt_kept, 1)

        @block.vector
        def _(dve):
            dve.memset(none[:, 0:1], 0.0).then_inc(turned, TURNS)
            dve.memset(none[:, 1:2], 0.0).then_inc(added, SUMS)
            dve.memset(none[:, 2:3], 0.0).then_inc(xt_kept, 2)
            dve.memset(none[:, 3:4], 0.0).then_inc(back_out, BACK)
            with dve.Fori(0, NCH // 2) as i:
                for u in range(2):
                    c = i * 2 + u
                    tiles = i * (2 * TPC) + u * TPC
                    dve.wait_ge(biased, c + 1)
                    dve.wait_ge(sums_ready, c)
                    for half in range(2):
                        k = TURNS + half
                        dve.wait_ge(front_ready, c * FRONT + (k + 1))
                        pair = slice(2 * half, 2 * half + 2)
                        dve.tensor_tensor(hidden[:, pair, :], banks[:, k, :].rearrange("p (j d) -> p j d", d=D),
                                          xn[:, u, pair, :], ALU.add).then_inc(added, 1)
                    dve.wait_ge(added, c * SUMS + (2 + SUMS))
                    for j in range(TPC):
                        last = dve.bn_stats(stats[:, j, :], hidden[:, j, :])
                    last.then_inc(norm_step, 1)
                    dve.wait_ge(norm_step, c * 4 + 1)
                    dve.memset(none[:, 4:5], 0.0)
                    for j in range(TPC):
                        last = dve.bn_aggr(meanvar[:, j, :], stats[:, j, :])
                    last.then_inc(var_ready, 1)
                    dve.wait_ge(std_ready, c + 1)
                    dve.reciprocal(rstd[:, :], std[:, :]).then_inc(norm_step, 1)
                    dve.wait_ge(norm_step, c * 4 + 2)
                    dve.wait_ge(xt_kept, c + 1)
                    for j in range(TPC):
                        last = dve.tensor_scalar(xt_now[:, u, j, :], hidden[:, j, :], meanvar[:, j, 0:1],
                                                 rstd[:, j:j + 1], ALU.subtract, ALU.mult)
                    last.then_inc(norm_step, 1)
                    now = xt_now[:, u]
                    dve.wait_ge(norm_step, c * 4 + 3)
                    dve.tensor_tensor(now, now, const["ln2w"][:, :].unsqueeze(1).to_broadcast([P, TPC, D]),
                                      ALU.mult).then_inc(norm_step, 1)
                    dve.wait_ge(norm_step, c * 4 + 4)
                    dve.tensor_tensor(now, now, const["ln2b"][:, :].unsqueeze(1).to_broadcast([P, TPC, D]),
                                      ALU.add).then_inc(xt_ready, 1)
                    dve.wait_ge(sums_ready, c + 1)
                    for half in range(2):
                        k = TURNS + 2 + half
                        dve.wait_ge(front_ready, c * FRONT + (k + 1))
                        dve.tensor_tensor(base[:, bass.ds(tiles + 2 * half, 2), :],
                                          banks[:, k, :].rearrange("p (j d) -> p j d", d=D),
                                          sums[:, 2 * half:2 * half + 2, :], ALU.add).then_inc(added, 1)

        @block.scalar
        def _(act):
            def turn(c):
                for k in range(TURNS):
                    how = {"bias": const["vb"][:, k:k + 1]} if k < KD else {}
                    act.wait_ge(front_ready, c * FRONT + (k + 1))
                    act.activation(attT[:, k // 2, k % 2, :], banks[:, k, :], ACT.Identity, **how).then_inc(turned, 1)

            def root(c):
                act.wait_ge(var_ready, c + 1)
                act.activation(std[:, :], meanvar[:, :, 1], ACT.Sqrt, bias=const["eps"][:, 0:1]).then_inc(std_ready, 1)

            def back(c, tiles):
                for k in range(BACK):
                    src, out = banks[:, k, :], None
                    if k < KD:
                        out = xtT[:, k, :]
                    else:
                        out = logits[:, bass.ds(tiles, TPC), :]
                        src = src[:, 0:TPC * E].rearrange("p (j e) -> p j e", e=E)
                    act.wait_ge(back_ready, c * BACK + (k + 1))
                    act.activation(out, src, ACT.Copy).then_inc(back_out, 1)

            turn(0)
            root(0)
            with act.Fori(0, NCH // 2 - 1) as i:
                for u in range(2):
                    c = i * 2 + (u + 1)
                    turn(c)
                    back(i * 2 + u, i * (2 * TPC) + u * TPC)
                    root(c)
            turn(NCH - 1)
            back(NCH - 2, (NCH - 2) * TPC)
            root(NCH - 1)
            back(NCH - 1, (NCH - 1) * TPC)

        @block.tensor
        def _(pe):
            def front(i, u):
                c, par = i * 2 + u, u % 2
                for k in range(FRONT):
                    bank = banks[:, k, :]
                    if k == 0:
                        pe.wait_ge(arrived[par], i * ARRIVED + ARRIVED * (1 + u // 2))
                    if k < BACK and u > 0:
                        pe.wait_ge(back_out, c * BACK + (k - 2))
                    elif k == BACK:
                        pe.wait_ge(turned, c * TURNS + TURNS)
                    elif k >= TURNS:
                        pe.wait_ge(added, c * SUMS + (k - 3))
                    if k == 4:
                        pe.wait_ge(turned, c * TURNS + (KD + TURNS))
                    elif k == 6:
                        pe.wait_ge(turned, c * TURNS + 2 * TURNS)
                    if k < TURNS:
                        for j in range(TPC):
                            src = att[:, par, k // 2, j, 2 * (k % 2):2 * (k % 2) + 2, :].rearrange("p g w -> p (g w)")
                            last = pe.transpose(bank[:, j * P:(j + 1) * P], src, const["ident"][:, :])
                    else:
                        a = (k - TURNS) // 2
                        for j in range(2):
                            tile = 2 * (k % 2) + j
                            for h in range(KD):
                                last = pe.matmul(bank[:, j * D:(j + 1) * D], attT[:, a, h, tile * P:(tile + 1) * P],
                                                 const[("ow", "Wo")[a]][:, h, :], start=h == 0, stop=h == KD - 1)
                    last.then_inc(front_ready, 1)

            def back(i, u, newest):
                c = i * 2 + u
                for k in range(BACK):
                    bank = banks[:, k, :]
                    pe.wait_ge(turned, newest * TURNS + (k + 1 + TURNS))
                    if k < KD:
                        pe.wait_ge(back_out, c * BACK + (k + 1))
                        if k == 0:
                            pe.wait_ge(xt_ready, c + 1)
                    else:
                        pe.wait_ge(back_out, c * BACK + (KD + BACK))
                    for j in range(TPC):
                        cols = slice(j * P, (j + 1) * P)
                        if k < KD:
                            last = pe.transpose(bank[:, cols], xt_now[:, u, j, k * P:(k + 1) * P], const["ident"][:, :])
                        else:
                            for h in range(KD):
                                last = pe.matmul(bank[:, j * E:(j + 1) * E], xtT[:, h, cols], const["rw"][:, h, :],
                                                 start=h == 0, stop=h == KD - 1)
                    last.then_inc(back_ready, 1)

            front(0, 0)
            with pe.Fori(0, NCH // 2 - 1) as i:
                for u in range(2):
                    front(i, u + 1)
                    back(i, u, i * 2 + (u + 1))
            last_pair = NCH // 2 - 1
            front(last_pair, 1)
            back(last_pair, 0, NCH - 1)
            back(last_pair, 1, NCH - 1)


def stage_d(nc, scratch, const, keep):
    xin_dram, = scratch
    xt, logits, gates, gather_row = keep
    with ExitStack() as ctx:
        def sb(name, shape, dt=F32):
            return ctx.enter_context(nc.sbuf_tensor(name, shape, dt))

        def sem(name):
            return ctx.enter_context(nc.semaphore(name))

        cube = [P, NTILE, E]
        flat = [P, NTILE]
        probs, other, expert_ids = sb("d_probs", cube), sb("d_other", cube), sb("expert_ids", cube)
        ids_int = sb("ids_int", [P, NTILE * E], mybir.dt.int32)
        mask = [sb(f"mask{n}", cube) for n in range(2)]
        place = [sb(f"place{n}", cube) for n in range(2)]
        total = [sb(f"total{n}", cube) for n in range(2)]
        upto = [sb(f"upto{n}", cube) for n in range(2)]
        kept = [sb(f"kept{n}", cube) for n in range(2)]
        work = sb("d_work", cube)
        top8 = sb("top8", [P, NTILE, 8])
        top8_id = sb("top8_id", [P, NTILE, 8], U32)
        expert = [sb(f"expert{n}", flat) for n in range(2)]
        slot = [sb(f"slot{n}", flat) for n in range(2)]
        any_kept = [sb(f"any_kept{n}", flat) for n in range(2)]
        one, two, denom = sb("d_one", flat), sb("d_two", flat), sb("denom", flat)
        scatter_row = [sb(f"scatter_row{n}", flat, U32) for n in range(2)]
        ones_cube = sb("ones_cube", [P, NTILE])
        banks = ctx.enter_context(nc.psum_tensor("d_banks", [P, 4, CH], F32))

        step_done = sem("d_step_done")
        shifted = sem("d_shifted")
        exped = sem("d_exped")
        ids_ready = sem("ids_ready")
        masks_ready = sem("masks_ready")
        counted = sem("counted")
        rows_ready = sem("rows_ready")
        scattered = sem("scattered")

        block = ctx.enter_context(nc.Block())

        @block.tensor
        def _(pe):
            for n in range(2):
                pe.wait_ge(masks_ready, n + 1)
                m = mask[n][:, :, :].rearrange("p t e -> p (t e)")
                pe.matmul(banks[:, 2 * n, :], const["upper"][:, :], m, start=True, stop=True)
                pe.matmul(banks[:, 2 * n + 1, :], const["ones"][:, :], m, start=True, stop=True).then_inc(counted, 1)

        @block.scalar
        def _(act):
            act.wait_ge(shifted, 1)
            act.activation(probs[:, :, :], work[:, :, :], ACT.Exp).then_inc(exped, 1)

        @block.gpsimd
        def _(pool):
            pool.iota(ids_int[:, :], [[0, NTILE], [1, E]], base=0, channel_multiplier=0).then_inc(ids_ready, 1)
            for n in range(2):
                pool.wait_ge(rows_ready, n + 1)
                for t in range(NTILE):
                    pool.indirect_dma_start(out=xin_dram, out_offset=bass.IndirectOffsetOnAxis(ap=scatter_row[n][:, t:t + 1], axis=0),
                                            in_=xt[:, t, :], in_offset=None, bounds_check=E * CAP - 1,
                                            oob_is_err=False).then_inc(scattered, 16)
            pool.wait_ge(scattered, 16 * 2 * NTILE)

        @block.vector
        def _(dve):
            count = [0]

            def settle(ins):
                count[0] += 1
                ins.then_inc(step_done, 1)
                dve.wait_ge(step_done, count[0])

            def wide(a):
                return a.unsqueeze(2).to_broadcast(cube)

            settle(dve.memset(ones_cube[:, :], 1.0))
            dve.wait_ge(ids_ready, 1)
            settle(dve.tensor_copy(expert_ids[:, :, :].rearrange("p t e -> p (t e)"), ids_int[:, :]))
            settle(dve.tensor_reduce(one[:, :], logits[:, :, :], AX.X, ALU.max))
            dve.tensor_tensor(work[:, :, :], logits[:, :, :], wide(one[:, :]), ALU.subtract).then_inc(shifted, 1)
            dve.wait_ge(exped, 1)
            settle(dve.tensor_reduce(two[:, :], probs[:, :, :], AX.X, ALU.add))
            settle(dve.reciprocal(denom[:, :], two[:, :]))
            settle(dve.tensor_tensor(probs[:, :, :], probs[:, :, :], wide(denom[:, :]), ALU.mult))

            def choose(n):
                src = (probs, other)[n]
                for t in range(NTILE):
                    ins = dve.max(top8[:, t, :], src[:, t, :])
                settle(ins)
                for t in range(NTILE):
                    ins = dve.max_index(top8_id[:, t, :], top8[:, t, :], src[:, t, :])
                settle(ins)
                settle(dve.tensor_copy(expert[n][:, :], top8_id[:, :, 0]))
                ins = dve.tensor_tensor(mask[n][:, :, :], expert_ids[:, :, :], wide(expert[n][:, :]), ALU.is_equal)
                ins.then_inc(masks_ready, 1)
                dve.wait_ge(masks_ready, n + 1)
                if n == 0:
                    settle(dve.scalar_tensor_tensor(out=other[:, :, :].rearrange("p t e -> p (t e)"),
                                                    in0=mask[0][:, :, :].rearrange("p t e -> p (t e)"), scalar=NEG,
                                                    in1=logits[:, :, :].rearrange("p t e -> p (t e)"), op0=ALU.mult, op1=ALU.add))

            def find_rows(n):
                dve.wait_ge(counted, n + 1)
                by_tile = banks[:, 2 * n + 1, :].rearrange("p (t e) -> p t e", e=E)
                settle(dve.tensor_copy(total[n][:, :, :], by_tile))
                for e in range(E):
                    ins = dve.tensor_tensor_scan(upto[n][:, :, e], ones_cube[:, :], total[n][:, :, e], 0.0, ALU.mult, ALU.add)
                settle(ins)
                settle(dve.tensor_tensor(work[:, :, :], upto[n][:, :, :], total[n][:, :, :], ALU.subtract))
                settle(dve.tensor_tensor(place[n][:, :, :], banks[:, 2 * n, :].rearrange("p (t e) -> p t e", e=E),
                                         work[:, :, :], ALU.add))
                settle(dve.tensor_scalar(place[n][:, :, :], place[n][:, :, :], -1.0, None, ALU.add))
                if n == 1:
                    firsts = upto[0][:, NTILE - 1:NTILE, :].to_broadcast(cube)
                    settle(dve.tensor_tensor(place[1][:, :, :], place[1][:, :, :], firsts, ALU.add))
                settle(dve.tensor_scalar(work[:, :, :], place[n][:, :, :], float(CAP), None, ALU.is_lt))
                settle(dve.tensor_tensor(kept[n][:, :, :], work[:, :, :], mask[n][:, :, :], ALU.mult))
                settle(dve.tensor_reduce(any_kept[n][:, :], kept[n][:, :, :], AX.X, ALU.add))
                settle(dve.tensor_tensor(work[:, :, :], place[n][:, :, :], kept[n][:, :, :], ALU.mult))
                settle(dve.tensor_reduce(slot[n][:, :], work[:, :, :], AX.X, ALU.add))
                settle(dve.tensor_scalar(one[:, :], expert[n][:, :], float(CAP), None, ALU.mult))
                settle(dve.tensor_tensor(one[:, :], one[:, :], slot[n][:, :], ALU.add))
                settle(dve.tensor_scalar(two[:, :], any_kept[n][:, :], -float(E * CAP), float(E * CAP), ALU.mult, ALU.add))
                settle(dve.tensor_tensor(two[:, :], one[:, :], two[:, :], ALU.add))
                dve.tensor_copy(scatter_row[n][:, :], two[:, :]).then_inc(rows_ready, 1)
                dve.wait_ge(rows_ready, n + 1)
                settle(dve.tensor_tensor(two[:, :], one[:, :], any_kept[n][:, :], ALU.mult))
                settle(dve.tensor_copy(gather_row[:, n, :], two[:, :]))

            for n in range(2):
                choose(n)
                find_rows(n)
            for n in range(2):
                settle(dve.tensor_tensor(work[:, :, :], probs[:, :, :], kept[n][:, :, :], ALU.mult))
                settle(dve.tensor_reduce(gates[:, n, :], work[:, :, :], AX.X, ALU.add))
            settle(dve.tensor_tensor(denom[:, :], gates[:, 0, :], gates[:, 1, :], ALU.add))
            settle(dve.tensor_scalar(denom[:, :], denom[:, :], 2.0 ** -23, None, ALU.max))
            settle(dve.reciprocal(one[:, :], denom[:, :]))
            settle(dve.tensor_tensor(gates[:, :, :], gates[:, :, :], one[:, :].unsqueeze(1).to_broadcast([P, 2, NTILE]), ALU.mult))


def stage_e(nc, weights, scratch, const):
    fc1_w, fc2_w = weights
    xin_dram, eout_dram = scratch
    FB = F // P
    XBANK, HBANK, OBANK = 0, KD, KD + 4
    HRING = 4
    HI, LO = 0, 1
    PASSES = ((HI, HI), (HI, LO), (LO, HI))
    with ExitStack() as ctx:
        def sb(name, shape, dt=F32):
            return ctx.enter_context(nc.sbuf_tensor(name, shape, dt))

        def sem(name):
            return ctx.enter_context(nc.semaphore(name))

        w1 = sb("w1", [P, KD, F])
        w2 = sb("w2", [P, FB, D])
        w1_parts = sb("w1_parts", [P, 2, KD, F], F32R)
        w2_parts = sb("w2_parts", [P, 2, FB, D], F32R)
        xin = sb("xin", [P, 2, CAP // P, D])
        xinT = sb("xinT", [P, 2, KD, CAP], F32R)
        hid = sb("e_hid", [P, HRING, CAP])
        hid_parts = sb("hid_parts", [P, 2, FB, CAP], F32R)
        eout = sb("eout", [P, 2, CAP // P, D])
        none = sb("e_none", [P, 8])
        banks = ctx.enter_context(nc.psum_tensor("e_banks", [P, 8, CAP], F32))

        rows_in = [sem(f"rows_in{i}") for i in range(2)]
        w1_in, w2_in = sem("w1_in"), sem("w2_in")
        w_high = sem("w_high")
        w1_split, w2_split = sem("w1_split"), sem("w2_split")
        turned = sem("e_turned")
        x_high = sem("x_high")
        x_split = sem("x_split")
        h_ready = sem("h_ready")
        hid_ready = sem("hid_ready")
        hid_split = sem("hid_split")
        o_ready = sem("o_ready")
        added = sem("e_added")
        stored = [sem(f"e_stored{i}") for i in range(2)]

        block = ctx.enter_context(nc.Block())

        def f32(part):
            return part.bitcast(F32)

        @block.sync
        def _(sp):
            def load_rows(e, u):
                sp.dma_start(xin[:, u], xin_dram[bass.ds(e * CAP, CAP), :].rearrange("(j p) d -> p j d", p=P)).then_inc(rows_in[u], 16)

            def load_w1(e):
                sp.dma_start(w1[:, :, :], fc1_w[e].rearrange("(h p) f -> p h f", p=P)).then_inc(w1_in, 16)

            def load_w2(e):
                sp.dma_start(w2[:, :, :], fc2_w[e].rearrange("(f p) d -> p f d", p=P)).then_inc(w2_in, 16)

            load_w1(0)
            load_rows(0, 0)
            load_w2(0)
            load_rows(1, 1)
            with sp.Fori(0, E // 2 - 1) as i:
                for u in range(2):
                    sp.wait_ge(turned, i * (2 * KD) + KD * (u + 1))
                    load_rows(i * 2 + (u + 2), u)
                    sp.wait_ge(w1_split, i * 4 + 2 * (u + 1))
                    load_w1(i * 2 + (u + 1))
                    sp.wait_ge(w2_split, i * 4 + 2 * (u + 1))
                    load_w2(i * 2 + (u + 1))
            sp.wait_ge(w1_split, 2 * (E - 1))
            load_w1(E - 1)
            sp.wait_ge(w2_split, 2 * (E - 1))
            load_w2(E - 1)

        @block.gpsimd
        def _(pool):
            with pool.Fori(0, E // 2) as i:
                for u in range(2):
                    e = i * 2 + u
                    pool.wait_ge(added, e * 2 + 4)
                    dst = eout_dram[bass.ds(e * CAP, CAP), :].rearrange("(j p) d -> p j d", p=P)
                    pool.dma_start(dst, eout[:, u]).then_inc(stored[u], 16)
            for u in range(2):
                pool.wait_ge(stored[u], 16 * E // 2)

        @block.vector
        def _(dve):
            dve.memset(none[:, 0:1], 0.0).then_inc(hid_ready, HRING)
            dve.memset(none[:, 1:2], 0.0).then_inc(hid_split, HRING)
            dve.memset(none[:, 2:3], 0.0).then_inc(added, 2)

            def split(whole, parts, nth, done):
                n = whole.shape[1] // 2
                for half in range(2):
                    cut = slice(half * n, (half + 1) * n)
                    dve.tensor_copy(parts[:, HI, cut, :], whole[:, cut, :]).then_inc(w_high, 1)
                for half in range(2):
                    cut = slice(half * n, (half + 1) * n)
                    dve.wait_ge(w_high, nth * 2 + (half + 1))
                    dve.tensor_tensor(parts[:, LO, cut, :], whole[:, cut, :], f32(parts[:, HI, cut, :]),
                                      ALU.subtract).then_inc(done, 1)

            def prepare(i, u):
                e = i * 2 + u
                for h in range(KD):
                    dve.wait_ge(x_high, e * KD + (h + 1))
                    dve.tensor_tensor(xinT[:, LO, h, :], banks[:, XBANK + h, :], f32(xinT[:, HI, h, :]),
                                      ALU.subtract).then_inc(x_split, 1)
                dve.wait_ge(w1_in, e * 16 + 16)
                dve.wait_ge(h_ready, e * FB)
                split(w1, w1_parts, e * 2, w1_split)

            def expert(i, u, more):
                e = i * 2 + u
                dve.wait_ge(w2_in, e * 16 + 16)
                dve.wait_ge(o_ready, e * 2)
                split(w2, w2_parts, e * 2 + 1, w2_split)
                for f in range(FB):
                    dve.wait_ge(hid_ready, e * FB + (f + 1 + HRING))
                    dve.tensor_tensor(hid_parts[:, LO, f, :], hid[:, f % HRING, :], f32(hid_parts[:, HI, f, :]),
                                      ALU.subtract).then_inc(hid_split, 1)
                if more:
                    prepare(i, u + 1)
                dve.wait_ge(stored[u], i * 16)
                for n in range(2):
                    dve.wait_ge(o_ready, e * 2 + (n + 1))
                    src = banks[:, OBANK + n, :].rearrange("p (j d) -> p j d", d=D)
                    bias = const["b2"][:, bass.ds(e, 1), :].to_broadcast([P, 2, D])
                    dve.scalar_tensor_tensor(out=eout[:, u, 2 * n:2 * n + 2, :], in0=src, scalar=KEEP, in1=bias,
                                             op0=ALU.mult, op1=ALU.add).then_inc(added, 1)

            prepare(0, 0)
            with dve.Fori(0, E // 2 - 1) as i:
                for u in range(2):
                    expert(i, u, True)
            expert(E // 2 - 1, 0, True)
            expert(E // 2 - 1, 1, False)

        @block.scalar
        def _(act):
            def rows(e):
                for h in range(KD):
                    act.wait_ge(turned, e * KD + (h + 1))
                    act.activation(xinT[:, HI, h, :], banks[:, XBANK + h, :], ACT.Copy).then_inc(x_high, 1)

            def expert(i, u, more):
                e = i * 2 + u
                for f in range(FB):
                    bank = banks[:, HBANK + f % HRING, :]
                    bias = const["b1T"][:, bass.ds(e * FB + f, 1)]
                    act.wait_ge(h_ready, e * FB + (f + 1))
                    act.wait_ge(hid_split, e * FB + (f + 1))
                    act.activation(hid_parts[:, HI, f, :], bank, ACT.Gelu, bias=bias)
                    act.activation(hid[:, f % HRING, :], bank, ACT.Gelu, bias=bias).then_inc(hid_ready, 1)
                if more:
                    rows(e + 1)

            rows(0)
            with act.Fori(0, E // 2 - 1) as i:
                for u in range(2):
                    expert(i, u, True)
            expert(E // 2 - 1, 0, True)
            expert(E // 2 - 1, 1, False)

        @block.tensor
        def _(pe):
            def rows(i, u):
                pe.wait_ge(rows_in[u % 2], i * 16 + 16 * (1 + u // 2))
                for h in range(KD):
                    for j in range(CAP // P):
                        last = pe.transpose(banks[:, XBANK + h, j * P:(j + 1) * P], xin[:, u % 2, j, h * P:(h + 1) * P],
                                            const["ident"][:, :])
                    last.then_inc(turned, 1)

            def expert(i, u, more):
                e = i * 2 + u
                for f in range(FB):
                    if f == 0:
                        pe.wait_ge(x_split, e * KD + KD)
                        pe.wait_ge(w1_split, e * 2 + 2)
                    pe.wait_ge(hid_ready, e * FB + (f + 1))
                    for h in range(KD):
                        for a, b in PASSES:
                            last = pe.matmul(banks[:, HBANK + f % HRING, :], w1_parts[:, a, h, f * P:(f + 1) * P], xinT[:, b, h, :],
                                             start=h == 0 and (a, b) == PASSES[0], stop=h == KD - 1 and (a, b) == PASSES[-1])
                    last.then_inc(h_ready, 1)
                if more:
                    rows(i, u + 1)
                for tile in range(CAP // P):
                    n, j = tile // 2, tile % 2
                    if j == 0:
                        pe.wait_ge(added, e * 2 + (n + 1))
                    for f in range(FB):
                        if tile == 0:
                            if f % (FB // 2) == 0:
                                pe.wait_ge(w2_split, e * 2 + (f // (FB // 2) + 1))
                            pe.wait_ge(hid_split, e * FB + (f + 1 + HRING))
                        for a, b in PASSES:
                            last = pe.matmul(banks[:, OBANK + n, j * D:(j + 1) * D], hid_parts[:, a, f, tile * P:(tile + 1) * P],
                                             w2_parts[:, b, f, :], start=f == 0 and (a, b) == PASSES[0],
                                             stop=f == FB - 1 and (a, b) == PASSES[-1])
                    if j == 1:
                        last.then_inc(o_ready, 1)

            rows(0, 0)
            with pe.Fori(0, E // 2 - 1) as i:
                for u in range(2):
                    expert(i, u, True)
            expert(E // 2 - 1, 0, True)
            expert(E // 2 - 1, 1, False)


def stage_f(nc, out, eout_dram, keep):
    base, gates, gather_row = keep
    RING = 4
    with ExitStack() as ctx:
        def sb(name, shape, dt=F32):
            return ctx.enter_context(nc.sbuf_tensor(name, shape, dt))

        def sem(name):
            return ctx.enter_context(nc.semaphore(name))

        rows = sb("rows", [P, RING, 2, D])
        half = sb("half", [P, RING, D])
        total = sb("f_total", [P, RING, D])
        gathered = [sem(f"gathered{i}") for i in range(RING)]
        half_ready = sem("half_ready")
        total_ready = sem("total_ready")
        stored = [sem(f"f_stored{i}") for i in range(RING)]
        block = ctx.enter_context(nc.Block())
        out_tiles = out.rearrange("b (t p) d -> (b t) p d", p=P)

        @block.gpsimd
        def _(pool):
            for t in range(NTILE):
                if t >= RING:
                    pool.wait_ge(total_ready, t - RING + 1)
                for n in range(2):
                    pool.indirect_dma_start(out=rows[:, t % RING, n, :], out_offset=None, in_=eout_dram,
                                            in_offset=bass.IndirectOffsetOnAxis(ap=gather_row[:, n, t:t + 1], axis=0))\
                        .then_inc(gathered[t % RING], 16)

        @block.vector
        def _(dve):
            for t in range(NTILE):
                r = t % RING
                dve.wait_ge(gathered[r], 32 * (t // RING + 1))
                dve.scalar_tensor_tensor(out=half[:, r, :], in0=rows[:, r, 0, :], scalar=gates[:, 0, t:t + 1],
                                         in1=base[:, t, :], op0=ALU.mult, op1=ALU.add).then_inc(half_ready, 1)
                dve.wait_ge(half_ready, t + 1)
                if t >= RING:
                    dve.wait_ge(stored[r], 16 * (t // RING))
                dve.scalar_tensor_tensor(out=total[:, r, :], in0=rows[:, r, 1, :], scalar=gates[:, 1, t:t + 1],
                                         in1=half[:, r, :], op0=ALU.mult, op1=ALU.add).then_inc(total_ready, 1)

        @block.sync
        def _(sp):
            for t in range(NTILE):
                sp.wait_ge(total_ready, t + 1)
                sp.dma_start(out_tiles[t], total[:, t % RING, :]).then_inc(stored[t % RING], 16)
            for r in range(RING):
                sp.wait_ge(stored[r], 16 * (NTILE // RING))


def load_constants(nc, w, const, b1_rows):
    with ExitStack() as ctx:
        def sem(name):
            return ctx.enter_context(nc.semaphore(name))

        arrived, blank, made, turned, scaled = sem("w_arrived"), sem("w_blank"), sem("w_made"), sem("b1_turned"), sem("b2_scaled")
        bank = ctx.enter_context(nc.psum_tensor("w_bank", [P, P], F32))
        loads = []
        halves = "(h p) n -> p h n"
        loads.append((const["wd"][:, :, 0:DC], w["W_dq"].rearrange(halves, p=P)))
        loads.append((const["wd"][:, :, DC:2 * DC], w["W_dkv"].rearrange(halves, p=P)))
        loads.append((const["wu"][0:DC, 0, :], w["W_uq"]))
        loads.append((const["wu"][DC:2 * DC, 1, :], w["W_uk"]))
        loads.append((const["wu"][DC:2 * DC, 2, :], w["W_uv"]))
        for name, key in (("qw", "q_w"), ("kw", "k_w"), ("vw", "v_w"), ("ow", "o_w"), ("Wo", "W_o"), ("rw", "router_w")):
            loads.append((const[name][:, :, :], w[key].rearrange(halves, p=P)))
        for name, key in (("ln2w", "ln2_w"), ("ln2b", "ln2_b"), ("ob", "o_b")):
            loads.append((const[name][:, :], w[key].rearrange("(a d) -> a d", a=1).to_broadcast([P, D])))
        loads.append((const["b2"][:, :, :], w["fc2_b"].rearrange("(a e) d -> a e d", a=1).to_broadcast([P, E, D])))
        loads.append((b1_rows[:, :], w["fc1_b"].rearrange("e (f p) -> (e f) p", p=P)))
        columns = [(const[name][:, :], w[key].rearrange("(h p) -> p h", p=P))
                   for name, key in (("ln1w", "ln1_w"), ("ln1b", "ln1_b"), ("qb", "q_b"), ("kb", "k_b"), ("vb", "v_b"))]
        ALL = 16 * (len(loads) + len(columns))
        block = ctx.enter_context(nc.Block())

        @block.sync
        def _(sp):
            sp.wait_ge(blank, 1)
            for dst, src in loads:
                sp.dma_start(dst, src).then_inc(arrived, 16)
            with nc.allow_non_contiguous_dma(reason="short vectors, one value per partition"):
                for dst, src in columns:
                    sp.dma_start(dst, src).then_inc(arrived, 16)
            sp.wait_ge(arrived, ALL)

        @block.gpsimd
        def _(pool):
            pool.memset(const["ident"][:, :], 0.0)
            pool.memset(const["maskq"][:, :], 0.0)
            pool.memset(const["maskk"][:, :], 0.0)
            pool.memset(const["identb"][:, :], 0.0)
            pool.memset(const["wu"][:, :, :], 0.0)
            pool.memset(const["upper"][:, :], 1.0)
            pool.memset(const["eps"][:, :], EPS)
            pool.memset(const["ones"][:, :], 1.0).then_inc(blank, 1)
            pool.wait_ge(blank, 1)
            for m in ("ident", "identb"):
                pool.affine_select(out=const[m][:, :], in_=const[m][:, :], compare_op=ALU.not_equal, fill=1.0, base=0,
                                   pattern=[[-1, P]], channel_multiplier=1).then_inc(made, 1)
            diagonal = const["maskq"][:, CH - P:CH]
            pool.affine_select(out=diagonal, in_=diagonal, compare_op=ALU.is_ge, fill=NEG, base=0,
                               pattern=[[-1, P]], channel_multiplier=1).then_inc(made, 1)
            pool.affine_select(out=const["maskk"][:, :], in_=const["maskk"][:, :], compare_op=ALU.is_ge, fill=NEG, base=0,
                               pattern=[[1, P]], channel_multiplier=-1).then_inc(made, 1)
            pool.affine_select(out=const["upper"][:, :], in_=const["upper"][:, :], compare_op=ALU.is_ge, fill=0.0, base=0,
                               pattern=[[1, P]], channel_multiplier=-1).then_inc(made, 1)

        @block.tensor
        def _(pe):
            pe.wait_ge(arrived, ALL)
            pe.wait_ge(made, 5)
            pe.transpose(bank[:, :], b1_rows[:, :], const["ident"][:, :]).then_inc(turned, 1)

        @block.vector
        def _(dve):
            dve.wait_ge(turned, 1)
            dve.tensor_copy(const["b1T"][:, :], bank[:, :])
            dve.tensor_scalar(const["b2"][:, :, :], const["b2"][:, :, :], KEEP, None, ALU.mult).then_inc(scaled, 1)


def layer(nc, x, w, out):
    xn_dram = nc.dram_tensor("xn_scratch", [T, D], F32).ap()
    q_dram = nc.dram_tensor("q_scratch", [G, GH, SPLIT * HD, S], BF16).ap()
    k_dram = nc.dram_tensor("k_scratch", [G, GH, SPLIT * HD, S], BF16).ap()
    v_dram = nc.dram_tensor("v_scratch", [G, S, GH * VW], F32).ap()
    ctx_dram = nc.dram_tensor("ctx_scratch", [G, S, GH * HD], F32).ap()
    xin_dram = nc.dram_tensor("xin_scratch", [E * CAP, D], F32).ap()
    eout_dram = nc.dram_tensor("eout_scratch", [E * CAP, D], F32).ap()
    with ExitStack() as ctx:
        shapes = {"wd": [P, KD, 2 * DC], "wu": [P, 3, D], "qw": [P, KD, D], "kw": [P, KD, D], "vw": [P, KD, D],
                  "ow": [P, KD, D], "Wo": [P, KD, D], "rw": [P, KD, E], "vb": [P, KD], "ob": [P, D],
                  "ln1w": [P, KD], "ln1b": [P, KD], "qb": [P, KD], "kb": [P, KD], "ln2w": [P, D], "ln2b": [P, D],
                  "b2": [P, E, D], "b1T": [P, E * F // P], "ident": [P, P], "upper": [P, P], "ones": [P, P], "eps": [P, 1],
                  "maskq": [P, CH]}
        const = {n: ctx.enter_context(nc.sbuf_tensor(f"c_{n}", s, F32)) for n, s in shapes.items()}
        for n in ("identb", "maskk"):
            const[n] = ctx.enter_context(nc.sbuf_tensor(f"c_{n}", [P, P], BF16))
        with nc.sbuf_tensor("b1_rows", [E * F // P, P], F32) as b1_rows:
            load_constants(nc, w, const, b1_rows)
        stage_a(nc, x, (xn_dram, q_dram, k_dram, v_dram), const)
        stage_b(nc, (xin_dram, q_dram, k_dram, v_dram, ctx_dram), const)
        with ExitStack() as late:
            def sb(name, shape, dt=F32):
                return late.enter_context(nc.sbuf_tensor(name, shape, dt))

            base = sb("base", [P, NTILE, D])
            gates = sb("gates", [P, 2, NTILE])
            gather_row = sb("gather_row", [P, 2, NTILE], U32)
            with nc.sbuf_tensor("xt", [P, NTILE, D], F32) as xt, nc.sbuf_tensor("logits", [P, NTILE, E], F32) as logits:
                stage_c(nc, x, (xn_dram, ctx_dram), const, (xt, base, logits))
                stage_d(nc, (xin_dram,), const, (xt, logits, gates, gather_row))
            stage_e(nc, (w["fc1_w"], w["fc2_w"]), (xin_dram, eout_dram), const)
            stage_f(nc, out, eout_dram, (base, gates, gather_row))


_ATTN = ["W_dq", "W_uq", "W_dkv", "W_uk", "W_uv", "W_o"]
_FFN = ["ln1_w", "ln1_b", "q_w", "q_b", "k_w", "k_b", "v_w", "v_b", "o_w", "o_b", "ln2_w", "ln2_b", "router_w",
        "fc1_w", "fc1_b", "fc2_w", "fc2_b"]
_INS = {"x": "L0_attn_x", **{n: f"L0_attn_{n}" for n in _ATTN}, **{n: f"L0_ffn_{n}" for n in _FFN}}


def kernel(**inputs):
    import numpy as _np
    import concourse.bacc as _bacc
    from concourse import mybir as _mybir
    from concourse.bass_utils import run_bass_kernel_spmd as _run

    nc = _bacc.Bacc("TRN2", target_bir_lowering=False, num_devices=1)
    arrays, args = {}, {}
    for short, name in _INS.items():
        a = _np.ascontiguousarray(inputs[name])
        arrays[f"in_{name}"] = a
        args[short] = nc.dram_tensor(f"in_{name}", a.shape, _mybir.dt.from_np(a.dtype), kind="ExternalInput").ap()
    out = nc.dram_tensor("out_0", (B, S, D), F32, kind="ExternalOutput").ap()
    layer(nc, args.pop("x"), args, out)
    r = _run(nc, [arrays], core_ids=[0])
    return r.results[0]["out_0"]
```
